# Optimizing a Trainium2 kernel written in Bass

```python
import numpy as np
import jax
import jax.numpy as jnp

def _softmax(x, axis=-1):
    return jax.nn.softmax(x, axis=axis)

def _gelu(x):
    return jax.nn.gelu(x, approximate=True)

def _silu(x):
    return jax.nn.silu(x)

def _sigmoid(x):
    return jax.nn.sigmoid(x)

def _layernorm(x, axis=-1, eps=1e-05):
    m = jnp.mean(x, axis=axis, keepdims=True)
    v = jnp.var(x, axis=axis, keepdims=True)
    return (x - m) / jnp.sqrt(v + eps)

def _scatter_add(tgt, idx, src, axis=0):
    return tgt.at[idx].add(src)

def _segment_sum(src, seg, n):
    return jax.ops.segment_sum(src, seg, n)
kernel_name = 'mk_gnn_preln_d2_gnn_r32_d9957d'

def setup_inputs(seed: int=0):
    np.random.seed(seed)
    _w = jnp.asarray

    def _rec_inputs():
        import jax
        import jax.numpy as jnp
        _gk = jax.random.key(seed)
        x = -0.0001006 + 1 * jax.random.normal(jax.random.fold_in(_gk, 1), (50000, 96), jnp.float32)
        src = jax.random.randint(jax.random.fold_in(_gk, 2), (50000,), 0, 50000, jnp.int32)
        dst = jax.random.randint(jax.random.fold_in(_gk, 3), (50000,), 0, 50000, jnp.int32)
        _o = jnp.argsort(dst, stable=True)
        src = src[_o]
        dst = dst[_o]
        edge_attr_4 = 0.000714719 + 1.00021 * jax.random.normal(jax.random.fold_in(_gk, 12), (50000, 4), jnp.float32)
        return (x, src, dst, edge_attr_4)
    x, src, dst, edge_attr_4 = _rec_inputs()

    def _L0_gnn_setup():
        import jax, jax.numpy as jnp
        import numpy as np
        N_NODES = 50000
        key = jax.random.key(seed)
        k1, k2, k3 = jax.random.split(key, 3)
        feat = jax.random.normal(k1, (N_NODES, 96), dtype=jnp.float32)
        src = jax.random.randint(k2, (25000,), 0, N_NODES, dtype=jnp.int64)
        dst = jax.random.randint(k3, (25000,), 0, N_NODES, dtype=jnp.int64)
        return {'feat': feat, 'src': src, 'dst': dst}
    _L0_gnn_all = _L0_gnn_setup()
    _L0_gnn_in = {k: v for k, v in _L0_gnn_all.items() if k in ()}
    del _L0_gnn_all

    def _L1_gnn_setup():
        import jax, jax.numpy as jnp
        import numpy as np
        EPS = 1e-05

        def _mlp(h, W, b, gamma, beta):
            h = jax.nn.relu(h @ W + b)
            mu = jnp.mean(h, axis=0)
            var = jnp.mean(jnp.square(h - mu), axis=0)
            return gamma * (h - mu) * jax.lax.rsqrt(var + EPS) + beta
        key = jax.random.key(seed)
        ks = jax.random.split(key, 10)
        N, E, C_in, C_out, E_dim = (50000, 25000, 96, 96, 4)
        x = jax.random.normal(ks[0], (N, C_in), dtype=jnp.float32)
        edge_index = jax.random.randint(ks[1], (2, E), 0, N, dtype=jnp.int64)
        edge_attr = jax.random.normal(ks[2], (E, E_dim), dtype=jnp.float32)
        s = lambda fan_in: 1.0 / np.sqrt(fan_in)
        W_node = jax.random.uniform(ks[3], (C_in, C_out), jnp.float32, -s(C_in), s(C_in))
        b_node = jnp.zeros((C_out,), jnp.float32)
        g_node = jnp.ones((C_out,), jnp.float32)
        beta_node = jnp.zeros((C_out,), jnp.float32)
        W_edge = jax.random.uniform(ks[4], (E_dim, C_out), jnp.float32, -s(E_dim), s(E_dim))
        b_edge = jnp.zeros((C_out,), jnp.float32)
        g_edge = jnp.ones((C_out,), jnp.float32)
        beta_edge = jnp.zeros((C_out,), jnp.float32)
        M_in = 2 * C_in + C_out
        W_msg = jax.random.uniform(ks[5], (M_in, C_out), jnp.float32, -s(M_in), s(M_in))
        b_msg = jnp.zeros((C_out,), jnp.float32)
        g_msg = jnp.ones((C_out,), jnp.float32)
        beta_msg = jnp.zeros((C_out,), jnp.float32)
        return dict(x=x, edge_index=edge_index, edge_attr=edge_attr, W_node=W_node, b_node=b_node, g_node=g_node, beta_node=beta_node, W_edge=W_edge, b_edge=b_edge, g_edge=g_edge, beta_edge=beta_edge, W_msg=W_msg, b_msg=b_msg, g_msg=g_msg, beta_msg=beta_msg)
    _L1_gnn_all = _L1_gnn_setup()
    _L1_gnn_in = {k: v for k, v in _L1_gnn_all.items() if k in ('W_node', 'b_node', 'g_node', 'beta_node', 'W_edge', 'b_edge', 'g_edge', 'beta_edge', 'W_msg', 'b_msg', 'g_msg', 'beta_msg')}
    del _L1_gnn_all
    return {'x': x, 'src': src, 'dst': dst, 'edge_attr_4': edge_attr_4, 'L1_gnn_W_node': _L1_gnn_in['W_node'], 'L1_gnn_b_node': _L1_gnn_in['b_node'], 'L1_gnn_g_node': _L1_gnn_in['g_node'], 'L1_gnn_beta_node': _L1_gnn_in['beta_node'], 'L1_gnn_W_edge': _L1_gnn_in['W_edge'], 'L1_gnn_b_edge': _L1_gnn_in['b_edge'], 'L1_gnn_g_edge': _L1_gnn_in['g_edge'], 'L1_gnn_beta_edge': _L1_gnn_in['beta_edge'], 'L1_gnn_W_msg': _L1_gnn_in['W_msg'], 'L1_gnn_b_msg': _L1_gnn_in['b_msg'], 'L1_gnn_g_msg': _L1_gnn_in['g_msg'], 'L1_gnn_beta_msg': _L1_gnn_in['beta_msg']}

def reference(x, src, dst, edge_attr_4, L1_gnn_W_node, L1_gnn_b_node, L1_gnn_g_node, L1_gnn_beta_node, L1_gnn_W_edge, L1_gnn_b_edge, L1_gnn_g_edge, L1_gnn_beta_edge, L1_gnn_W_msg, L1_gnn_b_msg, L1_gnn_g_msg, L1_gnn_beta_msg):
    import jax
    import jax.numpy as jnp

    def _L0_gnn_ref(feat, src, dst):
        import jax, jax.numpy as jnp
        import numpy as np
        N_NODES = 50000
        msgs = feat[src]
        sums = jax.ops.segment_sum(msgs, dst, num_segments=N_NODES)
        deg = jax.ops.segment_sum(jnp.ones_like(dst, dtype=feat.dtype), dst, num_segments=N_NODES)
        return sums / jnp.maximum(deg, 1.0)[:, None]

    def _L1_gnn_ref(x, edge_index, edge_attr, W_node, b_node, g_node, beta_node, W_edge, b_edge, g_edge, beta_edge, W_msg, b_msg, g_msg, beta_msg):
        import jax, jax.numpy as jnp
        import numpy as np
        EPS = 1e-05

        def _mlp(h, W, b, gamma, beta):
            h = jax.nn.relu(h @ W + b)
            mu = jnp.mean(h, axis=0)
            var = jnp.mean(jnp.square(h - mu), axis=0)
            return gamma * (h - mu) * jax.lax.rsqrt(var + EPS) + beta
        node_feat = _mlp(x, W_node, b_node, g_node, beta_node)
        edge_feat = _mlp(edge_attr, W_edge, b_edge, g_edge, beta_edge)
        row, col = (edge_index[0], edge_index[1])
        message = jnp.concatenate([x[row], x[col], edge_feat], axis=1)
        message = _mlp(message, W_msg, b_msg, g_msg, beta_msg)
        agg = jax.ops.segment_sum(message, col, num_segments=node_feat.shape[0])
        return agg + node_feat
    edge_index = jnp.stack([src, dst])
    h = jnp.maximum(_layernorm(x, axis=-1), 0.0)
    x = x + _L0_gnn_ref(h, src, dst)
    h = jnp.maximum(_layernorm(x, axis=-1), 0.0)
    x = x + _L1_gnn_ref(h, edge_index, edge_attr_4, L1_gnn_W_node, L1_gnn_b_node, L1_gnn_g_node, L1_gnn_beta_node, L1_gnn_W_edge, L1_gnn_b_edge, L1_gnn_g_edge, L1_gnn_beta_edge, L1_gnn_W_msg, L1_gnn_b_msg, L1_gnn_g_msg, L1_gnn_beta_msg)
    return x

_drawn_inputs = setup_inputs


def setup_inputs(seed=0):
    import zlib

    import numpy as np

    out = dict(_drawn_inputs(seed))
    spreads = {'L1_gnn_b_node': (0.0, 0.1),
     'L1_gnn_g_node': (1.0, 0.2),
     'L1_gnn_beta_node': (0.0, 0.1),
     'L1_gnn_b_edge': (0.0, 0.1),
     'L1_gnn_g_edge': (1.0, 0.2),
     'L1_gnn_beta_edge': (0.0, 0.27),
     'L1_gnn_b_msg': (0.0, 0.1),
     'L1_gnn_g_msg': (1.0, 0.2),
     'L1_gnn_beta_msg': (0.0, 0.1)}
    factors = {}
    for name, (base, spread) in spreads.items():
        noise = np.random.default_rng([zlib.crc32(name.encode()), seed]).standard_normal(out[name].shape)
        drawn = base * np.exp(spread * noise) if base else spread * noise
        out[name] = jnp.asarray(drawn.astype(out[name].dtype))
    for name, factor in factors.items():
        out[name] = (out[name] * factor).astype(out[name].dtype)
    return out
```

```python
import concourse.bass as bass
from concourse import mybir
from contextlib import ExitStack

F32 = mybir.dt.float32
I32 = mybir.dt.int32
ALU = mybir.AluOpType
ACT = mybir.ActivationFunctionType
AXX = mybir.AxisListType.X

P = 128
N = 50000
E = 50000
C = 96
ED = 4
EPS = 1e-5
W = 4
NODE_GROUPS = 98
NWIN = W * NODE_GROUPS
NPAD = NWIN * P
FULL_WIN = N // P
REST = N - FULL_WIN * P
T = 8
EDGE_GROUPS = 50
EPAD = EDGE_GROUPS * T * P
PAD_DST = NPAD
DUMP = NPAD + 1
TABLE_ROWS = NPAD + 1 + P
R = 15
ROW_GROUPS = FULL_WIN // R
CHUNK = 500
NCHUNK = E // CHUNK
A1 = C + 1
NACC = 2


class Shared:
    pass


def loop(engine, n, body):
    body(0)
    with engine.Fori(1, n - 1) as i:
        body(i)
    body(n - 1)


def wait(engine, sem, value):
    if not (isinstance(value, int) and value <= 0):
        engine.wait_ge(sem, value)


def is_last(i, n):
    return isinstance(i, int) and i == n - 1


def program(nc, x, src_g, dst_g, dst_row, ea_t, valid, w_node, b_node, g_node, beta_node, w_edge, b_edge,
            g_edge, beta_edge, w_msg, b_msg, g_msg, beta_msg, out):
    h1_tab = nc.dram_tensor("h1_tab", [N, C], F32, kind="Internal").ap()
    p_tab = nc.dram_tensor("p_tab", [NPAD, C], F32, kind="Internal").ap()
    q_tab = nc.dram_tensor("q_tab", [NPAD + 1, C], F32, kind="Internal").ap()
    sums = [nc.dram_tensor(f"sums{a}", [TABLE_ROWS, A1], F32, kind="Internal").ap() for a in range(NACC)]
    msgs = [nc.dram_tensor(f"msgs{a}", [TABLE_ROWS, C], F32, kind="Internal").ap() for a in range(NACC)]

    whole = ExitStack()
    with whole:
        def keep(name, shape, dt=F32):
            return whole.enter_context(nc.sbuf_tensor(name, shape, dt))

        x1 = keep("x1", [P, NWIN * C])
        ident = keep("ident", [P, P])
        ones = keep("ones", [P, P])
        earlier = keep("earlier", [P, P])
        eps = keep("eps", [P, 1])
        dump_row = keep("dump_row", [P, 1])
        w_cat = keep("w_cat", [A1, 3 * C])
        w_ef = keep("w_ef", [C, C])
        w_e = keep("w_e", [ED, C])
        cols = keep("cols", [C, 16])
        be, ge, bte, gn, btn, gm, btm = (cols[:, k:k + 1] for k in range(7))
        small = keep("small", [C, 32])
        rows4 = keep("rows4", [P, 4 * C])
        kept = keep("kept", [P, NODE_GROUPS, 3 * W])
        grams = keep("grams", [C, 2, A1])


        v = Shared()
        v.x, v.src_g, v.dst_g, v.dst_row = x, src_g, dst_g, dst_row
        v.ea_t, v.valid, v.w_node, v.b_node = ea_t, valid, w_node, b_node
        v.g_node, v.beta_node, v.w_edge, v.b_edge = g_node, beta_node, w_edge, b_edge
        v.g_edge, v.beta_edge, v.w_msg, v.b_msg = g_edge, beta_edge, w_msg, b_msg
        v.g_msg, v.beta_msg, v.out, v.h1_tab = g_msg, beta_msg, out, h1_tab
        v.p_tab, v.q_tab, v.sums, v.msgs = p_tab, q_tab, sums, msgs
        v.x1, v.ident, v.ones, v.earlier = x1, ident, ones, earlier
        v.eps, v.dump_row, v.w_cat, v.w_ef = eps, dump_row, w_cat, w_ef
        v.w_e, v.be, v.ge, v.bte = w_e, be, ge, bte
        v.gn, v.btn, v.gm, v.btm = gn, btn, gm, btm
        v.small, v.rows4, v.kept, v.grams = small, rows4, kept, grams
        setup_phase(nc, v)
        edge_phase(nc, v, second=False)
        node_phase(nc, v, last=False)
        edge_phase(nc, v, second=True)
        norm_rows_phase(nc, v)
        node_phase(nc, v, last=True)


def setup_phase(nc, v):
    H = 2
    STEPS = ROW_GROUPS // H
    span = R * C
    main = FULL_WIN * P
    with ExitStack() as st:
        def sb(name, shape, dt=F32):
            return st.enter_context(nc.sbuf_tensor(name, shape, dt))

        def sem(name):
            return st.enter_context(nc.semaphore(name))

        xin = v.x1[:, 0:H * span].rearrange("p (u c) -> p u c", u=H)
        xout = v.x1[:, H * span:2 * H * span].rearrange("p (u c) -> p u c", u=H)
        zero = v.x1[:, 2 * H * span:2 * H * span + 32 * A1]
        ea = v.x1[0:ED, 12000:12000 + 2 * CHUNK].rearrange("p (u c) -> p u c", u=2)
        er = v.x1[0:C, 14000:14000 + 2 * CHUNK].rearrange("p (u c) -> p u c", u=2)
        est = v.x1[0:C, 16000:16000 + 6 * NCHUNK].rearrange("p (n s) -> p n s", s=6)
        pad_row = v.x1[0:1, 17000:17000 + C]
        bn = sb("bn", [P, H, R, 6])
        mom = sb("mom", [P, 8, R])
        ps = [st.enter_context(nc.psum_tensor(f"ps{k}", [P, 512], F32)) for k in range(3)]
        ids, consts = sem("ids"), sem("consts")
        weights, weights2 = sem("weights"), sem("weights2")
        x_in = [sem(f"x_in{u}") for u in range(H)]
        h_out = [sem(f"h_out{u}") for u in range(H)]
        chain, var_ready, std_ready, xn_ready, h_ready = (sem(n) for n in ("chain", "var_ready", "std_ready", "xn_ready", "h_ready"))
        x_free = sem("x_free")
        pads = sem("pads")
        zeroed = sem("zeroed")
        rest_in, rest_out = sem("rest_in"), sem("rest_out")
        ea_in = [sem(f"ea_in{u}") for u in range(2)]
        e_mm, e_relu, e_stat = sem("e_mm"), sem("e_relu"), sem("e_stat")
        fold, e_std, c_row, c_sum, b_moved = sem("fold"), sem("e_std"), sem("c_row"), sem("c_sum"), sem("b_moved")
        xv = v.x[0:main, :].rearrange("(p t) f -> p (t f)", p=P)
        hv = v.h1_tab[0:main, :].rearrange("(p t) f -> p (t f)", p=P)
        steps = STEPS

        with nc.Block() as block:
            @block.sync
            def _(sp):
                for dst, s in ((v.w_cat[0:C, 0:C], v.w_msg[0:C, :]), (v.w_cat[0:C, C:2 * C], v.w_msg[C:2 * C, :]),
                               (v.w_cat[0:C, 2 * C:], v.w_node[:, :]), (v.w_ef[:, :], v.w_msg[2 * C:3 * C, :]),
                               (v.w_e[:, :], v.w_edge[:, :]), (v.w_cat[C:A1, 2 * C:], v.b_node.rearrange("(a n) -> a n", a=1)),
                               (v.be, v.b_edge.rearrange("(n a) -> n a", a=1)), (v.ge, v.g_edge.rearrange("(n a) -> n a", a=1)),
                               (v.bte, v.beta_edge.rearrange("(n a) -> n a", a=1)), (v.gn, v.g_node.rearrange("(n a) -> n a", a=1)),
                               (v.btn, v.beta_node.rearrange("(n a) -> n a", a=1)), (v.gm, v.g_msg.rearrange("(n a) -> n a", a=1)),
                               (v.btm, v.beta_msg.rearrange("(n a) -> n a", a=1)),
                               (v.small[0:1, 31:32], v.valid[0:1, 0:1])):
                    sp.dma_start(dst, s).then_inc(weights, 16)

                def step(i):
                    for u in range(H):
                        g = H * i + u
                        wait(sp, x_free, g - H + 1)
                        sp.dma_start(xin[:, u, :], xv[:, bass.ds(g * span, span)]).then_inc(x_in[u], 16)
                loop(sp, steps, step)
                sp.wait_ge(x_free, ROW_GROUPS)
                sp.dma_start(xin[0:REST, 0, 0:C], v.x[main:N, :]).then_inc(rest_in, 16)
                sp.wait_ge(c_row, 1)
                sp.dma_start(v.w_cat[C:A1, C:2 * C], v.rows4[0:1, 0:C]).then_inc(b_moved, 16)
                sp.wait_ge(b_moved, 16)

            @block.gpsimd
            def _(pool):
                pool.memset(v.ident[:, :], 0.0).then_inc(ids, 1)
                pool.memset(v.earlier[:, :], 1.0).then_inc(ids, 1)
                pool.memset(v.ones[:, :], 1.0).then_inc(ids, 1)
                pool.memset(v.eps[:, :], EPS).then_inc(ids, 1)
                pool.memset(zero, 0.0).then_inc(ids, 1)
                pool.iota(v.dump_row[:, :], [[0, 1]], base=DUMP, channel_multiplier=1,
                          allow_small_or_imprecise_dtypes=True).then_inc(ids, 1)
                pool.wait_ge(ids, 6)
                pool.affine_select(out=v.ident[:, :], in_=v.ident[:, :], compare_op=ALU.not_equal, fill=1.0,
                                   base=0, pattern=[[-1, P]], channel_multiplier=1).then_inc(consts, 1)
                pool.affine_select(out=v.earlier[:, :], in_=v.earlier[:, :], compare_op=ALU.is_gt, fill=0.0,
                                   base=0, pattern=[[-1, P]], channel_multiplier=1).then_inc(consts, 1)
                pool.wait_ge(consts, 2)
                n_zero = 0
                for tab, wdt in [(s, A1) for s in v.sums] + [(m, C) for m in v.msgs]:
                    rows = TABLE_ROWS // P
                    for r0 in range(0, rows, 32):
                        r1 = min(r0 + 32, rows)
                        pool.dma_start(tab[r0 * P:r1 * P, :].rearrange("(p r) f -> p (r f)", p=P),
                                       zero[:, 0:(r1 - r0) * wdt]).then_inc(zeroed, 16)
                        n_zero += 1
                    pool.dma_start(tab[rows * P:TABLE_ROWS, :], zero[0:TABLE_ROWS - rows * P, 0:wdt]).then_inc(zeroed, 16)
                    n_zero += 1
                pool.wait_ge(pads, 2)
                pool.dma_start(v.q_tab[PAD_DST:PAD_DST + 1, :], pad_row).then_inc(zeroed, 16)
                pool.wait_ge(zeroed, 16 * (n_zero + 1))

            def norm(dve, rows, nrow, xi, xo, u, g, loaded, loads, stores):
                wait(dve, loaded, loads)
                for r in range(nrow):
                    last = dve.bn_stats(bn[0:rows, u, r, :], xi[0:rows, r * C:(r + 1) * C])
                last.then_inc(chain, 1)
                m = [mom[0:rows, k, 0:nrow] for k in range(8)]
                me, se, mo, so = (bn[0:rows, u, 0:nrow, k] for k in (1, 2, 4, 5))
                wait(dve, chain, 5 * g + 1)
                dve.tensor_tensor(m[0], me, mo, ALU.add)
                dve.tensor_tensor(m[1], me, mo, ALU.subtract)
                dve.tensor_tensor(m[2], se, so, ALU.add).then_inc(chain, 1)
                wait(dve, chain, 5 * g + 2)
                dve.scalar_tensor_tensor(m[3], m[1], 0.25, m[1], ALU.mult, ALU.mult).then_inc(chain, 1)
                wait(dve, chain, 5 * g + 3)
                dve.scalar_tensor_tensor(m[4], m[2], 1.0 / C, m[3], ALU.mult, ALU.add).then_inc(var_ready, 1)
                wait(dve, std_ready, g + 1)
                dve.reciprocal(m[6], m[5]).then_inc(chain, 1)
                wait(dve, chain, 5 * g + 4)
                dve.scalar_tensor_tensor(m[7], m[0], -0.5, m[6], ALU.mult, ALU.mult).then_inc(chain, 1)
                wait(dve, chain, 5 * g + 5)
                wait(dve, h_out[u], 16 * stores)
                for r in range(nrow):
                    last = dve.tensor_scalar(xo[0:rows, r * C:(r + 1) * C], xi[0:rows, r * C:(r + 1) * C],
                                             m[6][:, r:r + 1], m[7][:, r:r + 1], ALU.mult, ALU.add)
                last.then_inc(x_free, 1)

            @block.vector
            def _(dve):
                dve.memset(v.w_cat[C:A1, 0:C], 0.0).then_inc(pads, 1)
                dve.memset(pad_row, -1e30).then_inc(pads, 1)

                def step(i):
                    for u in range(H):
                        norm(dve, P, R, xin[:, u, :], xout[:, u, :], u, H * i + u, x_in[u], 16 * (i + 1), i)
                loop(dve, steps, step)
                norm(dve, REST, 1, xin[:, 0, :], xout[:, 0, :], 0, ROW_GROUPS, rest_in, 16, STEPS)

                def estep(i):
                    for u in range(2):
                        wait(dve, e_relu, 2 * i + u + 1)
                        dve.bn_stats(est[:, bass.ds(2 * i + u, 1), :], er[:, u, :]).then_inc(e_stat, 1)
                loop(dve, NCHUNK // 2, estep)
                dve.wait_ge(e_stat, NCHUNK)
                s = v.small
                dve.bn_aggr(s[:, 0:2], est[:, :, :]).then_inc(fold, 1)
                dve.wait_ge(e_std, 1)
                dve.reciprocal(s[:, 3:4], s[:, 2:3]).then_inc(fold, 1)
                dve.wait_ge(fold, 2)
                dve.tensor_tensor(s[:, 4:5], s[:, 3:4], v.ge, ALU.mult).then_inc(fold, 1)
                dve.wait_ge(fold, 3)
                dve.tensor_tensor(s[:, 5:6], s[:, 4:5], s[:, 0:1], ALU.mult).then_inc(fold, 1)
                dve.wait_ge(fold, 4)
                dve.tensor_tensor(s[:, 6:7], v.bte, s[:, 5:6], ALU.subtract).then_inc(fold, 1)
                dve.wait_ge(c_sum, 1)
                dve.tensor_scalar(v.w_ef[:, :], v.w_ef[:, :], s[:, 4:5], None, ALU.mult).then_inc(fold, 1)
                dve.tensor_tensor(v.rows4[0:1, 0:C], ps[2][0:1, 0:C], v.rows4[0:1, C:2 * C], ALU.add).then_inc(c_row, 1)

            @block.tensor
            def _(pe):
                pe.wait_ge(weights, 16 * 14)

                def estep(i):
                    for u in range(2):
                        wait(pe, ea_in[u], 16 * (i + 1))
                        wait(pe, e_relu, 2 * i + u - 1)
                        pe.matmul(ps[u][0:C, 0:CHUNK], v.w_e[:, :], ea[:, u, :], start=True, stop=True).then_inc(e_mm, 1)
                loop(pe, NCHUNK // 2, estep)
                pe.wait_ge(fold, 5)
                pe.matmul(ps[2][0:1, 0:C], v.small[:, 6:7], v.w_ef[:, :], start=True, stop=True).then_inc(c_sum, 1)

            @block.scalar
            def _(act):
                act.dma_start(v.rows4[0:1, C:2 * C], v.b_msg.rearrange("(a n) -> a n", a=1)).then_inc(weights2, 16)
                act.wait_ge(weights, 16 * 14)
                act.wait_ge(weights2, 16)
                act.wait_ge(ids, 6)

                def root(rows, nrow, g):
                    wait(act, var_ready, g + 1)
                    act.activation(mom[0:rows, 5, 0:nrow], mom[0:rows, 4, 0:nrow], ACT.Sqrt,
                                   bias=v.eps[0:rows, :]).then_inc(std_ready, 1)

                def step(i):
                    for u in range(H):
                        g = H * i + u
                        root(P, R, g)
                        wait(act, x_free, g + 1)
                        act.activation(xout[:, u, :], xout[:, u, :], ACT.Relu).then_inc(h_ready, 1)
                        wait(act, h_ready, g + 1)
                        act.dma_start(hv[:, bass.ds(g * span, span)], xout[:, u, :]).then_inc(h_out[u], 16)
                loop(act, steps, step)
                root(REST, 1, ROW_GROUPS)
                act.wait_ge(x_free, ROW_GROUPS + 1)
                act.activation(xout[0:REST, 0, 0:C], xout[0:REST, 0, 0:C], ACT.Relu).then_inc(h_ready, 1)
                act.wait_ge(h_ready, ROW_GROUPS + 1)
                act.dma_start(v.h1_tab[main:N, :], xout[0:REST, 0, 0:C]).then_inc(rest_out, 16)

                def load(i, u):
                    act.dma_start(ea[:, u, :], v.ea_t[:, bass.ds((2 * i + u) * CHUNK, CHUNK)]).then_inc(ea_in[u], 16)
                for u in range(2):
                    load(0, u)

                def estep(i):
                    for u in range(2):
                        wait(act, e_mm, 2 * i + u + 1)
                        if not is_last(i, NCHUNK // 2):
                            load(i + 1, u)
                        wait(act, e_stat, 2 * i + u - 1)
                        act.activation(er[:, u, :], ps[u][0:C, 0:CHUNK], ACT.Relu, bias=v.be).then_inc(e_relu, 1)
                loop(act, NCHUNK // 2, estep)
                act.wait_ge(fold, 1)
                act.activation(v.small[:, 2:3], v.small[:, 1:2], ACT.Sqrt, bias=v.eps[0:C, :]).then_inc(e_std, 1)
                for u in range(H):
                    act.wait_ge(h_out[u], 16 * steps)
                act.wait_ge(rest_out, 16)


def edge_phase(nc, v, second):
    H = 2
    STEPS = EDGE_GROUPS // H
    width = C if second else A1
    tables = v.msgs if second else v.sums
    tag = "b" if second else "a"
    HB = T // 4
    with ExitStack() as st:
        def sb(name, shape, dt=F32):
            return st.enter_context(nc.sbuf_tensor(name + tag, shape, dt))

        def sem(name):
            return st.enter_context(nc.semaphore(name + tag))

        def bank(name, n=1):
            return st.enter_context(nc.psum_tensor(name + tag, [P, n * 512], F32))

        src, dst, rows = (sb(n, [P, H, T], I32) for n in ("src", "dst", "rows"))
        dstf, cnt, away = (sb(n, [P, H, T]) for n in ("dstf", "cnt", "away"))
        scrap = sb("scrap", [P, P])
        if second:
            dst_rows = sb("dst_rows", [P, 1, T * P], I32)
            same = sb("same", [P, 1, T, P])
            got = sb("got", [P, H, T, C])
            gotq = sb("gotq", [P, H, T, C])
            msg = sb("msg", [P, 1, T, A1])
            tot = sb("tot", [P, H, T, C])
            ea = sb("ea", [ED, 1, T * P])
            ef = sb("ef", [C, 1, T * P])
            BH = 1
        else:
            dst_rows = sb("dst_rows", [P, H, T * P], I32)
            free = v.x1[:, :]
            o = H * T * P
            same = free[:, 0:o].rearrange("p (u k c) -> p u k c", u=H, k=T)
            got = free[:, o:o + H * T * A1].rearrange("p (u k c) -> p u k c", u=H, k=T)
            tot = free[:, 2 * o:2 * o + H * T * A1].rearrange("p (u k c) -> p u k c", u=H, k=T)
            BH = H
        ps_tot = bank("ps_tot", HB)
        if second:
            ps_ef, ps_msg, ps_gram = bank("ps_ef", HB), bank("ps_msg", HB), bank("ps_gram")
        idx_in = [sem(f"idx_in{u}") for u in range(H)]
        marks_in = [sem(f"marks_in{u}") for u in range(H)]
        gathered = [sem(f"gathered{u}") for u in range(H)]
        added = [sem(f"added{a}") for a in range(NACC)]
        ea_in = sem("ea_in")
        floats, marked, differ, masked, rows_ready = (sem(n) for n in ("floats", "marked", "differ", "masked", "rows_ready"))
        totals, copied, turn, ready = (sem(n) for n in ("totals", "copied", "turn", "ready"))
        ef_mm, ef_relu, msg_mm, with_p, with_q, msg_ready, gram_done = (
            sem(n) for n in ("ef_mm", "ef_relu", "msg_mm", "with_p", "with_q", "msg_ready", "gram_done"))

        def bu(u):
            return u % BH

        with nc.Block() as block:
            @block.sync
            def _(sp):
                def step(i):
                    for u in range(H):
                        g = H * i + u
                        wait(sp, gathered[u], (32 if second else 16) * T * i)
                        wait(sp, rows_ready, g - 1)
                        sp.dma_start(src[:, u, :], v.src_g[:, bass.ds(g * T, T)]).then_inc(idx_in[u], 16)
                        sp.dma_start(dst[:, u, :], v.dst_g[:, bass.ds(g * T, T)]).then_inc(idx_in[u], 16)
                        wait(sp, marked, g - BH + 1)
                        sp.dma_start(dst_rows[:, bu(u), :], v.dst_row[:, bass.ds(g * T * P, T * P)]
                                     .to_broadcast([P, T * P])).then_inc(marks_in[u], 16)
                        if second:
                            wait(sp, ef_mm, HB * g)
                            sp.dma_start(ea[:, 0, :], v.ea_t[:, bass.ds(g * T * P, T * P)]).then_inc(ea_in, 16)
                loop(sp, STEPS, step)

            @block.gpsimd
            def _(pool):
                def gather(i, u):
                    g = H * i + u
                    wait(pool, idx_in[u], 32 * (i + 1))
                    wait(pool, msg_ready if second else totals, (g - 1) * HB)
                    pool.sem_inc(turn, 1)
                    for k in range(T):
                        pool.indirect_dma_start(got[:, u, k, 0:C], None, (v.p_tab if second else v.h1_tab)[:, :],
                                                bass.IndirectOffsetOnAxis(ap=src[:, u, k:k + 1], axis=0)
                                                ).then_inc(gathered[u], 16)
                        if second:
                            pool.indirect_dma_start(gotq[:, u, k, :], None, v.q_tab[:, :],
                                                    bass.IndirectOffsetOnAxis(ap=dst[:, u, k:k + 1], axis=0)
                                                    ).then_inc(gathered[u], 16)

                def scatter(i, u):
                    g = H * i + u
                    wait(pool, rows_ready, g + 1)
                    for k in range(T):
                        if k % 4 == 0:
                            wait(pool, copied, HB * g + k // 4 + 1)
                        wait(pool, added[k % NACC], g * (16 * T // NACC) + 16 * (k // NACC))
                        pool.sem_inc(turn, 1)
                        pool.indirect_dma_start(tables[k % NACC][:, :],
                                                bass.IndirectOffsetOnAxis(ap=rows[:, u, k:k + 1], axis=0),
                                                tot[:, u, k, :], None, compute_op=ALU.add).then_inc(added[k % NACC], 16)
                gather(0, 0)

                def step(i):
                    gather(i, 1)
                    scatter(i, 0)
                    if not is_last(i, STEPS):
                        gather(i + 1, 0)
                    scatter(i, 1)
                loop(pool, STEPS, step)
                for a in range(NACC):
                    pool.wait_ge(added[a], 16 * EDGE_GROUPS * T // NACC)

            @block.vector
            def _(dve):
                if second:
                    dve.memset(msg[:, 0, :, C:A1], 1.0).then_inc(ready, 1)
                else:
                    for u in range(H):
                        dve.memset(got[:, u, :, C:A1], 1.0).then_inc(ready, 1)

                def step(i):
                    for u in range(H):
                        g = H * i + u
                        wait(dve, idx_in[u], 32 * (i + 1))
                        dve.tensor_copy(dstf[:, u, :], dst[:, u, :]).then_inc(floats, 1)
                        wait(dve, floats, g + 1)
                        wait(dve, marks_in[u], 16 * (i + 1))
                        wait(dve, totals, HB * (g - BH + 1))
                        if second:
                            wait(dve, gram_done, g)
                        for k in range(T):
                            line = dst_rows[:, bu(u), k * P:(k + 1) * P]
                            dve.tensor_scalar(same[:, bu(u), k, :], line, dstf[:, u, k:k + 1], None, ALU.is_equal)
                            dve.scalar_tensor_tensor(scrap[:, :], line, dstf[:, u, k:k + 1], v.earlier[:, :],
                                                     ALU.is_equal, ALU.mult, accum_out=cnt[:, u, k:k + 1])
                            last = dve.drain()
                        last.then_inc(marked, 1)
                        wait(dve, marked, g + 1)
                        dve.tensor_scalar(cnt[:, u, :], cnt[:, u, :], 1.0, None, ALU.min)
                        dve.tensor_scalar(away[:, u, :], dstf[:, u, :], -1.0, v.dump_row[:, :], ALU.mult, ALU.add).then_inc(differ, 1)
                        wait(dve, differ, g + 1)
                        dve.tensor_tensor(away[:, u, :], away[:, u, :], cnt[:, u, :], ALU.mult).then_inc(masked, 1)
                        wait(dve, masked, g + 1)
                        for a in range(NACC):
                            wait(dve, added[a], (g - 1) * (16 * T // NACC))
                        dve.tensor_tensor(rows[:, u, :], away[:, u, :], dstf[:, u, :], ALU.add).then_inc(rows_ready, 1)
                        if second:
                            wait(dve, gathered[u], 32 * T * (i + 1))
                            for h in range(HB):
                                ks = slice(4 * h, 4 * h + 4)
                                wait(dve, msg_mm, HB * g + h + 1)
                                dve.tensor_tensor(got[:, u, ks, :], got[:, u, ks, :],
                                                  ps_msg[:, h * 512:h * 512 + 4 * C].rearrange("p (k c) -> p k c", k=4),
                                                  ALU.add).then_inc(with_p, 1)
                                wait(dve, with_p, HB * g + h + 1)
                                dve.tensor_tensor(got[:, u, ks, :], got[:, u, ks, :], gotq[:, u, ks, :],
                                                  ALU.add).then_inc(with_q, 1)
                        for h in range(HB):
                            wait(dve, totals, HB * g + h + 1)
                            dve.tensor_copy(tot[:, u, 4 * h:4 * h + 4, :],
                                            ps_tot[:, h * 512:h * 512 + 4 * width].rearrange("p (k c) -> p k c", k=4)
                                            ).then_inc(copied, 1)
                loop(dve, STEPS, step)
                if second:
                    dve.wait_ge(gram_done, EDGE_GROUPS)
                    dve.tensor_copy(v.grams[:, 1, :], ps_gram[0:C, 0:A1]).then_inc(ready, 1)
                    dve.wait_ge(ready, 2)

            @block.tensor
            def _(pe):
                pe.wait_ge(ready, 1 if second else H)

                def step(i):
                    for u in range(H):
                        g = H * i + u
                        if second:
                            wait(pe, ea_in, 16 * (g + 1))
                            for h in range(HB):
                                wait(pe, ef_relu, HB * (g - 1) + h + 1)
                                pe.matmul(ps_ef[0:C, h * 512:h * 512 + 512], v.w_e[:, :], ea[:, 0, h * 512:h * 512 + 512],
                                          start=True, stop=True).then_inc(ef_mm, 1)
                            for k in range(T):
                                h = k // 4
                                if k % 4 == 0:
                                    wait(pe, ef_relu, HB * g + h + 1)
                                    wait(pe, with_p, HB * (g - 1) + h + 1)
                                c0 = h * 512 + (k % 4) * C
                                m = pe.matmul(ps_msg[:, c0:c0 + C], ef[:, 0, k * P:(k + 1) * P], v.w_ef[:, :],
                                              start=True, stop=True)
                                if k % 4 == 3:
                                    m.then_inc(msg_mm, 1)
                        wait(pe, marked, g + 1)
                        if not second:
                            wait(pe, gathered[u], 16 * T * (i + 1))
                        for k in range(T):
                            h = k // 4
                            if k % 4 == 0:
                                wait(pe, copied, HB * (g - 1) + h + 1)
                                if second:
                                    wait(pe, msg_ready, HB * g + h + 1)
                            c0 = h * 512 + (k % 4) * width
                            m = pe.matmul(ps_tot[:, c0:c0 + width], same[:, bu(u), k, :],
                                          msg[:, 0, k, 0:C] if second else got[:, u, k, :], start=True, stop=True)
                            if k % 4 == 3:
                                m.then_inc(totals, 1)
                        if second:
                            for k in range(T):
                                first = isinstance(i, int) and i == 0 and u == 0 and k == 0
                                end = is_last(i, STEPS) and u == H - 1 and k == T - 1
                                m = pe.matmul(ps_gram[0:C, 0:A1], msg[:, 0, k, 0:C], msg[:, 0, k, :], start=first, stop=end,
                                              skip_group_check=True)
                            m.then_inc(gram_done, 1)
                loop(pe, STEPS, step)

            if second:
                @block.scalar
                def _(act):
                    def step(i):
                        for u in range(H):
                            g = H * i + u
                            for h in range(HB):
                                wait(act, ef_mm, HB * g + h + 1)
                                wait(act, msg_mm, HB * (g - 1) + h + 1)
                                act.activation(ef[:, 0, h * 512:h * 512 + 512], ps_ef[0:C, h * 512:h * 512 + 512], ACT.Relu,
                                               bias=v.be).then_inc(ef_relu, 1)
                            for h in range(HB):
                                wait(act, with_q, HB * g + h + 1)
                                wait(act, gram_done, g)
                                act.activation(msg[:, 0, 4 * h:4 * h + 4, 0:C], got[:, u, 4 * h:4 * h + 4, :],
                                               ACT.Relu).then_inc(msg_ready, 1)
                    loop(act, STEPS, step)


def node_phase(nc, v, last):
    H = 2
    STEPS = NODE_GROUPS // H
    width = C if last else A1
    tables = v.msgs if last else v.sums
    tag = "d" if last else "c"
    WP = W * P
    with ExitStack() as st:
        def sb(name, shape, dt=F32):
            return st.enter_context(nc.sbuf_tensor(name + tag, shape, dt))

        def sem(name):
            return st.enter_context(nc.semaphore(name + tag))

        def bank(name, n=1):
            return st.enter_context(nc.psum_tensor(name + tag, [P, n * 512], F32))

        xs = sb("xs", [P, H, W, C])
        sa, sb_ = sb("sa", [P, H, W, width]), sb("sb", [P, H, W, width])
        xn = sb("xn", [P, H, W, C])
        ht = sb("ht", [A1, H, WP])
        ps_t, ps_o = bank("ps_t", H), bank("ps_o", H if last else W)
        mine = sb("mine", [P, H, 3 * W])
        y = sb("y", [P, H, W, C if last else A1])
        if last:
            fin = sb("fin", [P, H, W, C])
        else:
            pq = sb("pq", [P, H, W, 2 * C])
            bn, mom = sb("bn", [P, H, W, 6]), sb("mom", [P, H, 8, W])
            ps_gram = bank("ps_gram")
        names = ("chain", "xn_ready", "t_mm", "ht_ready", "o_mm", "y_ready", "gram_done", "kept_it", "turn",
                 "var_ready", "std_ready", "x1_ready", "scaled", "y_scaled", "fin_ready", "pq_ready", "took", "ready", "pool_chain")
        (chain, xn_ready, t_mm, ht_ready, o_mm, y_ready, gram_done, kept_it, turn, var_ready, std_ready, x1_ready,
         scaled, y_scaled, fin_ready, pq_ready, took, ready, pool_chain) = (sem(n) for n in names)
        loaded = [sem(f"loaded{u}") for u in range(H)]
        stored = [sem(f"stored{u}") for u in range(H)]
        xw = v.x[0:FULL_WIN * P, :].rearrange("(w p) f -> p w f", p=P)
        tw = [t[0:NPAD, :].rearrange("(w p) f -> p w f", p=P) for t in tables]
        LOADS = 16 * (3 if last else 4)
        LAST_LOADS = LOADS + (0 if last else 3 * 16)

        def bias_rows(u):
            return ht[C:A1, u, :]

        with nc.Block() as block:
            @block.sync
            def _(sp):
                def step(i):
                    for u in range(H):
                        g = H * i + u
                        wait(sp, fin_ready if last else x1_ready, g - 1)
                        wait(sp, o_mm, g - 1)
                        if not last:
                            if is_last(i, STEPS) and u == H - 1:
                                k = FULL_WIN - W * g
                                wait(sp, kept_it, g - 1)
                                sp.dma_start(xs[:, u, 0:k, :], xw[:, FULL_WIN - k:FULL_WIN, :]).then_inc(loaded[u], 16)
                                sp.dma_start(xs[0:REST, u, k, :], v.x[FULL_WIN * P:N, :]).then_inc(loaded[u], 16)
                                sp.dma_start(xs[REST:P, u, k, :], v.sums[0][N:(FULL_WIN + 1) * P, 0:C]).then_inc(loaded[u], 16)
                                sp.dma_start(xs[:, u, k + 1:W, :], tw[0][:, FULL_WIN + 1:NWIN, 0:C]).then_inc(loaded[u], 16)
                                assert k + 2 == W
                            else:
                                wait(sp, kept_it, g - 1)
                                sp.dma_start(xs[:, u, :, :], xw[:, bass.ds(W * g, W), :]).then_inc(loaded[u], 16)
                        for s, t in ((sa, tw[0]), (sb_, tw[1])):
                            sp.dma_start(s[:, u, :, :], t[:, bass.ds(W * g, W), :]).then_inc(loaded[u], 16)
                        sp.dma_start(bias_rows(u), v.valid[:, bass.ds(g * WP, WP)]).then_inc(loaded[u], 16)
                loop(sp, STEPS, step)

            @block.gpsimd
            def _(pool):
                def step(i):
                    for u in range(H):
                        g = H * i + u
                        if last:
                            wait(pool, fin_ready, g - 1)
                            pool.sem_inc(turn, 1)
                            pool.tensor_copy(xs[:, u, :, :].rearrange("p w c -> p (w c)"), v.x1[:, bass.ds(g * W * C, W * C)])
                            pool.tensor_copy(mine[:, u, :], v.kept[:, bass.ds(g, 1), :].rearrange("p a c -> p (a c)")).then_inc(took, 1)
                            wait(pool, y_ready, g + 1)
                            a_node = v.rows4[:, 0:C].unsqueeze(1).to_broadcast([P, W, C])
                            pool.tensor_tensor(y[:, u, :, :], y[:, u, :, :], a_node, ALU.mult).then_inc(pool_chain, 1)
                            wait(pool, pool_chain, 2 * g + 1)
                            pool.tensor_tensor(y[:, u, :, :], y[:, u, :, :], xs[:, u, :, :], ALU.add).then_inc(pool_chain, 1)
                            wait(pool, pool_chain, 2 * g + 2)
                            pool.sem_inc(y_scaled, 1)
                        else:
                            wait(pool, xn_ready, g + 1)
                            pool.sem_inc(turn, 1)
                            pool.tensor_copy(v.x1[:, bass.ds(g * W * C, W * C)], xs[:, u, :, :].rearrange("p w c -> p (w c)"))
                            pool.tensor_copy(v.kept[:, bass.ds(g, 1), :].rearrange("p a c -> p (a c)"), mine[:, u, :]).then_inc(kept_it, 1)
                loop(pool, STEPS, step)

            @block.vector
            def _(dve):
                if not last:
                    for u in range(H):
                        dve.memset(y[:, u, :, C:A1], 1.0).then_inc(ready, 1)

                def make_x1(i, u, g):
                    m = [mom[:, u, k, :] for k in range(8)]
                    rstd, shift, dg = (mine[:, u, k * W:(k + 1) * W] for k in range(3))
                    wait(dve, kept_it, g - 1)
                    dve.tensor_tensor(sa[:, u, :, :], sa[:, u, :, :], sb_[:, u, :, :], ALU.add).then_inc(chain, 1)
                    wait(dve, chain, 7 * g + 1)
                    dve.tensor_copy(dg, sa[:, u, :, C])
                    dve.tensor_scalar(m[0], sa[:, u, :, C], 1.0, None, ALU.max).then_inc(chain, 1)
                    wait(dve, chain, 7 * g + 2)
                    dve.reciprocal(m[1], m[0]).then_inc(chain, 1)
                    wait(dve, chain, 7 * g + 3)
                    for w in range(W):
                        last_ = dve.scalar_tensor_tensor(xs[:, u, w, :], sa[:, u, w, 0:C], m[1][:, w:w + 1], xs[:, u, w, :],
                                                         ALU.mult, ALU.add)
                    last_.then_inc(x1_ready, 1)
                    wait(dve, x1_ready, g + 1)
                    for w in range(W):
                        last_ = dve.bn_stats(bn[:, u, w, :], xs[:, u, w, :])
                    last_.then_inc(chain, 1)
                    wait(dve, chain, 7 * g + 4)
                    me, se, mo, so = (bn[:, u, :, k] for k in (1, 2, 4, 5))
                    dve.tensor_tensor(m[2], me, mo, ALU.add)
                    dve.tensor_tensor(m[3], me, mo, ALU.subtract)
                    dve.tensor_tensor(m[4], se, so, ALU.add).then_inc(chain, 1)
                    wait(dve, chain, 7 * g + 5)
                    dve.scalar_tensor_tensor(m[5], m[3], 0.25, m[3], ALU.mult, ALU.mult).then_inc(chain, 1)
                    wait(dve, chain, 7 * g + 6)
                    dve.scalar_tensor_tensor(m[6], m[4], 1.0 / C, m[5], ALU.mult, ALU.add).then_inc(var_ready, 1)
                    wait(dve, std_ready, g + 1)
                    dve.reciprocal(rstd, m[7]).then_inc(chain, 1)
                    wait(dve, chain, 7 * g + 7)
                    dve.scalar_tensor_tensor(shift, m[2], -0.5, rstd, ALU.mult, ALU.mult).then_inc(scaled, 1)
                    wait(dve, scaled, g + 1)

                def step(i):
                    for u in range(H):
                        g = H * i + u
                        wait(dve, loaded[u], LAST_LOADS + LOADS * i if is_last(i, STEPS) and u == H - 1 else LOADS * (i + 1))
                        if last:
                            wait(dve, took, g + 1)
                        else:
                            make_x1(i, u, g)
                        wait(dve, t_mm, g - 1)
                        for w in range(W):
                            last_ = dve.tensor_scalar(xn[:, u, w, :], xs[:, u, w, :], mine[:, u, w:w + 1],
                                                      mine[:, u, W + w:W + w + 1], ALU.mult, ALU.add)
                        last_.then_inc(xn_ready, 1)
                        if last:
                            c_node, a_msg, c_msg = (v.rows4[:, k * C:(k + 1) * C] for k in (1, 2, 3))
                            wait(dve, stored[u], 16 * i)
                            dve.tensor_tensor(sa[:, u, :, :], sa[:, u, :, :], sb_[:, u, :, :], ALU.add).then_inc(chain, 1)
                            wait(dve, chain, 4 * g + 1)
                            dve.tensor_tensor(sa[:, u, :, :], sa[:, u, :, :], a_msg.unsqueeze(1).to_broadcast([P, W, C]),
                                              ALU.mult).then_inc(chain, 1)
                            wait(dve, chain, 4 * g + 2)
                            for w in range(W):
                                last_ = dve.scalar_tensor_tensor(sa[:, u, w, :], c_msg, mine[:, u, 2 * W + w:2 * W + w + 1],
                                                                 sa[:, u, w, :], ALU.mult, ALU.add)
                            last_.then_inc(chain, 1)
                            wait(dve, chain, 4 * g + 3)
                            dve.tensor_tensor(sa[:, u, :, :], sa[:, u, :, :], c_node.unsqueeze(1).to_broadcast([P, W, C]),
                                              ALU.add).then_inc(chain, 1)
                            wait(dve, chain, 4 * g + 4)
                            wait(dve, y_scaled, g + 1)
                            dve.tensor_tensor(fin[:, u, :, :], sa[:, u, :, :], y[:, u, :, :], ALU.add).then_inc(fin_ready, 1)
                loop(dve, STEPS, step)
                if not last:
                    dve.wait_ge(gram_done, NODE_GROUPS)
                    dve.tensor_copy(v.grams[:, 0, :], ps_gram[0:C, 0:A1]).then_inc(ready, 1)
                    dve.wait_ge(ready, H + 1)

            @block.tensor
            def _(pe):
                if not last:
                    pe.wait_ge(ready, H)

                def step(i):
                    for u in range(H):
                        g = H * i + u
                        wait(pe, xn_ready, g + 1)
                        wait(pe, ht_ready, g - 1)
                        for w in range(W):
                            m = pe.transpose(ps_t[0:C, u * 512 + w * P:u * 512 + (w + 1) * P], xn[:, u, w, :], v.ident[:, :])
                        m.then_inc(t_mm, 1)
                        wait(pe, ht_ready, g + 1)
                        wait(pe, loaded[u], LAST_LOADS + LOADS * i if is_last(i, STEPS) and u == H - 1 else LOADS * (i + 1))
                        if last:
                            wait(pe, y_ready, g - 1)
                            for w in range(W):
                                m = pe.matmul(ps_o[:, u * 512 + w * C:u * 512 + (w + 1) * C], ht[:, u, w * P:(w + 1) * P],
                                              v.w_cat[:, 2 * C:], start=True, stop=True)
                            m.then_inc(o_mm, 1)
                        else:
                            wait(pe, y_ready, g)
                            for w in range(W):
                                m = pe.matmul(ps_o[:, w * 512:w * 512 + 3 * C], ht[:, u, w * P:(w + 1) * P], v.w_cat[:, :],
                                              start=True, stop=True)
                            m.then_inc(o_mm, 1)
                            wait(pe, y_ready, g + 1)
                            for w in range(W):
                                first = isinstance(i, int) and i == 0 and u == 0 and w == 0
                                end = is_last(i, STEPS) and u == H - 1 and w == W - 1
                                m = pe.matmul(ps_gram[0:C, 0:A1], y[:, u, w, 0:C], y[:, u, w, :], start=first, stop=end,
                                              skip_group_check=True)
                            m.then_inc(gram_done, 1)
                loop(pe, STEPS, step)

            @block.scalar
            def _(act):
                def step(i):
                    for u in range(H):
                        g = H * i + u
                        if not last:
                            wait(act, var_ready, g + 1)
                            act.activation(mom[:, u, 7, :], mom[:, u, 6, :], ACT.Sqrt, bias=v.eps[:, :]).then_inc(std_ready, 1)
                        wait(act, t_mm, g + 1)
                        wait(act, o_mm, g - 1)
                        act.activation(ht[0:C, u, :], ps_t[0:C, u * 512:u * 512 + WP], ACT.Relu).then_inc(ht_ready, 1)
                        wait(act, o_mm, g + 1)
                        if last:
                            wait(act, fin_ready, g - 1)
                            act.activation(y[:, u, :, :], ps_o[:, u * 512:u * 512 + W * C].rearrange("p (w c) -> p w c", w=W),
                                           ACT.Relu).then_inc(y_ready, 1)
                            wait(act, fin_ready, g + 1)
                            if is_last(i, STEPS) and u == H - 1:
                                k = FULL_WIN - W * g
                                act.dma_start(v.out[W * g * P:FULL_WIN * P, :].rearrange("(w p) f -> p w f", p=P),
                                              fin[:, u, 0:k, :]).then_inc(stored[u], 16)
                                act.dma_start(v.out[FULL_WIN * P:N, :], fin[0:REST, u, k, :]).then_inc(stored[u], 16)
                            else:
                                act.dma_start(v.out[bass.ds(g * WP, WP), :].rearrange("(w p) f -> p w f", p=P),
                                              fin[:, u, :, :]).then_inc(stored[u], 16)
                        else:
                            o = ps_o[:, :].rearrange("p (w c) -> p w c", w=W)
                            wait(act, stored[u], 32 * i)
                            act.activation(pq[:, u, :, :], o[:, :, 0:2 * C], ACT.Copy).then_inc(pq_ready, 1)
                            wait(act, gram_done, g - 1)
                            act.activation(y[:, u, :, 0:C], o[:, :, 2 * C:3 * C], ACT.Relu).then_inc(y_ready, 1)
                            wait(act, pq_ready, g + 1)
                            for t, part in ((v.p_tab, pq[:, u, :, 0:C]), (v.q_tab, pq[:, u, :, C:2 * C])):
                                act.dma_start(t[bass.ds(g * WP, WP), :].rearrange("(w p) f -> p w f", p=P), part
                                              ).then_inc(stored[u], 16)
                loop(act, STEPS, step)
                act.wait_ge(stored[0], (1 if last else 2) * 16 * STEPS)
                act.wait_ge(stored[1], (16 * STEPS + 16) if last else 32 * STEPS)


def norm_rows_phase(nc, v):
    with ExitStack() as st:
        diag = st.enter_context(nc.sbuf_tensor("diag", [C, 4, C], F32))
        scrap = st.enter_context(nc.sbuf_tensor("scrap_n", [C, C], F32))
        ps = st.enter_context(nc.psum_tensor("ps_rows", [P, 512], F32))
        chain, std_ready, diag_ready, rows_mm = (st.enter_context(nc.semaphore(n)) for n in ("chain_n", "std_n", "diag_n", "rows_n"))
        s = v.small
        with nc.Block() as block:
            @block.vector
            def _(dve):
                n = [0]

                def link(ins):
                    n[0] += 1
                    ins.then_inc(chain, 1)
                    dve.wait_ge(chain, n[0])

                for l, (gamma, beta) in enumerate(((v.gn, v.btn), (v.gm, v.btm))):
                    sq, mean, msq, var, std, rstd, a, am, c = (s[:, 9 * l + k:9 * l + k + 1] for k in range(9))
                    count = (N, E)[l]
                    link(dve.scalar_tensor_tensor(scrap[:, :], v.grams[:, l, 0:C], 1.0, v.ident[0:C, 0:C], ALU.mult, ALU.mult,
                                                  accum_out=sq))
                    link(dve.tensor_scalar(mean, v.grams[:, l, C:A1], 1.0 / count, None, ALU.mult))
                    link(dve.tensor_tensor(msq, mean, mean, ALU.mult))
                    dve.scalar_tensor_tensor(var, sq, 1.0 / count, msq, ALU.mult, ALU.subtract).then_inc(chain, 1)
                    n[0] += 1
                    dve.wait_ge(std_ready, l + 1)
                    link(dve.reciprocal(rstd, std))
                    link(dve.tensor_tensor(a, gamma, rstd, ALU.mult))
                    link(dve.tensor_tensor(am, a, mean, ALU.mult))
                    link(dve.tensor_tensor(c, beta, am, ALU.subtract))
                    for k, col in ((2 * l, a), (2 * l + 1, c)):
                        dve.tensor_scalar(diag[:, k, :], v.ident[0:C, 0:C], col, None, ALU.mult).then_inc(diag_ready, 1)
                dve.wait_ge(rows_mm, 1)
                link(dve.tensor_copy(v.rows4[:, :], ps[:, 0:4 * C]))

            @block.scalar
            def _(act):
                for l in range(2):
                    act.wait_ge(chain, 8 * l + 4)
                    act.activation(s[:, 9 * l + 4:9 * l + 5], s[:, 9 * l + 3:9 * l + 4], ACT.Sqrt, bias=v.eps[0:C, :]).then_inc(std_ready, 1)

            @block.tensor
            def _(pe):
                pe.wait_ge(diag_ready, 4)
                pe.matmul(ps[:, 0:4 * C], v.ones[0:C, :], diag[:, :, :].rearrange("p k c -> p (k c)"),
                          start=True, stop=True).then_inc(rows_mm, 1)


_OUT = ((N, C), "float32")


def kernel(x, src, dst, edge_attr_4, L1_gnn_W_node, L1_gnn_b_node, L1_gnn_g_node, L1_gnn_beta_node, L1_gnn_W_edge,
           L1_gnn_b_edge, L1_gnn_g_edge, L1_gnn_beta_edge, L1_gnn_W_msg, L1_gnn_b_msg, L1_gnn_g_msg, L1_gnn_beta_msg):
    import numpy as np
    import concourse.bacc as bacc
    from concourse.bass_utils import run_bass_kernel_spmd as run

    def padded(a, fill):
        a = np.asarray(a)
        return np.concatenate([a, np.full((EPAD - E,) + a.shape[1:], fill, a.dtype)])

    src_p, dst_p = padded(src, 0), padded(dst, PAD_DST)
    valid = np.zeros((1, NPAD), np.float32)
    valid[0, :N] = 1.0
    arrays = {
        "x": x, "src_g": src_p.reshape(-1, P).T, "dst_g": dst_p.reshape(-1, P).T, "dst_row": dst_p.reshape(1, -1),
        "ea_t": padded(edge_attr_4, 0).T, "valid": valid,
        "w_node": L1_gnn_W_node, "b_node": L1_gnn_b_node, "g_node": L1_gnn_g_node, "beta_node": L1_gnn_beta_node,
        "w_edge": L1_gnn_W_edge, "b_edge": L1_gnn_b_edge, "g_edge": L1_gnn_g_edge, "beta_edge": L1_gnn_beta_edge,
        "w_msg": L1_gnn_W_msg, "b_msg": L1_gnn_b_msg, "g_msg": L1_gnn_g_msg, "beta_msg": L1_gnn_beta_msg,
    }
    arrays = {k: np.ascontiguousarray(a) for k, a in arrays.items()}
    nc = bacc.Bacc("TRN2", target_bir_lowering=False, num_devices=1)
    args = [nc.dram_tensor("in_" + k, a.shape, mybir.dt.from_np(a.dtype), kind="ExternalInput").ap() for k, a in arrays.items()]
    out = nc.dram_tensor("out", _OUT[0], mybir.dt.from_np(np.dtype(_OUT[1])), kind="ExternalOutput").ap()
    program(nc, *args, out)
    r = run(nc, [{"in_" + k: a for k, a in arrays.items()}], core_ids=[0])
    return r.results[0]["out"]
```

```python
import concourse.bass as bass
from concourse import mybir
from contextlib import ExitStack

F32 = mybir.dt.float32
I32 = mybir.dt.int32
ALU = mybir.AluOpType
ACT = mybir.ActivationFunctionType
AXX = mybir.AxisListType.X

P = 128
N = 50000
E = 50000
C = 96
ED = 4
EPS = 1e-5
W = 4
NODE_GROUPS = 98
NWIN = W * NODE_GROUPS
NPAD = NWIN * P
FULL_WIN = N // P
REST = N - FULL_WIN * P
T = 8
EDGE_GROUPS = 50
EPAD = EDGE_GROUPS * T * P
PAD_DST = NPAD
DUMP = NPAD + 1
TABLE_ROWS = NPAD + 1 + P
R = 15
ROW_GROUPS = FULL_WIN // R
CHUNK = E // (2 * EDGE_GROUPS)
NCHUNK = 2 * EDGE_GROUPS
SLOTS = 2
WP_E = 96
ROW = C + 2
HI, LO = 13, 32
A1 = C + 1
NACC = 2


class Shared:
    pass


def loop(engine, n, body):
    body(0)
    with engine.Fori(1, n - 1) as i:
        body(i)
    body(n - 1)


def wait(engine, sem, value):
    if not (isinstance(value, int) and value <= 0):
        engine.wait_ge(sem, value)


def is_last(i, n):
    return isinstance(i, int) and i == n - 1


def program(nc, x, src_g, dst_g, dst_row, dst_line, ea_t, ea_g, valid, w_node, b_node, g_node, beta_node, w_edge, b_edge,
            g_edge, beta_edge, w_msg, b_msg, g_msg, beta_msg, out):
    h1_tab = nc.dram_tensor("h1_tab", [N, C], F32, kind="Internal").ap()
    p_tab = nc.dram_tensor("p_tab", [NPAD, C], F32, kind="Internal").ap()
    q_tab = nc.dram_tensor("q_tab", [NPAD + 1, C], F32, kind="Internal").ap()
    sums = [nc.dram_tensor(f"sums{a}", [TABLE_ROWS, A1], F32, kind="Internal").ap() for a in range(NACC)]
    edge_rows = nc.dram_tensor("edge_rows", [EPAD, ROW], F32, kind="Internal").ap()
    src_p = nc.dram_tensor("src_p", [P, EDGE_GROUPS * T], I32, kind="Internal").ap()
    dst_q = nc.dram_tensor("dst_q", [P, EDGE_GROUPS * T], I32, kind="Internal").ap()
    msgs = [nc.dram_tensor(f"msgs{a}", [TABLE_ROWS, C], F32, kind="Internal").ap() for a in range(NACC)]

    whole = ExitStack()
    with whole:
        def keep(name, shape, dt=F32):
            return whole.enter_context(nc.sbuf_tensor(name, shape, dt))

        x1 = keep("x1", [P, NWIN * C])
        ident = keep("ident", [P, P])
        ones = keep("ones", [P, P])
        earlier = keep("earlier", [P, P])
        eps = keep("eps", [P, 1])
        dump_row = keep("dump_row", [P, 1])
        w_cat = keep("w_cat", [A1, 3 * C])
        w_ef = keep("w_ef", [C, C])
        w_e = keep("w_e", [ED, C])
        cols = keep("cols", [C, 16])
        be, ge, bte, gn, btn, gm, btm = (cols[:, k:k + 1] for k in range(7))
        small = keep("small", [C, 32])
        rows4 = keep("rows4", [P, 4 * C])
        kept = keep("kept", [P, NODE_GROUPS, 3 * W])
        grams = keep("grams", [C, 2, A1])


        starts = keep("starts", [1, 416], I32)
        flag = keep("flag", [1, 1], I32)
        line = keep("line", [P, P])
        v = Shared()
        v.edge_rows, v.src_p, v.dst_q, v.dst_line = edge_rows, src_p, dst_q, dst_line
        v.starts, v.flag, v.line, v.ea_g = starts, flag, line, ea_g
        v.x, v.src_g, v.dst_g, v.dst_row = x, src_g, dst_g, dst_row
        v.ea_t, v.valid, v.w_node, v.b_node = ea_t, valid, w_node, b_node
        v.g_node, v.beta_node, v.w_edge, v.b_edge = g_node, beta_node, w_edge, b_edge
        v.g_edge, v.beta_edge, v.w_msg, v.b_msg = g_edge, beta_edge, w_msg, b_msg
        v.g_msg, v.beta_msg, v.out, v.h1_tab = g_msg, beta_msg, out, h1_tab
        v.p_tab, v.q_tab, v.sums, v.msgs = p_tab, q_tab, sums, msgs
        v.x1, v.ident, v.ones, v.earlier = x1, ident, ones, earlier
        v.eps, v.dump_row, v.w_cat, v.w_ef = eps, dump_row, w_cat, w_ef
        v.w_e, v.be, v.ge, v.bte = w_e, be, ge, bte
        v.gn, v.btn, v.gm, v.btm = gn, btn, gm, btm
        v.small, v.rows4, v.kept, v.grams = small, rows4, kept, grams
        setup_phase(nc, v)
        plan_phase(nc, v)
        sorted_ok = nc.values_load(v.flag[0:1, 0:1], min_val=0, max_val=1)
        with nc.If(sorted_ok > 0):
            layers(nc, v, fast=True)
        with nc.Else():
            layers(nc, v, fast=False)


def layers(nc, v, fast):
    v.tag = "f" if fast else "s"
    if not fast:
        zero_phase(nc, v)
    edges, nodes = (gather_phase, sorted_node_phase) if fast else (scatter_phase, scattered_node_phase)
    edges(nc, v, second=False)
    nodes(nc, v, last=False)
    edges(nc, v, second=True)
    norm_rows_phase(nc, v)
    nodes(nc, v, last=True)


def setup_phase(nc, v):
    H = 2
    STEPS = ROW_GROUPS // H
    span = R * C
    main = FULL_WIN * P
    with ExitStack() as st:
        def sb(name, shape, dt=F32):
            return st.enter_context(nc.sbuf_tensor(name, shape, dt))

        def sem(name):
            return st.enter_context(nc.semaphore(name))

        xin = v.x1[:, 0:H * span].rearrange("p (u c) -> p u c", u=H)
        xout = v.x1[:, H * span:2 * H * span].rearrange("p (u c) -> p u c", u=H)
        pad_row = v.x1[0:1, 17000:17000 + C]
        bn = sb("bn", [P, H, R, 6])
        mom = sb("mom", [P, 8, R])
        ids, consts = sem("ids"), sem("consts")
        weights, weights2 = sem("weights"), sem("weights2")
        x_in = [sem(f"x_in{u}") for u in range(H)]
        h_out = [sem(f"h_out{u}") for u in range(H)]
        chain, var_ready, std_ready, xn_ready, h_ready = (sem(n) for n in ("chain", "var_ready", "std_ready", "xn_ready", "h_ready"))
        x_free = sem("x_free")
        pads = sem("pads")
        padded = sem("padded")
        rest_in, rest_out = sem("rest_in"), sem("rest_out")
        xv = v.x[0:main, :].rearrange("(p t) f -> p (t f)", p=P)
        hv = v.h1_tab[0:main, :].rearrange("(p t) f -> p (t f)", p=P)
        steps = STEPS

        with nc.Block() as block:
            @block.sync
            def _(sp):
                for dst, s in ((v.w_cat[0:C, 0:C], v.w_msg[0:C, :]), (v.w_cat[0:C, C:2 * C], v.w_msg[C:2 * C, :]),
                               (v.w_cat[0:C, 2 * C:], v.w_node[:, :]), (v.w_ef[:, :], v.w_msg[2 * C:3 * C, :]),
                               (v.w_e[:, :], v.w_edge[:, :]), (v.w_cat[C:A1, 2 * C:], v.b_node.rearrange("(a n) -> a n", a=1)),
                               (v.be, v.b_edge.rearrange("(n a) -> n a", a=1)), (v.ge, v.g_edge.rearrange("(n a) -> n a", a=1)),
                               (v.bte, v.beta_edge.rearrange("(n a) -> n a", a=1)), (v.gn, v.g_node.rearrange("(n a) -> n a", a=1)),
                               (v.btn, v.beta_node.rearrange("(n a) -> n a", a=1)), (v.gm, v.g_msg.rearrange("(n a) -> n a", a=1)),
                               (v.btm, v.beta_msg.rearrange("(n a) -> n a", a=1)),
                               (v.small[0:1, 31:32], v.valid[0:1, 0:1])):
                    sp.dma_start(dst, s).then_inc(weights, 16)

                def step(i):
                    for u in range(H):
                        g = H * i + u
                        wait(sp, x_free, g - H + 1)
                        sp.dma_start(xin[:, u, :], xv[:, bass.ds(g * span, span)]).then_inc(x_in[u], 16)
                loop(sp, steps, step)
                sp.wait_ge(x_free, ROW_GROUPS)
                sp.dma_start(xin[0:REST, 0, 0:C], v.x[main:N, :]).then_inc(rest_in, 16)

            @block.gpsimd
            def _(pool):
                pool.memset(v.ident[:, :], 0.0).then_inc(ids, 1)
                pool.memset(v.earlier[:, :], 1.0).then_inc(ids, 1)
                pool.memset(v.ones[:, :], 1.0).then_inc(ids, 1)
                pool.memset(v.eps[:, :], EPS).then_inc(ids, 1)
                pool.iota(v.dump_row[:, :], [[0, 1]], base=DUMP, channel_multiplier=1,
                          allow_small_or_imprecise_dtypes=True).then_inc(ids, 1)
                pool.iota(v.line[:, :], [[1, P]], base=0, channel_multiplier=0,
                          allow_small_or_imprecise_dtypes=True).then_inc(ids, 1)
                pool.wait_ge(ids, 6)
                pool.affine_select(out=v.ident[:, :], in_=v.ident[:, :], compare_op=ALU.not_equal, fill=1.0,
                                   base=0, pattern=[[-1, P]], channel_multiplier=1).then_inc(consts, 1)
                pool.affine_select(out=v.earlier[:, :], in_=v.earlier[:, :], compare_op=ALU.is_gt, fill=0.0,
                                   base=0, pattern=[[-1, P]], channel_multiplier=1).then_inc(consts, 1)
                pool.wait_ge(consts, 2)
                pool.wait_ge(pads, 2)
                pool.dma_start(v.q_tab[PAD_DST:PAD_DST + 1, :], pad_row).then_inc(padded, 16)
                pool.wait_ge(padded, 16)

            def norm(dve, rows, nrow, xi, xo, u, g, loaded, loads, stores):
                wait(dve, loaded, loads)
                for r in range(nrow):
                    last = dve.bn_stats(bn[0:rows, u, r, :], xi[0:rows, r * C:(r + 1) * C])
                last.then_inc(chain, 1)
                m = [mom[0:rows, k, 0:nrow] for k in range(8)]
                me, se, mo, so = (bn[0:rows, u, 0:nrow, k] for k in (1, 2, 4, 5))
                wait(dve, chain, 5 * g + 1)
                dve.tensor_tensor(m[0], me, mo, ALU.add)
                dve.tensor_tensor(m[1], me, mo, ALU.subtract)
                dve.tensor_tensor(m[2], se, so, ALU.add).then_inc(chain, 1)
                wait(dve, chain, 5 * g + 2)
                dve.scalar_tensor_tensor(m[3], m[1], 0.25, m[1], ALU.mult, ALU.mult).then_inc(chain, 1)
                wait(dve, chain, 5 * g + 3)
                dve.scalar_tensor_tensor(m[4], m[2], 1.0 / C, m[3], ALU.mult, ALU.add).then_inc(var_ready, 1)
                wait(dve, std_ready, g + 1)
                dve.reciprocal(m[6], m[5]).then_inc(chain, 1)
                wait(dve, chain, 5 * g + 4)
                dve.scalar_tensor_tensor(m[7], m[0], -0.5, m[6], ALU.mult, ALU.mult).then_inc(chain, 1)
                wait(dve, chain, 5 * g + 5)
                wait(dve, h_out[u], 16 * stores)
                for r in range(nrow):
                    last = dve.tensor_scalar(xo[0:rows, r * C:(r + 1) * C], xi[0:rows, r * C:(r + 1) * C],
                                             m[6][:, r:r + 1], m[7][:, r:r + 1], ALU.mult, ALU.add)
                last.then_inc(x_free, 1)

            @block.vector
            def _(dve):
                dve.memset(v.w_cat[C:A1, 0:C], 0.0).then_inc(pads, 1)
                dve.memset(pad_row, -1e30).then_inc(pads, 1)

                def step(i):
                    for u in range(H):
                        norm(dve, P, R, xin[:, u, :], xout[:, u, :], u, H * i + u, x_in[u], 16 * (i + 1), i)
                loop(dve, steps, step)
                norm(dve, REST, 1, xin[:, 0, :], xout[:, 0, :], 0, ROW_GROUPS, rest_in, 16, STEPS)

            @block.scalar
            def _(act):
                act.dma_start(v.rows4[0:1, C:2 * C], v.b_msg.rearrange("(a n) -> a n", a=1)).then_inc(weights2, 16)
                act.wait_ge(weights, 16 * 14)
                act.wait_ge(weights2, 16)
                act.wait_ge(ids, 6)

                def root(rows, nrow, g):
                    wait(act, var_ready, g + 1)
                    act.activation(mom[0:rows, 5, 0:nrow], mom[0:rows, 4, 0:nrow], ACT.Sqrt,
                                   bias=v.eps[0:rows, :]).then_inc(std_ready, 1)

                def step(i):
                    for u in range(H):
                        g = H * i + u
                        root(P, R, g)
                        wait(act, x_free, g + 1)
                        act.activation(xout[:, u, :], xout[:, u, :], ACT.Relu).then_inc(h_ready, 1)
                        wait(act, h_ready, g + 1)
                        act.dma_start(hv[:, bass.ds(g * span, span)], xout[:, u, :]).then_inc(h_out[u], 16)
                loop(act, steps, step)
                root(REST, 1, ROW_GROUPS)
                act.wait_ge(x_free, ROW_GROUPS + 1)
                act.activation(xout[0:REST, 0, 0:C], xout[0:REST, 0, 0:C], ACT.Relu).then_inc(h_ready, 1)
                act.wait_ge(h_ready, ROW_GROUPS + 1)
                act.dma_start(v.h1_tab[main:N, :], xout[0:REST, 0, 0:C]).then_inc(rest_out, 16)
                for u in range(H):
                    act.wait_ge(h_out[u], 16 * steps)
                act.wait_ge(rest_out, 16)


def zero_phase(nc, v):
    BR = 32
    rows = TABLE_ROWS // P
    zero = v.x1[:, 0:BR * A1]
    with nc.semaphore("blank") as blank, nc.semaphore("zeroed") as zeroed:
        with nc.Block() as block:
            @block.vector
            def _(dve):
                dve.memset(zero, 0.0).then_inc(blank, 1)

            @block.sync
            def _(sp):
                sp.wait_ge(blank, 1)
                n = 0
                for tab, wdt in [(s, A1) for s in v.sums] + [(m, C) for m in v.msgs]:
                    for r0 in range(0, rows, BR):
                        r1 = min(r0 + BR, rows)
                        sp.dma_start(tab[r0 * P:r1 * P, :].rearrange("(p r) f -> p (r f)", p=P),
                                     zero[:, 0:(r1 - r0) * wdt]).then_inc(zeroed, 16)
                        n += 1
                    sp.dma_start(tab[rows * P:TABLE_ROWS, :], zero[0:TABLE_ROWS - rows * P, 0:wdt]).then_inc(zeroed, 16)
                    n += 1
                sp.wait_ge(zeroed, 16 * n)


def plan_phase(nc, v):
    NT = EDGE_GROUPS * T
    with ExitStack() as st:
        def sem(name):
            return st.enter_context(nc.semaphore(name + "p"))

        def part(dt, lo, n, rows=P):
            t = v.x1[0:rows, lo:lo + n]
            return t if dt == F32 else t.bitcast(dt)

        dg, sg, da, db = (part(I32, k * NT, NT) for k in range(4))
        hi, lo, t0, t1, t2, t3 = (part(I32, (4 + k) * NT, NT) for k in range(6))
        hif, lof, up = (part(F32, (10 + k) * NT, NT) for k in range(3))
        BF = mybir.dt.bfloat16
        oh_hi = part(BF, 14 * NT, NT * HI // 2)
        oh_lo = part(BF, 14 * NT + NT * HI // 2, NT * LO // 2)
        base = 14 * NT + NT * (HI + LO) // 2
        cross = part(F32, base, T * LO)
        blocks = part(F32, base + T * LO, T * HI * LO, 1)
        o = base + T * LO + T * HI * LO
        cnt, incl, one, sc = part(F32, o, 416, 1), part(F32, o + 416, 416, 1), part(F32, o + 832, 416, 1), part(F32, o + 1248, 8, 1)
        ups = part(F32, o + 1256, 1)
        ps = st.enter_context(nc.psum_tensor("ps_plan", [P, 512], F32))
        ps1 = st.enter_context(nc.psum_tensor("ps_plan1", [P, 512], F32))
        loaded, chain, hot, crossed, moved, summed, stored = (sem(n) for n in ("loaded", "chain", "hot", "crossed", "moved", "summed", "stored"))
        with nc.Block() as block:
            @block.sync
            def _(sp):
                sp.dma_start(dg, v.dst_g).then_inc(loaded, 16)
                sp.dma_start(sg, v.src_g).then_inc(loaded, 16)
                sp.dma_start(da, v.dst_line[:, 0:EPAD].rearrange("a (p c) -> (a p) c", p=P)).then_inc(loaded, 16)
                sp.dma_start(db, v.dst_line[:, 1:EPAD + 1].rearrange("a (p c) -> (a p) c", p=P)).then_inc(loaded, 16)
                sp.wait_ge(crossed, 1)
                for k in range(T):
                    sp.dma_start(blocks[:, k * HI * LO:(k + 1) * HI * LO],
                                 cross[k * HI:(k + 1) * HI, k * LO:(k + 1) * LO]).then_inc(moved, 16)
                sp.wait_ge(stored, 32)

            @block.scalar
            def _(act):
                act.wait_ge(chain, 12)
                act.dma_start(v.src_p, t0).then_inc(stored, 16)
                act.dma_start(v.dst_q, t3).then_inc(stored, 16)
                act.wait_ge(stored, 32)

            @block.vector
            def _(dve):
                n = [0]

                def link(ins):
                    n[0] += 1
                    ins.then_inc(chain, 1)
                    dve.wait_ge(chain, n[0])

                dve.wait_ge(loaded, 64)
                shr, shl, band = ALU.arith_shift_right, ALU.logical_shift_left, ALU.bitwise_and
                dve.tensor_scalar(hi, dg, 12, None, shr)
                link(dve.tensor_scalar(lo, dg, 7, LO - 1, shr, band))
                dve.tensor_copy(hif, hi)
                link(dve.tensor_copy(lof, lo))
                dve.tensor_tensor(oh_hi.rearrange("p (t a) -> p t a", a=HI), hif.unsqueeze(2).to_broadcast([P, NT, HI]),
                                  v.line[:, 0:HI].unsqueeze(1).to_broadcast([P, NT, HI]), ALU.is_equal)
                dve.tensor_tensor(oh_lo.rearrange("p (t a) -> p t a", a=LO), lof.unsqueeze(2).to_broadcast([P, NT, LO]),
                                  v.line[:, 0:LO].unsqueeze(1).to_broadcast([P, NT, LO]), ALU.is_equal).then_inc(hot, 1)
                dve.wait_ge(hot, 1)
                dve.tensor_copy(hif, da)
                link(dve.tensor_copy(lof, db))
                link(dve.tensor_tensor(up, hif, lof, ALU.is_gt))
                dve.tensor_reduce(ups, up, AXX, ALU.add).then_inc(hot, 1)
                for a, out_ in ((sg, t0), (dg, t3)):
                    dve.tensor_scalar(t1, a, P - 1, 2, band, shl)
                    link(dve.tensor_scalar(t2, a, 7, W - 1, shr, band))
                    link(dve.tensor_tensor(t1, t1, t2, ALU.add))
                    link(dve.tensor_scalar(t2, a, 9, 9, shr, shl))
                    link(dve.tensor_tensor(out_, t1, t2, ALU.add))
                assert n[0] == 12
                link(dve.memset(one, 1.0))
                dve.wait_ge(summed, 1)
                link(dve.tensor_copy(cross[0:T * HI, :], ps[0:T * HI, 0:T * LO]))
                dve.sem_inc(crossed, 1)
                dve.wait_ge(moved, 16 * T)
                link(dve.tensor_reduce(cnt, blocks.rearrange("o (k c) -> o c k", k=T), AXX, ALU.add))
                link(dve.tensor_tensor_scan(incl, one, cnt, 0.0, ALU.mult, ALU.add))
                dve.memset(v.starts[:, 0:1], 0)
                dve.tensor_copy(v.starts[:, 1:NWIN + 1], incl[:, 0:NWIN])
                link(dve.tensor_reduce(sc[:, 0:1], cnt[:, 0:NWIN], AXX, ALU.max))
                dve.wait_ge(summed, 2)
                dve.tensor_scalar(sc[:, 1:2], sc[:, 0:1], float(SLOTS * WP_E), None, ALU.is_le)
                link(dve.tensor_scalar(sc[:, 2:3], ps1[0:1, 0:1], 0.0, None, ALU.is_equal))
                link(dve.tensor_tensor(v.flag[:, :], sc[:, 1:2], sc[:, 2:3], ALU.mult))

            @block.tensor
            def _(pe):
                pe.wait_ge(hot, 1)

                def step(i):
                    m = pe.matmul(ps[0:T * HI, 0:T * LO], oh_hi[:, bass.ds(i * T * HI, T * HI)],
                                  oh_lo[:, bass.ds(i * T * LO, T * LO)], start=isinstance(i, int) and i == 0,
                                  stop=is_last(i, EDGE_GROUPS), skip_group_check=True)
                    if is_last(i, EDGE_GROUPS):
                        m.then_inc(summed, 1)
                loop(pe, EDGE_GROUPS, step)
                pe.wait_ge(hot, 2)
                pe.matmul(ps1[0:1, 0:1], ups, v.ones[:, 0:1], start=True, stop=True).then_inc(summed, 1)


class EdgeStats:

    def __init__(self, nc, v, st, at):
        def sem(name):
            return st.enter_context(nc.semaphore(name + "e" + v.tag))
        self.v = v
        self.attr = v.x1[0:ED, at:at + 4 * CHUNK].rearrange("p (u k c) -> p u k c", u=2, k=2)
        self.feat = v.x1[0:C, at + 4 * CHUNK:at + 6 * CHUNK].rearrange("p (k c) -> p k c", k=2)
        self.stats = v.x1[0:C, at + 6 * CHUNK:at + 6 * CHUNK + 6 * NCHUNK].rearrange("p (n s) -> p n s", s=6)
        self.ps = [st.enter_context(nc.psum_tensor(f"ps_e{k}{v.tag}", [P, 512], F32)) for k in range(2)]
        self.ps_row = st.enter_context(nc.psum_tensor("ps_row" + v.tag, [P, 512], F32))
        self.attr_in = [sem(f"attr_in{u}") for u in range(2)]
        self.mm, self.relu, self.stat, self.fold, self.std, self.c_sum, self.c_row, self.moved = (
            sem(n) for n in ("mm", "relu", "stat", "fold", "std", "c_sum", "c_row", "moved"))

    def load(self, sp, i, u):
        g = 2 * i + u
        wait(sp, self.mm, 2 * (g - 1))
        sp.dma_start(self.attr[:, u, :, :].rearrange("p k c -> p (k c)"), self.v.ea_t[:, bass.ds(g * 2 * CHUNK, 2 * CHUNK)]
                     ).then_inc(self.attr_in[u], 16)

    def multiply(self, pe, i, u):
        g = 2 * i + u
        wait(pe, self.attr_in[u], 16 * (i + 1))
        for k in range(2):
            wait(pe, self.relu, 2 * (g - 1) + k + 1)
            pe.matmul(self.ps[k][0:C, 0:CHUNK], self.v.w_e[:, :], self.attr[:, u, k, :], start=True, stop=True).then_inc(self.mm, 1)

    def relus(self, act, i, u):
        g = 2 * i + u
        for k in range(2):
            wait(act, self.mm, 2 * g + k + 1)
            wait(act, self.stat, 2 * (g - 1) + k + 1)
            act.activation(self.feat[:, k, :], self.ps[k][0:C, 0:CHUNK], ACT.Relu, bias=self.v.be).then_inc(self.relu, 1)

    def take(self, dve, i, u):
        g = 2 * i + u
        for k in range(2):
            wait(dve, self.relu, 2 * g + k + 1)
            dve.bn_stats(self.stats[:, bass.ds(2 * g + k, 1), :].rearrange("p a s -> p (a s)"), self.feat[:, k, :]).then_inc(self.stat, 1)

    def finish_dve(self, dve):
        v, s = self.v, self.v.small
        dve.wait_ge(self.stat, NCHUNK)
        dve.bn_aggr(s[:, 0:2], self.stats[:, :, :].rearrange("p n s -> p (n s)")).then_inc(self.fold, 1)
        dve.wait_ge(self.std, 1)
        dve.reciprocal(s[:, 3:4], s[:, 2:3]).then_inc(self.fold, 1)
        dve.wait_ge(self.fold, 2)
        dve.tensor_tensor(s[:, 4:5], s[:, 3:4], v.ge, ALU.mult).then_inc(self.fold, 1)
        dve.wait_ge(self.fold, 3)
        dve.tensor_tensor(s[:, 5:6], s[:, 4:5], s[:, 0:1], ALU.mult).then_inc(self.fold, 1)
        dve.wait_ge(self.fold, 4)
        dve.tensor_tensor(s[:, 6:7], v.bte, s[:, 5:6], ALU.subtract).then_inc(self.fold, 1)
        dve.wait_ge(self.c_sum, 1)
        dve.tensor_scalar(v.w_ef[:, :], v.w_ef[:, :], s[:, 4:5], None, ALU.mult).then_inc(self.fold, 1)
        dve.tensor_tensor(v.rows4[0:1, 0:C], self.ps_row[0:1, 0:C], v.rows4[0:1, C:2 * C], ALU.add).then_inc(self.c_row, 1)

    def finish_act(self, act):
        act.wait_ge(self.fold, 1)
        act.activation(self.v.small[:, 2:3], self.v.small[:, 1:2], ACT.Sqrt, bias=self.v.eps[0:C, :]).then_inc(self.std, 1)

    def finish_pe(self, pe):
        pe.wait_ge(self.fold, 5)
        pe.matmul(self.ps_row[0:1, 0:C], self.v.small[:, 6:7], self.v.w_ef[:, :], start=True, stop=True).then_inc(self.c_sum, 1)

    def finish_sp(self, sp):
        sp.wait_ge(self.c_row, 1)
        sp.dma_start(self.v.w_cat[C:A1, C:2 * C], self.v.rows4[0:1, 0:C]).then_inc(self.moved, 16)
        sp.wait_ge(self.moved, 16)


class Messages:

    def __init__(self, nc, v, st, got, gotq, msg, gathered, msg_free):
        def sb(name, shape):
            return st.enter_context(nc.sbuf_tensor(name + "m" + v.tag, shape, F32))

        def sem(name):
            return st.enter_context(nc.semaphore(name + "m" + v.tag))

        def bank(name, n=1):
            return st.enter_context(nc.psum_tensor(name + "m" + v.tag, [P, n * 512], F32))
        self.v, self.got, self.gotq, self.msg, self.gathered = v, got, gotq, msg, gathered
        self.msg_free = msg_free
        self.HB = T // 4
        self.ea, self.ef = sb("ea", [ED, T * P]), sb("ef", [C, T * P])
        self.ps_ef, self.ps_msg, self.ps_gram = bank("ps_ef", self.HB), bank("ps_msg", self.HB), bank("ps_gram")
        self.ea_in, self.ef_mm, self.ef_relu, self.msg_mm, self.with_p, self.with_q, self.ready, self.gram_done, self.ones, self.out = (
            sem(n) for n in ("ea_in", "ef_mm", "ef_relu", "msg_mm", "with_p", "with_q", "ready", "gram_done", "ones", "out"))

    def load(self, sp, g):
        wait(sp, self.ef_mm, self.HB * g)
        sp.dma_start(self.ea[:, :], self.v.ea_g[:, bass.ds(g * T * P, T * P)]).then_inc(self.ea_in, 16)

    def edge_part(self, pe, g):
        HB = self.HB
        wait(pe, self.ea_in, 16 * (g + 1))
        for h in range(HB):
            wait(pe, self.ef_relu, HB * (g - 1) + h + 1)
            pe.matmul(self.ps_ef[0:C, h * 512:h * 512 + 512], self.v.w_e[:, :], self.ea[:, h * 512:h * 512 + 512],
                      start=True, stop=True).then_inc(self.ef_mm, 1)
        for k in range(T):
            h = k // 4
            if k % 4 == 0:
                wait(pe, self.ef_relu, HB * g + h + 1)
                wait(pe, self.with_p, HB * (g - 1) + h + 1)
            c0 = h * 512 + (k % 4) * C
            m = pe.matmul(self.ps_msg[:, c0:c0 + C], self.ef[:, k * P:(k + 1) * P], self.v.w_ef[:, :], start=True, stop=True)
            if k % 4 == 3:
                m.then_inc(self.msg_mm, 1)

    def gram(self, pe, i, u, k):
        first = isinstance(i, int) and i == 0 and u == 0 and k == 0
        end = is_last(i, EDGE_GROUPS // 2) and u == 1 and k == T - 1
        m = pe.matmul(self.ps_gram[0:C, 0:A1], self.msg(u, k, 0, C), self.msg(u, k, 0, A1), start=first, stop=end,
                      skip_group_check=True)
        if k == T - 1:
            m.then_inc(self.gram_done, 1)

    def edge_relu(self, act, g):
        HB = self.HB
        for h in range(HB):
            wait(act, self.ef_mm, HB * g + h + 1)
            wait(act, self.msg_mm, HB * (g - 1) + h + 1)
            act.activation(self.ef[:, h * 512:h * 512 + 512], self.ps_ef[0:C, h * 512:h * 512 + 512], ACT.Relu,
                           bias=self.v.be).then_inc(self.ef_relu, 1)

    def add_parts(self, dve, i, u):
        g, HB = 2 * i + u, self.HB
        wait(dve, self.gathered[u], 32 * T * (i + 1))
        for h in range(HB):
            ks = slice(4 * h, 4 * h + 4)
            wait(dve, self.msg_mm, HB * g + h + 1)
            dve.tensor_tensor(self.got[:, u, ks, 0:C], self.got[:, u, ks, 0:C],
                              self.ps_msg[:, h * 512:h * 512 + 4 * C].rearrange("p (k c) -> p k c", k=4), ALU.add).then_inc(self.with_p, 1)
            wait(dve, self.with_p, HB * g + h + 1)
            dve.tensor_tensor(self.got[:, u, ks, 0:C], self.got[:, u, ks, 0:C], self.gotq[:, u, ks, :], ALU.add).then_inc(self.with_q, 1)

    def message_relu(self, act, g, u):
        for h in range(self.HB):
            wait(act, self.with_q, self.HB * g + h + 1)
            self.msg_free(act, g)
            act.activation(self.msg(u, slice(4 * h, 4 * h + 4), 0, C), self.got[:, u, 4 * h:4 * h + 4, 0:C],
                           ACT.Relu).then_inc(self.ready, 1)

    def finish_dve(self, dve):
        dve.wait_ge(self.gram_done, EDGE_GROUPS)
        dve.tensor_copy(self.v.grams[:, 1, :], self.ps_gram[0:C, 0:A1]).then_inc(self.out, 1)
        dve.wait_ge(self.out, 1)


def gather_phase(nc, v, second):
    H = 2
    STEPS = EDGE_GROUPS // H
    tag = "g2" if second else "g1"
    with ExitStack() as st:
        def sb(name, shape, dt=F32):
            return st.enter_context(nc.sbuf_tensor(name + tag, shape, dt))

        def sem(name):
            return st.enter_context(nc.semaphore(name + tag))

        idx = [sb("src", [P, H, T], I32), sb("row", [P, H, T], I32)]
        dst = sb("dst", [P, H, T], I32)
        got = sb("got", [P, H, T, C if second else ROW])
        gotq = sb("gotq", [P, H, T, C]) if second else None
        rows = sb("rows", [P, H, T, ROW]) if second else got
        idx_in = [sem(f"idx_in{u}") for u in range(H)]
        gathered = [sem(f"gathered{u}") for u in range(H)]
        stored = [sem(f"stored{u}") for u in range(H)]
        dst_set, turn, sp_turn, ready = sem("dst_set"), sem("turn"), sem("sp_turn"), sem("ready")
        tables = [v.p_tab, v.q_tab] if second else [v.h1_tab]
        indices = [v.src_p, v.dst_q] if second else [v.src_g]
        NI = len(tables)

        def msg(u, k, c0, c1):
            return rows[:, u, k, c0:c1]

        if second:
            m = Messages(nc, v, st, got, gotq, msg, gathered, lambda act, g: wait(act, m.gram_done, g - 1))
        else:
            es = EdgeStats(nc, v, st, 0)

        with nc.Block() as block:
            @block.sync
            def _(sp):
                def loads(i, u):
                    g = H * i + u
                    wait(sp, gathered[u], 16 * NI * T * i)
                    for ix, src in zip(idx, indices):
                        sp.dma_start(ix[:, u, :], src[:, bass.ds(g * T, T)]).then_inc(idx_in[u], 16)
                    wait(sp, dst_set, g - 1)
                    sp.dma_start(dst[:, u, :], v.dst_g[:, bass.ds(g * T, T)]).then_inc(idx_in[u], 16)
                    if second:
                        m.load(sp, g)
                    else:
                        es.load(sp, i, u)

                def store(i, u):
                    g = H * i + u
                    wait(sp, dst_set, g + 1)
                    sp.sem_inc(sp_turn, 1)
                    if second:
                        wait(sp, m.ready, m.HB * (g + 1))
                    else:
                        wait(sp, gathered[u], 16 * T * (i + 1))
                    sp.dma_start(v.edge_rows[bass.ds(g * T * P, T * P), :].rearrange("(p k) c -> p (k c)", p=P),
                                 rows[:, u, :, :].rearrange("p k c -> p (k c)")).then_inc(stored[u], 16)
                loads(0, 0)

                def step(i):
                    loads(i, 1)
                    store(i, 0)
                    if not is_last(i, STEPS):
                        loads(i + 1, 0)
                    store(i, 1)
                loop(sp, STEPS, step)
                if not second:
                    es.finish_sp(sp)
                for u in range(H):
                    sp.wait_ge(stored[u], 16 * STEPS)

            @block.gpsimd
            def _(pool):
                def step(i):
                    for u in range(H):
                        wait(pool, idx_in[u], 16 * (NI + 1) * (i + 1))
                        if second:
                            wait(pool, m.ready, m.HB * (2 * i + u - 1))
                        else:
                            wait(pool, stored[u], 16 * i)
                        pool.sem_inc(turn, 1)
                        for k in range(T):
                            for t, (table, ix) in enumerate(zip(tables, idx)):
                                pool.indirect_dma_start((gotq if t else got)[:, u, k, 0:C], None, table[:, :],
                                                        bass.IndirectOffsetOnAxis(ap=ix[:, u, k:k + 1], axis=0)
                                                        ).then_inc(gathered[u], 16)
                loop(pool, STEPS, step)

            @block.vector
            def _(dve):
                for u in range(H):
                    dve.memset(rows[:, u, :, C:A1], 1.0).then_inc(ready, 1)

                def step(i):
                    for u in range(H):
                        wait(dve, idx_in[u], 16 * (NI + 1) * (i + 1))
                        wait(dve, stored[u], 16 * i)
                        dve.tensor_copy(rows[:, u, :, A1], dst[:, u, :]).then_inc(dst_set, 1)
                        if second:
                            m.add_parts(dve, i, u)
                        else:
                            es.take(dve, i, u)
                loop(dve, STEPS, step)
                (m if second else es).finish_dve(dve)

            @block.tensor
            def _(pe):
                pe.wait_ge(ready, H)

                def step(i):
                    for u in range(H):
                        g = 2 * i + u
                        if second:
                            m.edge_part(pe, g)
                            for k in range(T):
                                if k % 4 == 0:
                                    wait(pe, m.ready, m.HB * g + k // 4 + 1)
                                m.gram(pe, i, u, k)
                        else:
                            es.multiply(pe, i, u)
                loop(pe, STEPS, step)
                if not second:
                    es.finish_pe(pe)

            @block.scalar
            def _(act):
                act.wait_ge(ready, H)

                def step(i):
                    for u in range(H):
                        if second:
                            m.edge_relu(act, 2 * i + u)
                            wait(act, stored[u], 16 * i)
                            m.message_relu(act, 2 * i + u, u)
                        else:
                            es.relus(act, i, u)
                loop(act, STEPS, step)
                if not second:
                    es.finish_act(act)


def scatter_phase(nc, v, second):
    H = 2
    STEPS = EDGE_GROUPS // H
    width = C if second else A1
    tables = v.msgs if second else v.sums
    tag = "b" if second else "a"
    HB = T // 4
    with ExitStack() as st:
        def sb(name, shape, dt=F32):
            return st.enter_context(nc.sbuf_tensor(name + tag, shape, dt))

        def sem(name):
            return st.enter_context(nc.semaphore(name + tag))

        def bank(name, n=1):
            return st.enter_context(nc.psum_tensor(name + tag, [P, n * 512], F32))

        src, dst, rows = (sb(n, [P, H, T], I32) for n in ("src", "dst", "rows"))
        dst_rows_q = sb("dst_rows_q", [P, H, T], I32) if second else None
        dstf, cnt, away = (sb(n, [P, H, T]) for n in ("dstf", "cnt", "away"))
        scrap = sb("scrap", [P, P])
        if second:
            dst_rows = sb("dst_rows", [P, 1, T * P], I32)
            same = sb("same", [P, 1, T, P])
            got = sb("got", [P, H, T, C])
            gotq = sb("gotq", [P, H, T, C])
            msg = sb("msg", [P, 1, T, A1])
            tot = sb("tot", [P, H, T, C])
            BH = 1
        else:
            dst_rows = sb("dst_rows", [P, H, T * P], I32)
            free = v.x1[:, :]
            o = H * T * P
            same = free[:, 0:o].rearrange("p (u k c) -> p u k c", u=H, k=T)
            got = free[:, o:o + H * T * A1].rearrange("p (u k c) -> p u k c", u=H, k=T)
            tot = free[:, 2 * o:2 * o + H * T * A1].rearrange("p (u k c) -> p u k c", u=H, k=T)
            BH = H
        ps_tot = bank("ps_tot", HB)
        idx_in = [sem(f"idx_in{u}") for u in range(H)]
        marks_in = [sem(f"marks_in{u}") for u in range(H)]
        gathered = [sem(f"gathered{u}") for u in range(H)]
        added = [sem(f"added{a}") for a in range(NACC)]
        floats, marked, differ, masked, rows_ready = (sem(n) for n in ("floats", "marked", "differ", "masked", "rows_ready"))
        totals, copied, turn, ready = (sem(n) for n in ("totals", "copied", "turn", "ready"))
        if second:
            m = Messages(nc, v, st, got, gotq, lambda u, k, c0, c1: msg[:, 0, k, c0:c1], gathered,
                         lambda act, g: wait(act, m.gram_done, g))
        else:
            es = EdgeStats(nc, v, st, 3 * H * T * P)

        def bu(u):
            return u % BH

        with nc.Block() as block:
            @block.sync
            def _(sp):
                def step(i):
                    for u in range(H):
                        g = H * i + u
                        wait(sp, gathered[u], (32 if second else 16) * T * i)
                        wait(sp, rows_ready, g - 1)
                        sp.dma_start(src[:, u, :], (v.src_p if second else v.src_g)[:, bass.ds(g * T, T)]).then_inc(idx_in[u], 16)
                        if second:
                            sp.dma_start(dst_rows_q[:, u, :], v.dst_q[:, bass.ds(g * T, T)]).then_inc(idx_in[u], 16)
                        sp.dma_start(dst[:, u, :], v.dst_g[:, bass.ds(g * T, T)]).then_inc(idx_in[u], 16)
                        wait(sp, marked, g - BH + 1)
                        sp.dma_start(dst_rows[:, bu(u), :], v.dst_row[:, bass.ds(g * T * P, T * P)]
                                     .to_broadcast([P, T * P])).then_inc(marks_in[u], 16)
                        if second:
                            m.load(sp, g)
                        else:
                            es.load(sp, i, u)
                loop(sp, STEPS, step)
                if not second:
                    es.finish_sp(sp)

            @block.gpsimd
            def _(pool):
                def gather(i, u):
                    g = H * i + u
                    wait(pool, idx_in[u], (48 if second else 32) * (i + 1))
                    wait(pool, m.ready if second else totals, (g - 1) * HB)
                    pool.sem_inc(turn, 1)
                    for k in range(T):
                        pool.indirect_dma_start(got[:, u, k, 0:C], None, (v.p_tab if second else v.h1_tab)[:, :],
                                                bass.IndirectOffsetOnAxis(ap=src[:, u, k:k + 1], axis=0)
                                                ).then_inc(gathered[u], 16)
                        if second:
                            pool.indirect_dma_start(gotq[:, u, k, :], None, v.q_tab[:, :],
                                                    bass.IndirectOffsetOnAxis(ap=dst_rows_q[:, u, k:k + 1], axis=0)
                                                    ).then_inc(gathered[u], 16)

                def scatter(i, u):
                    g = H * i + u
                    wait(pool, rows_ready, g + 1)
                    for k in range(T):
                        if k % 4 == 0:
                            wait(pool, copied, HB * g + k // 4 + 1)
                        wait(pool, added[k % NACC], g * (16 * T // NACC) + 16 * (k // NACC))
                        pool.sem_inc(turn, 1)
                        pool.indirect_dma_start(tables[k % NACC][:, :],
                                                bass.IndirectOffsetOnAxis(ap=rows[:, u, k:k + 1], axis=0),
                                                tot[:, u, k, :], None, compute_op=ALU.add).then_inc(added[k % NACC], 16)
                gather(0, 0)

                def step(i):
                    gather(i, 1)
                    scatter(i, 0)
                    if not is_last(i, STEPS):
                        gather(i + 1, 0)
                    scatter(i, 1)
                loop(pool, STEPS, step)
                for a in range(NACC):
                    pool.wait_ge(added[a], 16 * EDGE_GROUPS * T // NACC)

            @block.vector
            def _(dve):
                if second:
                    dve.memset(msg[:, 0, :, C:A1], 1.0).then_inc(ready, 1)
                else:
                    for u in range(H):
                        dve.memset(got[:, u, :, C:A1], 1.0).then_inc(ready, 1)

                def step(i):
                    for u in range(H):
                        g = H * i + u
                        wait(dve, idx_in[u], (48 if second else 32) * (i + 1))
                        dve.tensor_copy(dstf[:, u, :], dst[:, u, :]).then_inc(floats, 1)
                        wait(dve, floats, g + 1)
                        wait(dve, marks_in[u], 16 * (i + 1))
                        wait(dve, totals, HB * (g - BH + 1))
                        if second:
                            wait(dve, m.gram_done, g)
                        for k in range(T):
                            line = dst_rows[:, bu(u), k * P:(k + 1) * P]
                            dve.tensor_scalar(same[:, bu(u), k, :], line, dstf[:, u, k:k + 1], None, ALU.is_equal)
                            dve.scalar_tensor_tensor(scrap[:, :], line, dstf[:, u, k:k + 1], v.earlier[:, :],
                                                     ALU.is_equal, ALU.mult, accum_out=cnt[:, u, k:k + 1])
                            last = dve.drain()
                        last.then_inc(marked, 1)
                        wait(dve, marked, g + 1)
                        dve.tensor_scalar(cnt[:, u, :], cnt[:, u, :], 1.0, None, ALU.min)
                        dve.tensor_scalar(away[:, u, :], dstf[:, u, :], -1.0, v.dump_row[:, :], ALU.mult, ALU.add).then_inc(differ, 1)
                        wait(dve, differ, g + 1)
                        dve.tensor_tensor(away[:, u, :], away[:, u, :], cnt[:, u, :], ALU.mult).then_inc(masked, 1)
                        wait(dve, masked, g + 1)
                        for a in range(NACC):
                            wait(dve, added[a], (g - 1) * (16 * T // NACC))
                        dve.tensor_tensor(rows[:, u, :], away[:, u, :], dstf[:, u, :], ALU.add).then_inc(rows_ready, 1)
                        if second:
                            m.add_parts(dve, i, u)
                        else:
                            es.take(dve, i, u)
                        for h in range(HB):
                            wait(dve, totals, HB * g + h + 1)
                            dve.tensor_copy(tot[:, u, 4 * h:4 * h + 4, :],
                                            ps_tot[:, h * 512:h * 512 + 4 * width].rearrange("p (k c) -> p k c", k=4)
                                            ).then_inc(copied, 1)
                loop(dve, STEPS, step)
                (m if second else es).finish_dve(dve)

            @block.tensor
            def _(pe):
                pe.wait_ge(ready, 1 if second else H)

                def step(i):
                    for u in range(H):
                        g = H * i + u
                        if second:
                            m.edge_part(pe, g)
                        else:
                            es.multiply(pe, i, u)
                        wait(pe, marked, g + 1)
                        if not second:
                            wait(pe, gathered[u], 16 * T * (i + 1))
                        for k in range(T):
                            h = k // 4
                            if k % 4 == 0:
                                wait(pe, copied, HB * (g - 1) + h + 1)
                                if second:
                                    wait(pe, m.ready, HB * g + h + 1)
                            c0 = h * 512 + (k % 4) * width
                            t = pe.matmul(ps_tot[:, c0:c0 + width], same[:, bu(u), k, :],
                                          msg[:, 0, k, 0:C] if second else got[:, u, k, :], start=True, stop=True)
                            if k % 4 == 3:
                                t.then_inc(totals, 1)
                        if second:
                            for k in range(T):
                                m.gram(pe, i, u, k)
                loop(pe, STEPS, step)
                if not second:
                    es.finish_pe(pe)

            @block.scalar
            def _(act):
                if second:
                    act.wait_ge(ready, 1)

                def step(i):
                    for u in range(H):
                        if second:
                            m.edge_relu(act, H * i + u)
                            m.message_relu(act, H * i + u, u)
                        else:
                            es.relus(act, i, u)
                loop(act, STEPS, step)
                if not second:
                    es.finish_act(act)


def scattered_node_phase(nc, v, last):
    H = 2
    STEPS = NODE_GROUPS // H
    width = C if last else A1
    tables = v.msgs if last else v.sums
    tag = "d" if last else "c"
    WP = W * P
    with ExitStack() as st:
        def sb(name, shape, dt=F32):
            return st.enter_context(nc.sbuf_tensor(name + tag, shape, dt))

        def sem(name):
            return st.enter_context(nc.semaphore(name + tag))

        def bank(name, n=1):
            return st.enter_context(nc.psum_tensor(name + tag, [P, n * 512], F32))

        xs = sb("xs", [P, H, W, C])
        sa, sb_ = sb("sa", [P, H, W, width]), sb("sb", [P, H, W, width])
        xn = sb("xn", [P, H, W, C])
        ht = sb("ht", [A1, H, WP])
        ps_t, ps_o = bank("ps_t", H), bank("ps_o", H if last else W)
        mine = sb("mine", [P, H, 3 * W])
        y = sb("y", [P, H, W, C if last else A1])
        if last:
            fin = sb("fin", [P, H, W, C])
        else:
            pq = sb("pq", [P, H, W, 2 * C])
            bn, mom = sb("bn", [P, H, W, 6]), sb("mom", [P, H, 8, W])
            ps_gram = bank("ps_gram")
        names = ("chain", "xn_ready", "t_mm", "ht_ready", "o_mm", "y_ready", "gram_done", "kept_it", "turn",
                 "var_ready", "std_ready", "x1_ready", "scaled", "y_scaled", "fin_ready", "pq_ready", "took", "ready", "pool_chain")
        (chain, xn_ready, t_mm, ht_ready, o_mm, y_ready, gram_done, kept_it, turn, var_ready, std_ready, x1_ready,
         scaled, y_scaled, fin_ready, pq_ready, took, ready, pool_chain) = (sem(n) for n in names)
        loaded = [sem(f"loaded{u}") for u in range(H)]
        stored = [sem(f"stored{u}") for u in range(H)]
        xw = v.x[0:FULL_WIN * P, :].rearrange("(w p) f -> p w f", p=P)
        tw = [t[0:NPAD, :].rearrange("(w p) f -> p w f", p=P) for t in tables]
        LOADS = 16 * (3 if last else 4)
        LAST_LOADS = LOADS + (0 if last else 3 * 16)

        def bias_rows(u):
            return ht[C:A1, u, :]

        with nc.Block() as block:
            @block.sync
            def _(sp):
                def step(i):
                    for u in range(H):
                        g = H * i + u
                        wait(sp, fin_ready if last else x1_ready, g - 1)
                        wait(sp, o_mm, g - 1)
                        if not last:
                            if is_last(i, STEPS) and u == H - 1:
                                k = FULL_WIN - W * g
                                wait(sp, kept_it, g - 1)
                                sp.dma_start(xs[:, u, 0:k, :], xw[:, FULL_WIN - k:FULL_WIN, :]).then_inc(loaded[u], 16)
                                sp.dma_start(xs[0:REST, u, k, :], v.x[FULL_WIN * P:N, :]).then_inc(loaded[u], 16)
                                sp.dma_start(xs[REST:P, u, k, :], v.sums[0][N:(FULL_WIN + 1) * P, 0:C]).then_inc(loaded[u], 16)
                                sp.dma_start(xs[:, u, k + 1:W, :], tw[0][:, FULL_WIN + 1:NWIN, 0:C]).then_inc(loaded[u], 16)
                                assert k + 2 == W
                            else:
                                wait(sp, kept_it, g - 1)
                                sp.dma_start(xs[:, u, :, :], xw[:, bass.ds(W * g, W), :]).then_inc(loaded[u], 16)
                        for s, t in ((sa, tw[0]), (sb_, tw[1])):
                            sp.dma_start(s[:, u, :, :], t[:, bass.ds(W * g, W), :]).then_inc(loaded[u], 16)
                        sp.dma_start(bias_rows(u), v.valid[:, bass.ds(g * WP, WP)]).then_inc(loaded[u], 16)
                loop(sp, STEPS, step)

            @block.gpsimd
            def _(pool):
                def step(i):
                    for u in range(H):
                        g = H * i + u
                        if last:
                            wait(pool, fin_ready, g - 1)
                            pool.sem_inc(turn, 1)
                            pool.tensor_copy(xs[:, u, :, :].rearrange("p w c -> p (w c)"), v.x1[:, bass.ds(g * W * C, W * C)])
                            pool.tensor_copy(mine[:, u, :], v.kept[:, bass.ds(g, 1), :].rearrange("p a c -> p (a c)")).then_inc(took, 1)
                            wait(pool, y_ready, g + 1)
                            a_node = v.rows4[:, 0:C].unsqueeze(1).to_broadcast([P, W, C])
                            pool.tensor_tensor(y[:, u, :, :], y[:, u, :, :], a_node, ALU.mult).then_inc(pool_chain, 1)
                            wait(pool, pool_chain, 2 * g + 1)
                            pool.tensor_tensor(y[:, u, :, :], y[:, u, :, :], xs[:, u, :, :], ALU.add).then_inc(pool_chain, 1)
                            wait(pool, pool_chain, 2 * g + 2)
                            pool.sem_inc(y_scaled, 1)
                        else:
                            wait(pool, xn_ready, g + 1)
                            pool.sem_inc(turn, 1)
                            pool.tensor_copy(v.x1[:, bass.ds(g * W * C, W * C)], xs[:, u, :, :].rearrange("p w c -> p (w c)"))
                            pool.tensor_copy(v.kept[:, bass.ds(g, 1), :].rearrange("p a c -> p (a c)"), mine[:, u, :]).then_inc(kept_it, 1)
                loop(pool, STEPS, step)

            @block.vector
            def _(dve):
                if not last:
                    for u in range(H):
                        dve.memset(y[:, u, :, C:A1], 1.0).then_inc(ready, 1)

                def make_x1(i, u, g):
                    m = [mom[:, u, k, :] for k in range(8)]
                    rstd, shift, dg = (mine[:, u, k * W:(k + 1) * W] for k in range(3))
                    wait(dve, kept_it, g - 1)
                    dve.tensor_tensor(sa[:, u, :, :], sa[:, u, :, :], sb_[:, u, :, :], ALU.add).then_inc(chain, 1)
                    wait(dve, chain, 7 * g + 1)
                    dve.tensor_copy(dg, sa[:, u, :, C])
                    dve.tensor_scalar(m[0], sa[:, u, :, C], 1.0, None, ALU.max).then_inc(chain, 1)
                    wait(dve, chain, 7 * g + 2)
                    dve.reciprocal(m[1], m[0]).then_inc(chain, 1)
                    wait(dve, chain, 7 * g + 3)
                    for w in range(W):
                        last_ = dve.scalar_tensor_tensor(xs[:, u, w, :], sa[:, u, w, 0:C], m[1][:, w:w + 1], xs[:, u, w, :],
                                                         ALU.mult, ALU.add)
                    last_.then_inc(x1_ready, 1)
                    wait(dve, x1_ready, g + 1)
                    for w in range(W):
                        last_ = dve.bn_stats(bn[:, u, w, :], xs[:, u, w, :])
                    last_.then_inc(chain, 1)
                    wait(dve, chain, 7 * g + 4)
                    me, se, mo, so = (bn[:, u, :, k] for k in (1, 2, 4, 5))
                    dve.tensor_tensor(m[2], me, mo, ALU.add)
                    dve.tensor_tensor(m[3], me, mo, ALU.subtract)
                    dve.tensor_tensor(m[4], se, so, ALU.add).then_inc(chain, 1)
                    wait(dve, chain, 7 * g + 5)
                    dve.scalar_tensor_tensor(m[5], m[3], 0.25, m[3], ALU.mult, ALU.mult).then_inc(chain, 1)
                    wait(dve, chain, 7 * g + 6)
                    dve.scalar_tensor_tensor(m[6], m[4], 1.0 / C, m[5], ALU.mult, ALU.add).then_inc(var_ready, 1)
                    wait(dve, std_ready, g + 1)
                    dve.reciprocal(rstd, m[7]).then_inc(chain, 1)
                    wait(dve, chain, 7 * g + 7)
                    dve.scalar_tensor_tensor(shift, m[2], -0.5, rstd, ALU.mult, ALU.mult).then_inc(scaled, 1)
                    wait(dve, scaled, g + 1)

                def step(i):
                    for u in range(H):
                        g = H * i + u
                        wait(dve, loaded[u], LAST_LOADS + LOADS * i if is_last(i, STEPS) and u == H - 1 else LOADS * (i + 1))
                        if last:
                            wait(dve, took, g + 1)
                        else:
                            make_x1(i, u, g)
                        wait(dve, t_mm, g - 1)
                        for w in range(W):
                            last_ = dve.tensor_scalar(xn[:, u, w, :], xs[:, u, w, :], mine[:, u, w:w + 1],
                                                      mine[:, u, W + w:W + w + 1], ALU.mult, ALU.add)
                        last_.then_inc(xn_ready, 1)
                        if last:
                            c_node, a_msg, c_msg = (v.rows4[:, k * C:(k + 1) * C] for k in (1, 2, 3))
                            wait(dve, stored[u], 16 * i)
                            dve.tensor_tensor(sa[:, u, :, :], sa[:, u, :, :], sb_[:, u, :, :], ALU.add).then_inc(chain, 1)
                            wait(dve, chain, 4 * g + 1)
                            dve.tensor_tensor(sa[:, u, :, :], sa[:, u, :, :], a_msg.unsqueeze(1).to_broadcast([P, W, C]),
                                              ALU.mult).then_inc(chain, 1)
                            wait(dve, chain, 4 * g + 2)
                            for w in range(W):
                                last_ = dve.scalar_tensor_tensor(sa[:, u, w, :], c_msg, mine[:, u, 2 * W + w:2 * W + w + 1],
                                                                 sa[:, u, w, :], ALU.mult, ALU.add)
                            last_.then_inc(chain, 1)
                            wait(dve, chain, 4 * g + 3)
                            dve.tensor_tensor(sa[:, u, :, :], sa[:, u, :, :], c_node.unsqueeze(1).to_broadcast([P, W, C]),
                                              ALU.add).then_inc(chain, 1)
                            wait(dve, chain, 4 * g + 4)
                            wait(dve, y_scaled, g + 1)
                            dve.tensor_tensor(fin[:, u, :, :], sa[:, u, :, :], y[:, u, :, :], ALU.add).then_inc(fin_ready, 1)
                loop(dve, STEPS, step)
                if not last:
                    dve.wait_ge(gram_done, NODE_GROUPS)
                    dve.tensor_copy(v.grams[:, 0, :], ps_gram[0:C, 0:A1]).then_inc(ready, 1)
                    dve.wait_ge(ready, H + 1)

            @block.tensor
            def _(pe):
                if not last:
                    pe.wait_ge(ready, H)

                def step(i):
                    for u in range(H):
                        g = H * i + u
                        wait(pe, xn_ready, g + 1)
                        wait(pe, ht_ready, g - 1)
                        for w in range(W):
                            m = pe.transpose(ps_t[0:C, u * 512 + w * P:u * 512 + (w + 1) * P], xn[:, u, w, :], v.ident[:, :])
                        m.then_inc(t_mm, 1)
                        wait(pe, ht_ready, g + 1)
                        wait(pe, loaded[u], LAST_LOADS + LOADS * i if is_last(i, STEPS) and u == H - 1 else LOADS * (i + 1))
                        if last:
                            wait(pe, y_ready, g - 1)
                            for w in range(W):
                                m = pe.matmul(ps_o[:, u * 512 + w * C:u * 512 + (w + 1) * C], ht[:, u, w * P:(w + 1) * P],
                                              v.w_cat[:, 2 * C:], start=True, stop=True)
                            m.then_inc(o_mm, 1)
                        else:
                            wait(pe, y_ready, g)
                            for w in range(W):
                                m = pe.matmul(ps_o[:, w * 512:w * 512 + 3 * C], ht[:, u, w * P:(w + 1) * P], v.w_cat[:, :],
                                              start=True, stop=True)
                            m.then_inc(o_mm, 1)
                            wait(pe, y_ready, g + 1)
                            for w in range(W):
                                first = isinstance(i, int) and i == 0 and u == 0 and w == 0
                                end = is_last(i, STEPS) and u == H - 1 and w == W - 1
                                m = pe.matmul(ps_gram[0:C, 0:A1], y[:, u, w, 0:C], y[:, u, w, :], start=first, stop=end,
                                              skip_group_check=True)
                            m.then_inc(gram_done, 1)
                loop(pe, STEPS, step)

            @block.scalar
            def _(act):
                def step(i):
                    for u in range(H):
                        g = H * i + u
                        if not last:
                            wait(act, var_ready, g + 1)
                            act.activation(mom[:, u, 7, :], mom[:, u, 6, :], ACT.Sqrt, bias=v.eps[:, :]).then_inc(std_ready, 1)
                        wait(act, t_mm, g + 1)
                        wait(act, o_mm, g - 1)
                        act.activation(ht[0:C, u, :], ps_t[0:C, u * 512:u * 512 + WP], ACT.Relu).then_inc(ht_ready, 1)
                        wait(act, o_mm, g + 1)
                        if last:
                            wait(act, fin_ready, g - 1)
                            act.activation(y[:, u, :, :], ps_o[:, u * 512:u * 512 + W * C].rearrange("p (w c) -> p w c", w=W),
                                           ACT.Relu).then_inc(y_ready, 1)
                            wait(act, fin_ready, g + 1)
                            if is_last(i, STEPS) and u == H - 1:
                                k = FULL_WIN - W * g
                                act.dma_start(v.out[W * g * P:FULL_WIN * P, :].rearrange("(w p) f -> p w f", p=P),
                                              fin[:, u, 0:k, :]).then_inc(stored[u], 16)
                                act.dma_start(v.out[FULL_WIN * P:N, :], fin[0:REST, u, k, :]).then_inc(stored[u], 16)
                            else:
                                act.dma_start(v.out[bass.ds(g * WP, WP), :].rearrange("(w p) f -> p w f", p=P),
                                              fin[:, u, :, :]).then_inc(stored[u], 16)
                        else:
                            o = ps_o[:, :].rearrange("p (w c) -> p w c", w=W)
                            wait(act, stored[u], 32 * i)
                            act.activation(pq[:, u, :, :], o[:, :, 0:2 * C], ACT.Copy).then_inc(pq_ready, 1)
                            wait(act, gram_done, g - 1)
                            act.activation(y[:, u, :, 0:C], o[:, :, 2 * C:3 * C], ACT.Relu).then_inc(y_ready, 1)
                            wait(act, pq_ready, g + 1)
                            for t, part in ((v.p_tab, pq[:, u, :, 0:C]), (v.q_tab, pq[:, u, :, C:2 * C])):
                                act.dma_start(t[bass.ds(g * WP, WP), :].rearrange("(p w) f -> p w f", w=W), part
                                              ).then_inc(stored[u], 16)
                loop(act, STEPS, step)
                act.wait_ge(stored[0], (1 if last else 2) * 16 * STEPS)
                act.wait_ge(stored[1], (16 * STEPS + 16) if last else 32 * STEPS)


def sorted_node_phase(nc, v, last):
    H = 2
    STEPS = NODE_GROUPS // H
    tag = "sd" if last else "sc"
    WP = W * P
    RS = W * SLOTS
    with ExitStack() as st:
        def sb(name, shape, dt=F32):
            return st.enter_context(nc.sbuf_tensor(name + tag, shape, dt))

        def sem(name):
            return st.enter_context(nc.semaphore(name + tag))

        def bank(name, n=1):
            return st.enter_context(nc.psum_tensor(name + tag, [P, n * 512], F32))

        er = sb("er", [WP_E, H, W, SLOTS * ROW])
        base = sb("base", [WP_E, RS])
        rel = sb("rel", [WP_E, H, RS])
        hot = sb("hot", [WP_E, H, RS, P])
        xn = sb("xn", [P, H, W, C])
        ht = sb("ht", [A1, H, WP])
        mine = sb("mine", [P, H, 3 * W])
        y = sb("y", [P, H, W, C if last else A1])
        ps_agg, ps_t = bank("ps_agg", H), bank("ps_t")
        if last:
            tot = sb("tot", [P, H, W, C])
            fin = sb("fin", [P, H, W, C])
            ps_o = bank("ps_o", 1)
        else:
            xs = sb("xs", [P, H, W, C])
            pq = sb("pq", [P, H, W, 2 * C])
            bn, mom = sb("bn", [P, H, W, 6]), sb("mom", [P, H, 8, W])
            ps_o = bank("ps_o", W)
            ps_gram = bank("ps_gram")
        names = ("base_set", "rel_ready", "hot_ready", "agg_mm", "deg_chain", "x1_ready", "stats_chain", "var_ready",
                 "std_ready", "rstd_ready", "scaled", "xn_ready", "t_mm", "ht_ready", "o_mm", "pq_ready", "y_ready",
                 "gram_done", "kept_it", "took", "agg_used", "tot_chain", "tot_ready", "pool_chain", "y_scaled",
                 "fin_ready", "turn", "act_turn", "sp_turn", "ready")
        (base_set, rel_ready, hot_ready, agg_mm, deg_chain, x1_ready, stats_chain, var_ready, std_ready, rstd_ready,
         scaled, xn_ready, t_mm, ht_ready, o_mm, pq_ready, y_ready, gram_done, kept_it, took, agg_used, tot_chain,
         tot_ready, pool_chain, y_scaled, fin_ready, turn, act_turn, sp_turn, ready) = (sem(n) for n in names)
        rows_in = [sem(f"rows_in{u}") for u in range(H)]
        x_in = [sem(f"x_in{u}") for u in range(H)]
        stored = [sem(f"stored{u}") for u in range(H)]
        xw = v.x[0:FULL_WIN * P, :].rearrange("(w p) f -> p w f", p=P)
        K_END = FULL_WIN - W * (NODE_GROUPS - 1)

        def at(i, u, d):
            return i + (u + d) // H, (u + d) % H

        def pipe(engine, body):
            body(0)
            body(1)
            with engine.Fori(2, STEPS - 1) as i:
                body(i)
            body(STEPS - 1)

        def is_first(i, u):
            return isinstance(i, int) and i == 0 and u == 0

        def is_end(i, u):
            return is_last(i, STEPS) and u == H - 1

        def before(i, u):
            return None if is_first(i, u) else at(i, u, -1)

        def after(i, u, d=1):
            a = at(i, u, d)
            return None if isinstance(a[0], int) and a[0] >= STEPS else a

        with nc.Block() as block:
            @block.sync
            def _(sp):
                def load_rows(i, u):
                    g = H * i + u
                    _, first_rows = nc.values_load_multi_w_load_instructions(
                        v.starts[0:1, bass.ds(W * g, W)], engines=(sp.engine,), min_val=0, max_val=E,
                        skip_runtime_bounds_check_because="sums of counts of E edges are at most E")
                    wait(sp, agg_mm, g - 1)
                    sp.sem_inc(sp_turn, 1)
                    for w in range(W):
                        sp.dma_start(er[:, u, w, :], v.edge_rows[bass.ds(first_rows[w], WP_E * SLOTS), :]
                                     .rearrange("(p r) c -> p (r c)", p=WP_E)).then_inc(rows_in[u], 16)

                def load_x(i, u):
                    g = H * i + u
                    wait(sp, kept_it, g - 1)
                    wait(sp, xn_ready, g - 1)
                    if is_end(i, u):
                        k = K_END
                        sp.dma_start(xs[:, u, 0:k, :], xw[:, FULL_WIN - k:FULL_WIN, :]).then_inc(x_in[u], 16)
                        sp.dma_start(xs[0:REST, u, k, :], v.x[FULL_WIN * P:N, :]).then_inc(x_in[u], 16)
                        nothing = v.valid[0:1, N:N + C]
                        sp.dma_start(xs[REST:P, u, k, :], nothing.to_broadcast([P - REST, C])).then_inc(x_in[u], 16)
                        sp.dma_start(xs[:, u, k + 1, :], nothing.to_broadcast([P, C])).then_inc(x_in[u], 16)
                        assert k + 2 == W
                        wait(sp, o_mm, g - 1)
                        sp.dma_start(ht[C:A1, u, :], v.valid[:, g * WP:(g + 1) * WP]).then_inc(x_in[u], 16)
                    else:
                        sp.dma_start(xs[:, u, :, :], xw[:, bass.ds(W * g, W), :]).then_inc(x_in[u], 16)

                def store(i, u):
                    g = H * i + u
                    if last:
                        wait(sp, fin_ready, g + 1)
                        if is_end(i, u):
                            k = K_END
                            sp.dma_start(v.out[W * g * P:FULL_WIN * P, :].rearrange("(w p) f -> p w f", p=P),
                                         fin[:, u, 0:k, :]).then_inc(stored[u], 16)
                            sp.dma_start(v.out[FULL_WIN * P:N, :], fin[0:REST, u, k, :]).then_inc(stored[u], 16)
                        else:
                            sp.dma_start(v.out[bass.ds(g * WP, WP), :].rearrange("(w p) f -> p w f", p=P),
                                         fin[:, u, :, :]).then_inc(stored[u], 16)
                    else:
                        wait(sp, pq_ready, g + 1)
                        for t, c0 in ((v.p_tab, 0), (v.q_tab, W * C)):
                            sp.dma_start(t[bass.ds(g * WP, WP), :].rearrange("(p w) f -> p (w f)", w=W),
                                         pq[:, u, :, :].rearrange("p w c -> p (w c)")[:, c0:c0 + W * C]).then_inc(stored[u], 16)

                load_rows(0, 0)
                load_rows(0, 1)
                if not last:
                    load_x(0, 0)

                def step(i):
                    for u in range(H):
                        if after(i, u, 2):
                            load_rows(*after(i, u, 2))
                        if after(i, u) and not last:
                            load_x(*after(i, u))
                        if before(i, u):
                            store(*before(i, u))
                pipe(sp, step)
                store(STEPS - 1, H - 1)
                for u in range(H):
                    sp.wait_ge(stored[u], (16 * STEPS + 16 * u) if last else 32 * STEPS)

            @block.gpsimd
            def _(pool):
                def take_factors(i, u):
                    g = H * i + u
                    wait(pool, xn_ready, g - 1)
                    pool.sem_inc(turn, 1)
                    pool.tensor_copy(mine[:, u, :], v.kept[:, bass.ds(g, 1), :].rearrange("p a c -> p (a c)")).then_inc(took, 1)

                def node_part(i, u):
                    g = H * i + u
                    a_node, c_node = (v.rows4[:, k * C:(k + 1) * C].unsqueeze(1).to_broadcast([P, W, C]) for k in (0, 1))
                    wait(pool, y_ready, g + 1)
                    pool.tensor_tensor(y[:, u, :, :], y[:, u, :, :], a_node, ALU.mult).then_inc(pool_chain, 1)
                    wait(pool, pool_chain, 2 * g + 1)
                    pool.tensor_tensor(y[:, u, :, :], y[:, u, :, :], c_node, ALU.add).then_inc(pool_chain, 1)
                    wait(pool, pool_chain, 2 * g + 2)
                    pool.sem_inc(turn, 1)
                    pool.tensor_tensor(y[:, u, :, :].rearrange("p w c -> p (w c)"), y[:, u, :, :].rearrange("p w c -> p (w c)"),
                                       v.x1[:, bass.ds(g * W * C, W * C)], ALU.add).then_inc(y_scaled, 1)

                if last:
                    take_factors(0, 0)

                def step(i):
                    for u in range(H):
                        g = H * i + u
                        if last:
                            if after(i, u):
                                take_factors(*after(i, u))
                            if before(i, u):
                                node_part(*before(i, u))
                        else:
                            wait(pool, x1_ready, g + 1)
                            wait(pool, scaled, g + 1)
                            pool.sem_inc(turn, 1)
                            pool.tensor_copy(v.x1[:, bass.ds(g * W * C, W * C)], xs[:, u, :, :].rearrange("p w c -> p (w c)"))
                            pool.tensor_copy(v.kept[:, bass.ds(g, 1), :].rearrange("p a c -> p (a c)"), mine[:, u, :]).then_inc(kept_it, 1)
                pipe(pool, step)
                if last:
                    node_part(STEPS - 1, H - 1)

            @block.vector
            def _(dve):
                for r in range(SLOTS):
                    for w in range(W):
                        dve.memset(base[:, w * SLOTS + r:w * SLOTS + r + 1], float(w * P))
                for u in range(H):
                    dve.memset(ht[C:A1, u, :], 1.0)
                    if not last:
                        dve.memset(y[:, u, :, C:A1], 1.0)
                dve.sem_inc(ready, 1)
                dve.drain().then_inc(base_set, 1)

                def one_hot(i, u):
                    g = H * i + u
                    wait(dve, rows_in[u], 16 * W * (i + 1))
                    wait(dve, base_set, g + 1)
                    dst = er[:, u, :, :].rearrange("p w (r c) -> p (w r) c", r=SLOTS)[:, :, A1]
                    dve.tensor_tensor(rel[:, u, :], dst, base[:, :], ALU.subtract).then_inc(rel_ready, 1)
                    wait(dve, rel_ready, g + 1)
                    wait(dve, agg_mm, g - 1)
                    dve.tensor_scalar(base[:, :], base[:, :], float(WP), None, ALU.add).then_inc(base_set, 1)
                    dve.tensor_tensor(hot[:, u, :, :], rel[:, u, :].unsqueeze(2).to_broadcast([WP_E, RS, P]),
                                      v.line[0:WP_E, :].unsqueeze(1).to_broadcast([WP_E, RS, P]), ALU.is_equal).then_inc(hot_ready, 1)

                def sums(u):
                    return ps_agg[:, u * 512:u * 512 + W * A1].rearrange("p (w c) -> p w c", w=W)

                def make_x1(i, u):
                    g = H * i + u
                    m = [mom[:, u, k, :] for k in range(8)]
                    agg = sums(u)
                    wait(dve, agg_mm, g + 1)
                    wait(dve, kept_it, g - 1)
                    dve.tensor_copy(mine[:, u, 2 * W:], agg[:, :, C])
                    dve.tensor_scalar(m[0], agg[:, :, C], 1.0, None, ALU.max).then_inc(deg_chain, 1)
                    wait(dve, deg_chain, 2 * g + 1)
                    dve.reciprocal(m[1], m[0]).then_inc(deg_chain, 1)
                    wait(dve, deg_chain, 2 * g + 2)
                    wait(dve, x_in[u], 16 * STEPS + 4 * 16 if is_end(i, u) else 16 * (i + 1))
                    for w in range(W):
                        op = dve.scalar_tensor_tensor(xs[:, u, w, :], agg[:, w, 0:C], m[1][:, w:w + 1], xs[:, u, w, :],
                                                      ALU.mult, ALU.add)
                    op.then_inc(x1_ready, 1)
                    wait(dve, x1_ready, g + 1)
                    for w in range(W):
                        op = dve.bn_stats(bn[:, u, w, :], xs[:, u, w, :])
                    op.then_inc(stats_chain, 1)
                    wait(dve, stats_chain, 3 * g + 1)
                    me, se, mo, so = (bn[:, u, :, k] for k in (1, 2, 4, 5))
                    dve.tensor_tensor(m[2], me, mo, ALU.add)
                    dve.tensor_tensor(m[3], me, mo, ALU.subtract)
                    dve.tensor_tensor(m[4], se, so, ALU.add).then_inc(stats_chain, 1)
                    wait(dve, stats_chain, 3 * g + 2)
                    dve.scalar_tensor_tensor(m[5], m[3], 0.25, m[3], ALU.mult, ALU.mult).then_inc(stats_chain, 1)
                    wait(dve, stats_chain, 3 * g + 3)
                    dve.scalar_tensor_tensor(m[6], m[4], 1.0 / C, m[5], ALU.mult, ALU.add).then_inc(var_ready, 1)

                def factors(i, u):
                    g = H * i + u
                    wait(dve, std_ready, g + 1)
                    dve.reciprocal(mine[:, u, 0:W], mom[:, u, 7, :]).then_inc(rstd_ready, 1)
                    wait(dve, rstd_ready, g + 1)
                    dve.scalar_tensor_tensor(mine[:, u, W:2 * W], mom[:, u, 2, :], -0.5, mine[:, u, 0:W], ALU.mult, ALU.mult
                                             ).then_inc(scaled, 1)

                def message_part(i, u):
                    g = H * i + u
                    a_msg, c_msg = (v.rows4[:, k * C:(k + 1) * C] for k in (2, 3))
                    agg = sums(u)
                    wait(dve, agg_mm, g + 1)
                    wait(dve, fin_ready, g - 1)
                    dve.tensor_tensor(tot[:, u, :, :], agg[:, :, 0:C], a_msg.unsqueeze(1).to_broadcast([P, W, C]),
                                      ALU.mult).then_inc(tot_chain, 1)
                    wait(dve, tot_chain, g + 1)
                    for w in range(W):
                        op = dve.scalar_tensor_tensor(tot[:, u, w, :], c_msg, agg[:, w, C:A1], tot[:, u, w, :], ALU.mult, ALU.add)
                    op.then_inc(agg_used, 1)

                def finish(i, u):
                    g = H * i + u
                    wait(dve, agg_used, g + 1)
                    wait(dve, stored[u], 16 * i)
                    wait(dve, y_scaled, g + 1)
                    dve.tensor_tensor(fin[:, u, :, :], tot[:, u, :, :], y[:, u, :, :], ALU.add).then_inc(fin_ready, 1)

                one_hot(0, 0)

                def step(i):
                    for u in range(H):
                        if last:
                            message_part(i, u)
                            if after(i, u):
                                one_hot(*after(i, u))
                            if before(i, u):
                                finish(*before(i, u))
                        else:
                            make_x1(i, u)
                            if after(i, u):
                                one_hot(*after(i, u))
                            factors(i, u)
                pipe(dve, step)
                if last:
                    finish(STEPS - 1, H - 1)
                else:
                    dve.wait_ge(gram_done, NODE_GROUPS)
                    dve.tensor_copy(v.grams[:, 0, :], ps_gram[0:C, 0:A1]).then_inc(ready, 1)
                    dve.wait_ge(ready, 2)

            @block.tensor
            def _(pe):
                pe.wait_ge(base_set, 1)

                def aggregate(i, u):
                    g = H * i + u
                    wait(pe, hot_ready, g + 1)
                    wait(pe, agg_used if last else x1_ready, g - 1)
                    for w in range(W):
                        for r in range(SLOTS):
                            m = pe.matmul(ps_agg[:, u * 512 + w * A1:u * 512 + (w + 1) * A1], hot[:, u, w * SLOTS + r, :],
                                          er[:, u, w, r * ROW:r * ROW + A1], start=r == 0, stop=r == SLOTS - 1)
                    m.then_inc(agg_mm, 1)

                def turn_rows(i, u):
                    g = H * i + u
                    wait(pe, xn_ready, g + 1)
                    wait(pe, ht_ready, g)
                    for w in range(W):
                        m = pe.transpose(ps_t[0:C, w * P:(w + 1) * P], xn[:, u, w, :], v.ident[:, :])
                    m.then_inc(t_mm, 1)

                def products(i, u):
                    g = H * i + u
                    wait(pe, ht_ready, g + 1)
                    wait(pe, y_ready, g)
                    if is_end(i, u) and not last:
                        wait(pe, x_in[u], 16 * STEPS + 4 * 16)
                    for w in range(W):
                        if last:
                            m = pe.matmul(ps_o[:, w * C:(w + 1) * C], ht[:, u, w * P:(w + 1) * P], v.w_cat[:, 2 * C:],
                                          start=True, stop=True)
                        else:
                            m = pe.matmul(ps_o[:, w * 512:w * 512 + 3 * C], ht[:, u, w * P:(w + 1) * P], v.w_cat[:, :],
                                          start=True, stop=True)
                    m.then_inc(o_mm, 1)

                def gram(i, u):
                    g = H * i + u
                    wait(pe, y_ready, g + 1)
                    for w in range(W):
                        m = pe.matmul(ps_gram[0:C, 0:A1], y[:, u, w, 0:C], y[:, u, w, :], start=is_first(i, u) and w == 0,
                                      stop=is_end(i, u) and w == W - 1, skip_group_check=True)
                    m.then_inc(gram_done, 1)

                aggregate(0, 0)

                def step(i):
                    for u in range(H):
                        if before(i, u):
                            products(*before(i, u))
                        if after(i, u):
                            aggregate(*after(i, u))
                        turn_rows(i, u)
                        if before(i, u) and not last:
                            gram(*before(i, u))
                pipe(pe, step)
                products(STEPS - 1, H - 1)
                if not last:
                    gram(STEPS - 1, H - 1)

            @block.scalar
            def _(act):
                def norm(i, u):
                    g = H * i + u
                    if last:
                        wait(act, took, g + 1)
                    else:
                        wait(act, scaled, g + 1)
                    wait(act, t_mm, g - 1)
                    if last:
                        act.sem_inc(act_turn, 1)
                    for w in range(W):
                        rows = v.x1[:, bass.ds(g * W * C + w * C, C)] if last else xs[:, u, w, :]
                        op = act.activation(xn[:, u, w, :], rows, ACT.Identity, scale=mine[:, u, w:w + 1],
                                            bias=mine[:, u, W + w:W + w + 1])
                    op.then_inc(xn_ready, 1)

                def outputs(i, u):
                    g = H * i + u
                    wait(act, o_mm, g + 1)
                    if last:
                        wait(act, fin_ready, g - 1)
                        act.activation(y[:, u, :, :], ps_o[:, 0:W * C].rearrange("p (w c) -> p w c", w=W), ACT.Relu).then_inc(y_ready, 1)
                    else:
                        o = ps_o[:, :].rearrange("p (w c) -> p w c", w=W)
                        wait(act, stored[u], 32 * i)
                        pq_ = pq[:, u, :, :].rearrange("p w c -> p (w c)").rearrange("p (t w c) -> p w t c", t=2, w=W)
                        act.activation(pq_, o[:, :, 0:2 * C].rearrange("p w (t c) -> p w t c", t=2), ACT.Copy).then_inc(pq_ready, 1)
                        wait(act, gram_done, g - 1)
                        act.activation(y[:, u, :, 0:C], o[:, :, 2 * C:3 * C], ACT.Relu).then_inc(y_ready, 1)

                def turned(i, u):
                    g = H * i + u
                    wait(act, t_mm, g + 1)
                    wait(act, o_mm, g - 1)
                    act.activation(ht[0:C, u, :], ps_t[0:C, :], ACT.Relu).then_inc(ht_ready, 1)

                def step(i):
                    for u in range(H):
                        if not last:
                            g = H * i + u
                            wait(act, var_ready, g + 1)
                            act.activation(mom[:, u, 7, :], mom[:, u, 6, :], ACT.Sqrt, bias=v.eps[:, :]).then_inc(std_ready, 1)
                        norm(i, u)
                        if before(i, u):
                            outputs(*before(i, u))
                        turned(i, u)
                pipe(act, step)
                outputs(STEPS - 1, H - 1)


def norm_rows_phase(nc, v):
    with ExitStack() as st:
        diag = st.enter_context(nc.sbuf_tensor("diag" + v.tag, [C, 4, C], F32))
        scrap = st.enter_context(nc.sbuf_tensor("scrap_n" + v.tag, [C, C], F32))
        ps = st.enter_context(nc.psum_tensor("ps_rows" + v.tag, [P, 512], F32))
        chain, std_ready, diag_ready, rows_mm = (st.enter_context(nc.semaphore(n + v.tag)) for n in ("chain_n", "std_n", "diag_n", "rows_n"))
        s = v.small
        with nc.Block() as block:
            @block.vector
            def _(dve):
                n = [0]

                def link(ins):
                    n[0] += 1
                    ins.then_inc(chain, 1)
                    dve.wait_ge(chain, n[0])

                for l, (gamma, beta) in enumerate(((v.gn, v.btn), (v.gm, v.btm))):
                    sq, mean, msq, var, std, rstd, a, am, c = (s[:, 9 * l + k:9 * l + k + 1] for k in range(9))
                    count = (N, E)[l]
                    link(dve.scalar_tensor_tensor(scrap[:, :], v.grams[:, l, 0:C], 1.0, v.ident[0:C, 0:C], ALU.mult, ALU.mult,
                                                  accum_out=sq))
                    link(dve.tensor_scalar(mean, v.grams[:, l, C:A1], 1.0 / count, None, ALU.mult))
                    link(dve.tensor_tensor(msq, mean, mean, ALU.mult))
                    dve.scalar_tensor_tensor(var, sq, 1.0 / count, msq, ALU.mult, ALU.subtract).then_inc(chain, 1)
                    n[0] += 1
                    dve.wait_ge(std_ready, l + 1)
                    link(dve.reciprocal(rstd, std))
                    link(dve.tensor_tensor(a, gamma, rstd, ALU.mult))
                    link(dve.tensor_tensor(am, a, mean, ALU.mult))
                    link(dve.tensor_tensor(c, beta, am, ALU.subtract))
                    for k, col in ((2 * l, a), (2 * l + 1, c)):
                        dve.tensor_scalar(diag[:, k, :], v.ident[0:C, 0:C], col, None, ALU.mult).then_inc(diag_ready, 1)
                dve.wait_ge(rows_mm, 1)
                link(dve.tensor_copy(v.rows4[:, :], ps[:, 0:4 * C]))

            @block.scalar
            def _(act):
                for l in range(2):
                    act.wait_ge(chain, 8 * l + 4)
                    act.activation(s[:, 9 * l + 4:9 * l + 5], s[:, 9 * l + 3:9 * l + 4], ACT.Sqrt, bias=v.eps[0:C, :]).then_inc(std_ready, 1)

            @block.tensor
            def _(pe):
                pe.wait_ge(diag_ready, 4)
                pe.matmul(ps[:, 0:4 * C], v.ones[0:C, :], diag[:, :, :].rearrange("p k c -> p (k c)"),
                          start=True, stop=True).then_inc(rows_mm, 1)


_OUT = ((N, C), "float32")


def kernel(x, src, dst, edge_attr_4, L1_gnn_W_node, L1_gnn_b_node, L1_gnn_g_node, L1_gnn_beta_node, L1_gnn_W_edge,
           L1_gnn_b_edge, L1_gnn_g_edge, L1_gnn_beta_edge, L1_gnn_W_msg, L1_gnn_b_msg, L1_gnn_g_msg, L1_gnn_beta_msg):
    import numpy as np
    import concourse.bacc as bacc
    from concourse.bass_utils import run_bass_kernel_spmd as run

    def padded(a, fill):
        a = np.asarray(a)
        return np.concatenate([a, np.full((EPAD - E,) + a.shape[1:], fill, a.dtype)])

    src_p, dst_p = padded(src, 0), padded(dst, PAD_DST)
    valid = np.zeros((1, NPAD), np.float32)
    valid[0, :N] = 1.0
    def by_partition(a):
        return a.reshape(EDGE_GROUPS, P, T).transpose(1, 0, 2).reshape(P, EDGE_GROUPS * T)

    def by_tile(a):
        return a.reshape(-1, EDGE_GROUPS, P, T).transpose(0, 1, 3, 2).reshape(-1, EPAD)

    arrays = {
        "x": x, "src_g": by_partition(src_p), "dst_g": by_partition(dst_p), "dst_row": by_tile(dst_p),
        "dst_line": np.concatenate([dst_p, np.full(P, PAD_DST, dst_p.dtype)]).reshape(1, -1),
        "ea_t": np.asarray(edge_attr_4).T, "ea_g": by_tile(np.ascontiguousarray(padded(edge_attr_4, 0).T)), "valid": valid,
        "w_node": L1_gnn_W_node, "b_node": L1_gnn_b_node, "g_node": L1_gnn_g_node, "beta_node": L1_gnn_beta_node,
        "w_edge": L1_gnn_W_edge, "b_edge": L1_gnn_b_edge, "g_edge": L1_gnn_g_edge, "beta_edge": L1_gnn_beta_edge,
        "w_msg": L1_gnn_W_msg, "b_msg": L1_gnn_b_msg, "g_msg": L1_gnn_g_msg, "beta_msg": L1_gnn_beta_msg,
    }
    arrays = {k: np.ascontiguousarray(a) for k, a in arrays.items()}
    nc = bacc.Bacc("TRN2", target_bir_lowering=False, num_devices=1)
    args = [nc.dram_tensor("in_" + k, a.shape, mybir.dt.from_np(a.dtype), kind="ExternalInput").ap() for k, a in arrays.items()]
    out = nc.dram_tensor("out", _OUT[0], mybir.dt.from_np(np.dtype(_OUT[1])), kind="ExternalOutput").ap()
    program(nc, *args, out)
    r = run(nc, [{"in_" + k: a for k, a in arrays.items()}], core_ids=[0])
    return r.results[0]["out"]
```

```python
import concourse.bass as bass
from concourse import mybir
from contextlib import ExitStack

F32 = mybir.dt.float32
I32 = mybir.dt.int32
ALU = mybir.AluOpType
ACT = mybir.ActivationFunctionType
AXX = mybir.AxisListType.X

P = 128
N = 50000
E = 50000
C = 96
ED = 4
EPS = 1e-5
LEAD = 4
W = 4
NODE_GROUPS = 98
NWIN = W * NODE_GROUPS
NPAD = NWIN * P
FULL_WIN = N // P
REST = N - FULL_WIN * P
T = 4
EDGE_GROUPS = 100
EPAD = EDGE_GROUPS * T * P
PAD_DST = NPAD
DUMP = NPAD + 1
TABLE_ROWS = NPAD + 1 + P
R = 10
ROW_GROUPS = FULL_WIN // R
CHUNK = 500
NCHUNK = E // CHUNK
SLOTS = 2
WP_E = 96
STEP_EDGES = 2 * T * P
ROW = C + 2
HI, LO = 13, 32
A1 = C + 1
NACC = 2


class Shared:
    pass


def loop(engine, n, body):
    body(0)
    with engine.Fori(1, n - 1) as i:
        body(i)
    body(n - 1)


def wait(engine, sem, value):
    if not (isinstance(value, int) and value <= 0):
        engine.wait_ge(sem, value)


def is_last(i, n):
    return isinstance(i, int) and i == n - 1


def program(nc, x, src_g, dst_g, dst_row, dst_line, ea_t, ea_g, valid, w_node, b_node, g_node, beta_node, w_edge, b_edge,
            g_edge, beta_edge, w_msg, b_msg, g_msg, beta_msg, out):
    h1_tab = nc.dram_tensor("h1_tab", [N, C], F32, kind="Internal").ap()
    pq_tab = nc.dram_tensor("pq_tab", [2 * NPAD + 1, C], F32, kind="Internal").ap()
    sums = [nc.dram_tensor(f"sums{a}", [TABLE_ROWS, A1], F32, kind="Internal").ap() for a in range(NACC)]
    edge_rows = nc.dram_tensor("edge_rows", [EPAD, ROW], F32, kind="Internal").ap()
    sum_tab = nc.dram_tensor("sum_tab", [NPAD, C], F32, kind="Internal").ap()
    edge_idx = nc.dram_tensor("edge_idx", [P, EDGE_GROUPS * 4 * T], I32, kind="Internal").ap()
    msgs = [nc.dram_tensor(f"msgs{a}", [TABLE_ROWS, C], F32, kind="Internal").ap() for a in range(NACC)]

    whole = ExitStack()
    with whole:
        def keep(name, shape, dt=F32):
            return whole.enter_context(nc.sbuf_tensor(name, shape, dt))

        x1 = keep("x1", [P, NWIN * C])
        ident = keep("ident", [P, P])
        ones = keep("ones", [P, P])
        earlier = keep("earlier", [P, P])
        eps = keep("eps", [P, 1])
        dump_row = keep("dump_row", [P, 1])
        w_cat = keep("w_cat", [A1, 3 * C])
        w_ef = keep("w_ef", [A1, C])
        w_e = keep("w_e", [ED, C])
        cols = keep("cols", [C, 16])
        be, ge, bte, gn, btn, gm, btm = (cols[:, k:k + 1] for k in range(7))
        small = keep("small", [C, 32])
        rows4 = keep("rows4", [P, 4 * C])
        kept = keep("kept", [P, NODE_GROUPS, 3 * W])
        grams = keep("grams", [C, 2, A1])


        starts = keep("starts", [1, 416], I32)
        flag = keep("flag", [1, 1], I32)
        line = keep("line", [P, P])
        v = Shared()
        v.sum_tab = sum_tab
        v.edge_rows, v.edge_idx, v.dst_line = edge_rows, edge_idx, dst_line
        v.starts, v.flag, v.line, v.ea_g = starts, flag, line, ea_g
        v.x, v.src_g, v.dst_g, v.dst_row = x, src_g, dst_g, dst_row
        v.ea_t, v.valid, v.w_node, v.b_node = ea_t, valid, w_node, b_node
        v.g_node, v.beta_node, v.w_edge, v.b_edge = g_node, beta_node, w_edge, b_edge
        v.g_edge, v.beta_edge, v.w_msg, v.b_msg = g_edge, beta_edge, w_msg, b_msg
        v.g_msg, v.beta_msg, v.out, v.h1_tab = g_msg, beta_msg, out, h1_tab
        v.pq_tab, v.sums, v.msgs = pq_tab, sums, msgs
        v.x1, v.ident, v.ones, v.earlier = x1, ident, ones, earlier
        v.eps, v.dump_row, v.w_cat, v.w_ef = eps, dump_row, w_cat, w_ef
        v.w_e, v.be, v.ge, v.bte = w_e, be, ge, bte
        v.gn, v.btn, v.gm, v.btm = gn, btn, gm, btm
        v.small, v.rows4, v.kept, v.grams = small, rows4, kept, grams
        setup_phase(nc, v)
        plan_phase(nc, v)
        sorted_ok = nc.values_load(v.flag[0:1, 0:1], min_val=0, max_val=1)
        unused = nc.snapshot_sems()
        with nc.If(sorted_ok > 0):
            layers(nc, v, fast=True)
        nc.restore_sems(unused)
        with nc.Else():
            layers(nc, v, fast=False)


def layers(nc, v, fast):
    v.tag = "f" if fast else "s"
    if fast:
        sorted_phase(nc, v, second=False)
        norm_rows_phase(nc, v, (0,))
        sorted_phase(nc, v, second=True)
        norm_rows_phase(nc, v, (1,))
        finish_phase(nc, v)
    else:
        zero_phase(nc, v)
        scatter_phase(nc, v, second=False)
        scattered_node_phase(nc, v, last=False)
        scatter_phase(nc, v, second=True)
        norm_rows_phase(nc, v, (0, 1))
        scattered_node_phase(nc, v, last=True)


def setup_phase(nc, v):
    H = 3
    STEPS = ROW_GROUPS // H
    span = R * C
    main = FULL_WIN * P
    SHARE = (3, 3, 2)
    PER = sum(SHARE)
    LEFT = NCHUNK - PER * (STEPS - 1)
    BANKS = 4
    with ExitStack() as st:
        def sb(name, shape, dt=F32):
            return st.enter_context(nc.sbuf_tensor(name, shape, dt))

        def sem(name):
            return st.enter_context(nc.semaphore(name))

        xin = v.x1[:, 0:H * span].rearrange("p (u c) -> p u c", u=H)
        xout = v.x1[:, H * span:2 * H * span].rearrange("p (u c) -> p u c", u=H)
        o = 2 * H * span
        attr = v.x1[0:ED, o:o + H * SHARE[0] * CHUNK].rearrange("p (u k c) -> p u k c", u=H, c=CHUNK)
        o += H * SHARE[0] * CHUNK
        feat = v.x1[0:C, o:o + BANKS * CHUNK].rearrange("p (k c) -> p k c", k=BANKS)
        o += BANKS * CHUNK
        stats = v.x1[0:C, o:o + 6 * NCHUNK].rearrange("p (n s) -> p n s", s=6)
        pad_row = v.x1[0:1, o + 6 * NCHUNK:o + 6 * NCHUNK + C]
        bn = sb("bn", [P, H, R, 6])
        mom = sb("mom", [P, H, 8, R])
        ps_e = [st.enter_context(nc.psum_tensor(f"ps_e{k}", [P, 512], F32)) for k in range(BANKS)]
        ps_row = st.enter_context(nc.psum_tensor("ps_row", [P, 512], F32))
        ids, consts, weights, weights2, pads, padded = (sem(n) for n in ("ids", "consts", "weights", "weights2", "pads", "padded"))
        x_in = [sem(f"x_in{u}") for u in range(H)]
        h_out = [sem(f"h_out{u}") for u in range(H)]
        attr_in = [sem(f"attr_in{u}") for u in range(H)]
        chain, var_ready, std_ready, rstd_ready, scaled, h_ready, rest_in, rest_out, turn = (sem(n) for n in (
            "chain", "var_ready", "std_ready", "rstd_ready", "scaled", "h_ready", "rest_in", "rest_out", "turn"))
        e_mm, e_relu, e_stat, fold, e_std, c_sum, c_row, moved = (sem(n) for n in (
            "e_mm", "e_relu", "e_stat", "fold", "e_std", "c_sum", "c_row", "moved"))
        xv = v.x[0:main, :].rearrange("(p t) f -> p (t f)", p=P)
        hv = v.h1_tab[0:main, :].rearrange("(p t) f -> p (t f)", p=P)

        def pipe(engine, body):
            body(0)
            body(1)
            with engine.Fori(2, STEPS - 1) as i:
                body(i)
            body(STEPS - 1)

        def before(i, u):
            return None if isinstance(i, int) and i == 0 and u == 0 else (i, u - 1) if u else (i - 1, H - 1)

        def chunks(i, u):
            j0 = sum(SHARE[:u])
            return range(j0, min(j0 + SHARE[u], LEFT if is_last(i, STEPS) else PER))

        with nc.Block() as block:
            @block.sync
            def _(sp):
                for dst, s in ((v.w_cat[0:C, 0:C], v.w_msg[0:C, :]), (v.w_cat[0:C, C:2 * C], v.w_msg[C:2 * C, :]),
                               (v.w_cat[0:C, 2 * C:], v.w_node[:, :]), (v.w_ef[0:C, :], v.w_msg[2 * C:3 * C, :]),
                               (v.w_e[:, :], v.w_edge[:, :]), (v.w_cat[C:A1, 2 * C:], v.b_node.rearrange("(a n) -> a n", a=1)),
                               (v.be, v.b_edge.rearrange("(n a) -> n a", a=1)), (v.ge, v.g_edge.rearrange("(n a) -> n a", a=1)),
                               (v.bte, v.beta_edge.rearrange("(n a) -> n a", a=1)), (v.gn, v.g_node.rearrange("(n a) -> n a", a=1)),
                               (v.btn, v.beta_node.rearrange("(n a) -> n a", a=1)), (v.gm, v.g_msg.rearrange("(n a) -> n a", a=1)),
                               (v.btm, v.beta_msg.rearrange("(n a) -> n a", a=1))):
                    sp.dma_start(dst, s).then_inc(weights, 16)

                def step(i):
                    for u in range(H):
                        g = H * i + u
                        wait(sp, h_ready, g - H + 1)
                        sp.dma_start(xin[:, u, :], xv[:, bass.ds(g * span, span)]).then_inc(x_in[u], 16)
                        cs = chunks(i, u)
                        if len(cs):
                            wait(sp, e_mm, PER * (i - 1) + sum(SHARE[:u + 1]))
                            sp.dma_start(attr[:, u, 0:len(cs), :].rearrange("p k c -> p (k c)"),
                                         v.ea_t[:, bass.ds((PER * i + cs[0]) * CHUNK, len(cs) * CHUNK)]).then_inc(attr_in[u], 16)
                pipe(sp, step)
                sp.wait_ge(h_ready, ROW_GROUPS)
                sp.dma_start(xin[0:REST, 0, 0:C], v.x[main:N, :]).then_inc(rest_in, 16)
                sp.wait_ge(c_row, 1)
                sp.dma_start(v.w_ef[C:A1, :], v.rows4[0:1, 0:C]).then_inc(moved, 16)
                sp.wait_ge(moved, 16)

            @block.gpsimd
            def _(pool):
                pool.memset(v.ident[:, :], 0.0).then_inc(ids, 1)
                pool.memset(v.earlier[:, :], 1.0).then_inc(ids, 1)
                pool.memset(v.ones[:, :], 1.0).then_inc(ids, 1)
                pool.memset(v.eps[:, :], EPS).then_inc(ids, 1)
                pool.iota(v.dump_row[:, :], [[0, 1]], base=DUMP, channel_multiplier=1,
                          allow_small_or_imprecise_dtypes=True).then_inc(ids, 1)
                pool.iota(v.line[:, :], [[1, P]], base=0, channel_multiplier=0,
                          allow_small_or_imprecise_dtypes=True).then_inc(ids, 1)
                pool.wait_ge(ids, 6)
                pool.affine_select(out=v.ident[:, :], in_=v.ident[:, :], compare_op=ALU.not_equal, fill=1.0,
                                   base=0, pattern=[[-1, P]], channel_multiplier=1).then_inc(consts, 1)
                pool.affine_select(out=v.earlier[:, :], in_=v.earlier[:, :], compare_op=ALU.is_gt, fill=0.0,
                                   base=0, pattern=[[-1, P]], channel_multiplier=1).then_inc(consts, 1)
                pool.wait_ge(consts, 2)
                pool.wait_ge(pads, 2)
                pool.dma_start(v.pq_tab[2 * NPAD:2 * NPAD + 1, :], pad_row).then_inc(padded, 16)
                pool.wait_ge(padded, 16)

                def step(i):
                    for u in range(H):
                        g = H * i + u
                        wait(pool, h_ready, g + 1)
                        pool.sem_inc(turn, 1)
                        pool.dma_start(hv[:, bass.ds(g * span, span)], xout[:, u, :]).then_inc(h_out[u], 16)
                loop(pool, STEPS, step)

            @block.vector
            def _(dve):
                dve.memset(v.w_cat[C:A1, 0:2 * C], 0.0).then_inc(pads, 1)
                dve.memset(pad_row, -1e30).then_inc(pads, 1)

                def variance(rows, nrow, u, g, loaded, loads):
                    m = [mom[0:rows, u, k, 0:nrow] for k in range(8)]
                    wait(dve, loaded, loads)
                    wait(dve, h_ready, g - H + 1)
                    for r in range(nrow):
                        op = dve.bn_stats(bn[0:rows, u, r, :], xin[0:rows, u, r * C:(r + 1) * C])
                    op.then_inc(chain, 1)
                    me, se, mo, so = (bn[0:rows, u, 0:nrow, k] for k in (1, 2, 4, 5))
                    wait(dve, chain, 3 * g + 1)
                    dve.tensor_tensor(m[0], me, mo, ALU.add)
                    dve.tensor_tensor(m[1], me, mo, ALU.subtract)
                    dve.tensor_tensor(m[2], se, so, ALU.add).then_inc(chain, 1)
                    wait(dve, chain, 3 * g + 2)
                    dve.scalar_tensor_tensor(m[3], m[1], 0.25, m[1], ALU.mult, ALU.mult).then_inc(chain, 1)
                    wait(dve, chain, 3 * g + 3)
                    dve.scalar_tensor_tensor(m[4], m[2], 1.0 / C, m[3], ALU.mult, ALU.add).then_inc(var_ready, 1)

                def factors(rows, nrow, u, g):
                    m = [mom[0:rows, u, k, 0:nrow] for k in range(8)]
                    wait(dve, std_ready, g + 1)
                    dve.reciprocal(m[6], m[5]).then_inc(rstd_ready, 1)
                    wait(dve, rstd_ready, g + 1)
                    dve.scalar_tensor_tensor(m[7], m[0], -0.5, m[6], ALU.mult, ALU.mult).then_inc(scaled, 1)

                def chunk_stats(i, u):
                    for j in chunks(i, u):
                        wait(dve, e_relu, PER * i + j + 1)
                        dve.bn_stats(stats[:, bass.ds(PER * i + j, 1), :].rearrange("p a s -> p (a s)"),
                                     feat[:, j % BANKS, :]).then_inc(e_stat, 1)

                def step(i):
                    for u in range(H):
                        g = H * i + u
                        variance(P, R, u, g, x_in[u], 16 * (i + 1))
                        if before(i, u):
                            i0, u0 = before(i, u)
                            factors(P, R, u0, H * i0 + u0)
                            chunk_stats(i0, u0)
                pipe(dve, step)
                factors(P, R, H - 1, ROW_GROUPS - 1)
                chunk_stats(STEPS - 1, H - 1)
                variance(REST, 1, 0, ROW_GROUPS, rest_in, 16)
                factors(REST, 1, 0, ROW_GROUPS)
                s = v.small
                dve.wait_ge(e_stat, NCHUNK)
                dve.bn_aggr(s[:, 0:2], stats.rearrange("p n s -> p (n s)")).then_inc(fold, 1)
                dve.wait_ge(e_std, 1)
                dve.reciprocal(s[:, 3:4], s[:, 2:3]).then_inc(fold, 1)
                dve.wait_ge(fold, 2)
                dve.tensor_tensor(s[:, 4:5], s[:, 3:4], v.ge, ALU.mult).then_inc(fold, 1)
                dve.wait_ge(fold, 3)
                dve.tensor_tensor(s[:, 5:6], s[:, 4:5], s[:, 0:1], ALU.mult).then_inc(fold, 1)
                dve.wait_ge(fold, 4)
                dve.tensor_tensor(s[:, 6:7], v.bte, s[:, 5:6], ALU.subtract).then_inc(fold, 1)
                dve.wait_ge(c_sum, 1)
                dve.tensor_scalar(v.w_ef[0:C, :], v.w_ef[0:C, :], s[:, 4:5], None, ALU.mult)
                dve.tensor_tensor(v.rows4[0:1, 0:C], ps_row[0:1, 0:C], v.rows4[0:1, C:2 * C], ALU.add).then_inc(c_row, 1)

            @block.tensor
            def _(pe):
                pe.wait_ge(weights, 16 * 13)

                def step(i):
                    for u in range(H):
                        if len(chunks(i, u)):
                            wait(pe, attr_in[u], 16 * (i + 1))
                        for j in chunks(i, u):
                            wait(pe, e_relu, PER * i + j - BANKS + 1)
                            pe.matmul(ps_e[j % BANKS][0:C, 0:CHUNK], v.w_e[:, :], attr[:, u, j - sum(SHARE[:u]), :],
                                      start=True, stop=True).then_inc(e_mm, 1)
                loop(pe, STEPS, step)
                pe.wait_ge(fold, 5)
                pe.matmul(ps_row[0:1, 0:C], v.small[:, 6:7], v.w_ef[0:C, :], start=True, stop=True).then_inc(c_sum, 1)

            @block.scalar
            def _(act):
                act.dma_start(v.rows4[0:1, C:2 * C], v.b_msg.rearrange("(a n) -> a n", a=1)).then_inc(weights2, 16)
                act.wait_ge(weights, 16 * 13)
                act.wait_ge(weights2, 16)
                act.wait_ge(ids, 6)

                def root(rows, nrow, u, g):
                    wait(act, var_ready, g + 1)
                    act.activation(mom[0:rows, u, 5, 0:nrow], mom[0:rows, u, 4, 0:nrow], ACT.Sqrt,
                                   bias=v.eps[0:rows, :]).then_inc(std_ready, 1)

                def normalise(rows, nrow, u, g, stored, stores):
                    wait(act, scaled, g + 1)
                    wait(act, stored, stores)
                    for r in range(nrow):
                        op = act.activation(xout[0:rows, u, r * C:(r + 1) * C], xin[0:rows, u, r * C:(r + 1) * C], ACT.Relu,
                                            scale=mom[0:rows, u, 6, r:r + 1], bias=mom[0:rows, u, 7, r:r + 1])
                    op.then_inc(h_ready, 1)

                def whole_group(i, u):
                    normalise(P, R, u, H * i + u, h_out[u], 16 * i)

                def step(i):
                    for u in range(H):
                        root(P, R, u, H * i + u)
                        if before(i, u):
                            whole_group(*before(i, u))
                        for j in chunks(i, u):
                            wait(act, e_mm, PER * i + j + 1)
                            wait(act, e_stat, PER * i + j - BANKS + 1)
                            act.activation(feat[:, j % BANKS, :], ps_e[j % BANKS][0:C, 0:CHUNK], ACT.Relu, bias=v.be
                                           ).then_inc(e_relu, 1)
                pipe(act, step)
                whole_group(STEPS - 1, H - 1)
                root(REST, 1, 0, ROW_GROUPS)
                normalise(REST, 1, 0, ROW_GROUPS, h_out[0], 16 * STEPS)
                act.wait_ge(h_ready, ROW_GROUPS + 1)
                act.dma_start(v.h1_tab[main:N, :], xout[0:REST, 0, 0:C]).then_inc(rest_out, 16)
                act.wait_ge(fold, 1)
                act.activation(v.small[:, 2:3], v.small[:, 1:2], ACT.Sqrt, bias=v.eps[0:C, :]).then_inc(e_std, 1)
                for u in range(H):
                    act.wait_ge(h_out[u], 16 * STEPS)
                act.wait_ge(rest_out, 16)


def zero_phase(nc, v):
    BR = 32
    rows = TABLE_ROWS // P
    zero = v.x1[:, 0:BR * A1]
    with nc.semaphore("blank") as blank, nc.semaphore("zeroed") as zeroed:
        with nc.Block() as block:
            @block.vector
            def _(dve):
                dve.memset(zero, 0.0).then_inc(blank, 1)

            @block.sync
            def _(sp):
                sp.wait_ge(blank, 1)
                n = 0
                for tab, wdt in [(s, A1) for s in v.sums] + [(m, C) for m in v.msgs]:
                    for r0 in range(0, rows, BR):
                        r1 = min(r0 + BR, rows)
                        sp.dma_start(tab[r0 * P:r1 * P, :].rearrange("(p r) f -> p (r f)", p=P),
                                     zero[:, 0:(r1 - r0) * wdt]).then_inc(zeroed, 16)
                        n += 1
                    sp.dma_start(tab[rows * P:TABLE_ROWS, :], zero[0:TABLE_ROWS - rows * P, 0:wdt]).then_inc(zeroed, 16)
                    n += 1
                sp.wait_ge(zeroed, 16 * n)


def plan_phase(nc, v):
    NT = EDGE_GROUPS * T
    B = 8
    PER = 5
    STEPS = NT // (B * PER)
    with ExitStack() as st:
        def sem(name):
            return st.enter_context(nc.semaphore(name + "p"))

        def part(dt, lo, n, rows=P):
            t = v.x1[0:rows, lo:lo + n]
            return t if dt == F32 else t.bitcast(dt)

        idx = part(I32, 30000, 4 * NT).rearrange("p (g q k) -> p g q k", q=4, k=T)
        dg, sg, da, db = (part(I32, k * NT, NT) for k in range(4))
        hi, lo, t1, t2 = (part(I32, (4 + k) * NT, NT) for k in range(4))
        hif, lof, up = (part(F32, (10 + k) * NT, NT) for k in range(3))
        BF = mybir.dt.bfloat16
        oh_hi = part(BF, 14 * NT, NT * HI // 2)
        oh_lo = part(BF, 14 * NT + NT * HI // 2, NT * LO // 2)
        base = 14 * NT + NT * (HI + LO) // 2
        cross = part(F32, base, B * LO)
        blocks = part(F32, base + B * LO, B * HI * LO, 1)
        o = base + B * LO + B * HI * LO
        cnt, incl, one, sc = part(F32, o, 416, 1), part(F32, o + 416, 416, 1), part(F32, o + 832, 416, 1), part(F32, o + 1248, 8, 1)
        ups = part(F32, o + 1256, 1)
        bound, over = part(F32, o + 1264, NWIN, 1), part(F32, o + 1264 + NWIN, NWIN, 1)
        ps = st.enter_context(nc.psum_tensor("ps_plan", [P, 512], F32))
        ps1 = st.enter_context(nc.psum_tensor("ps_plan1", [P, 512], F32))
        bounded = sem("bounded")
        loaded, chain, hot, crossed, moved, summed, stored = (sem(n) for n in ("loaded", "chain", "hot", "crossed", "moved", "summed", "stored"))
        with nc.Block() as block:
            @block.gpsimd
            def _(pool):
                pool.iota(bound, [[STEP_EDGES, NWIN // (2 * W)], [0, 2 * W]], base=2 * STEP_EDGES - SLOTS * WP_E,
                          channel_multiplier=0, allow_small_or_imprecise_dtypes=True).then_inc(bounded, 1)

            @block.sync
            def _(sp):
                sp.dma_start(dg, v.dst_g).then_inc(loaded, 16)
                sp.dma_start(sg, v.src_g).then_inc(loaded, 16)
                sp.dma_start(da, v.dst_line[:, 0:EPAD].rearrange("a (p c) -> (a p) c", p=P)).then_inc(loaded, 16)
                sp.dma_start(db, v.dst_line[:, 1:EPAD + 1].rearrange("a (p c) -> (a p) c", p=P)).then_inc(loaded, 16)
                sp.wait_ge(crossed, 1)
                for k in range(B):
                    sp.dma_start(blocks[:, k * HI * LO:(k + 1) * HI * LO],
                                 cross[k * HI:(k + 1) * HI, k * LO:(k + 1) * LO]).then_inc(moved, 16)
                sp.wait_ge(stored, 16)

            @block.scalar
            def _(act):
                act.wait_ge(chain, 13)
                act.dma_start(v.edge_idx, idx.rearrange("p g q k -> p (g q k)")).then_inc(stored, 16)
                act.wait_ge(stored, 16)

            @block.vector
            def _(dve):
                n = [0]

                def link(ins):
                    n[0] += 1
                    ins.then_inc(chain, 1)
                    dve.wait_ge(chain, n[0])

                dve.wait_ge(loaded, 64)
                shr, shl, band = ALU.arith_shift_right, ALU.logical_shift_left, ALU.bitwise_and
                dve.tensor_scalar(hi, dg, 12, None, shr)
                link(dve.tensor_scalar(lo, dg, 7, LO - 1, shr, band))
                dve.tensor_copy(hif, hi)
                link(dve.tensor_copy(lof, lo))
                dve.tensor_tensor(oh_hi.rearrange("p (t a) -> p t a", a=HI), hif.unsqueeze(2).to_broadcast([P, NT, HI]),
                                  v.line[:, 0:HI].unsqueeze(1).to_broadcast([P, NT, HI]), ALU.is_equal)
                dve.tensor_tensor(oh_lo.rearrange("p (t a) -> p t a", a=LO), lof.unsqueeze(2).to_broadcast([P, NT, LO]),
                                  v.line[:, 0:LO].unsqueeze(1).to_broadcast([P, NT, LO]), ALU.is_equal).then_inc(hot, 1)
                dve.wait_ge(hot, 1)
                dve.tensor_copy(hif, da)
                link(dve.tensor_copy(lof, db))
                link(dve.tensor_tensor(up, hif, lof, ALU.is_gt))
                dve.tensor_reduce(ups, up, AXX, ALU.add).then_inc(hot, 1)
                def by_group(a):
                    return a.rearrange("p (g k) -> p g k", k=T)
                dve.tensor_copy(idx[:, :, 0, :], by_group(sg))
                dve.tensor_copy(idx[:, :, 1, :], by_group(dg))
                for a, out_ in ((sg, idx[:, :, 2, :]), (dg, idx[:, :, 3, :])):
                    dve.tensor_scalar(t1, a, P - 1, 2, band, shl)
                    link(dve.tensor_scalar(t2, a, 7, W - 1, shr, band))
                    link(dve.tensor_tensor(t1, t1, t2, ALU.add))
                    link(dve.tensor_scalar(t2, a, 9, 9, shr, shl))
                    if a is dg:
                        link(dve.tensor_scalar(t2, t2, NPAD, None, ALU.add))
                    link(dve.tensor_tensor(out_, by_group(t1), by_group(t2), ALU.add))
                assert n[0] == 13
                link(dve.memset(one, 1.0))
                dve.wait_ge(summed, 1)
                link(dve.tensor_copy(cross[0:B * HI, :], ps[0:B * HI, 0:B * LO]))
                dve.sem_inc(crossed, 1)
                dve.wait_ge(moved, 16 * B)
                link(dve.tensor_reduce(cnt, blocks.rearrange("o (k c) -> o c k", k=B), AXX, ALU.add))
                link(dve.tensor_tensor_scan(incl, one, cnt, 0.0, ALU.mult, ALU.add))
                dve.memset(v.starts[:, 0:1], 0)
                dve.tensor_copy(v.starts[:, 1:NWIN + 1], incl[:, 0:NWIN])
                link(dve.tensor_reduce(sc[:, 0:1], cnt[:, 0:NWIN], AXX, ALU.max))
                dve.wait_ge(summed, 2)
                dve.wait_ge(bounded, 1)
                link(dve.tensor_tensor(over[:, 1:NWIN], incl[:, 0:NWIN - 1], bound[:, 1:NWIN], ALU.is_gt))
                link(dve.tensor_reduce(sc[:, 3:4], over[:, 1:NWIN], AXX, ALU.max))
                dve.tensor_scalar(sc[:, 4:5], sc[:, 3:4], 0.0, None, ALU.is_equal)
                dve.tensor_scalar(sc[:, 1:2], sc[:, 0:1], float(SLOTS * WP_E), None, ALU.is_le)
                link(dve.tensor_scalar(sc[:, 2:3], ps1[0:1, 0:1], 0.0, None, ALU.is_equal))
                link(dve.tensor_tensor(sc[:, 5:6], sc[:, 1:2], sc[:, 2:3], ALU.mult))
                link(dve.tensor_tensor(v.flag[:, :], sc[:, 5:6], sc[:, 4:5], ALU.mult))

            @block.tensor
            def _(pe):
                pe.wait_ge(hot, 1)

                def step(i):
                    for q in range(PER):
                        m = pe.matmul(ps[0:B * HI, 0:B * LO], oh_hi[:, bass.ds((i * PER + q) * B * HI, B * HI)],
                                      oh_lo[:, bass.ds((i * PER + q) * B * LO, B * LO)],
                                      start=isinstance(i, int) and i == 0 and q == 0,
                                      stop=is_last(i, STEPS) and q == PER - 1, skip_group_check=True)
                    if is_last(i, STEPS):
                        m.then_inc(summed, 1)
                loop(pe, STEPS, step)
                pe.wait_ge(hot, 2)
                pe.matmul(ps1[0:1, 0:1], ups, v.ones[:, 0:1], start=True, stop=True).then_inc(summed, 1)


class Messages:

    def __init__(self, nc, v, st, got, gotq, msg, gathered, msg_free):
        def sb(name, shape):
            return st.enter_context(nc.sbuf_tensor(name + "m" + v.tag, shape, F32))

        def sem(name):
            return st.enter_context(nc.semaphore(name + "m" + v.tag))

        def bank(name, n=1):
            return st.enter_context(nc.psum_tensor(name + "m" + v.tag, [P, n * 512], F32))
        self.v, self.got, self.gotq, self.msg, self.gathered = v, got, gotq, msg, gathered
        self.msg_free = msg_free
        self.HB = T // 4
        self.ea, self.ef = sb("ea", [ED, 2, T * P]), sb("ef", [A1, T * P])
        self.ps_ef, self.ps_msg, self.ps_gram = bank("ps_ef", self.HB), bank("ps_msg", self.HB), bank("ps_gram")
        self.ea_in = [sem(f"ea_in{u}") for u in range(2)]
        self.ef_mm, self.ef_relu, self.msg_mm, self.with_p, self.with_q, self.ready, self.gram_done, self.ones, self.out = (
            sem(n) for n in ("ef_mm", "ef_relu", "msg_mm", "with_p", "with_q", "ready", "gram_done", "ones", "out"))

    def start(self, dve):
        return dve.memset(self.ef[C:A1, :], 1.0)

    def load(self, sp, g, u):
        wait(sp, self.ef_mm, self.HB * (g - 1))
        sp.dma_start(self.ea[:, u, :], self.v.ea_g[:, bass.ds(g * T * P, T * P)]).then_inc(self.ea_in[u], 16)

    def edge_part(self, pe, i, u):
        g, HB = 2 * i + u, self.HB
        wait(pe, self.ea_in[u], 16 * (i + 1))
        for h in range(HB):
            wait(pe, self.ef_relu, HB * (g - 1) + h + 1)
            pe.matmul(self.ps_ef[0:C, h * 512:h * 512 + 512], self.v.w_e[:, :], self.ea[:, u, h * 512:h * 512 + 512],
                      start=True, stop=True).then_inc(self.ef_mm, 1)

    def message_part(self, pe, g):
        HB = self.HB
        for k in range(T):
            h = k // 4
            if k % 4 == 0:
                wait(pe, self.ef_relu, HB * g + h + 1)
                wait(pe, self.with_p, HB * (g - 1) + h + 1)
            c0 = h * 512 + (k % 4) * C
            m = pe.matmul(self.ps_msg[:, c0:c0 + C], self.ef[:, k * P:(k + 1) * P], self.v.w_ef[:, :], start=True, stop=True)
            if k % 4 == 3:
                m.then_inc(self.msg_mm, 1)

    def gram(self, pe, i, u, k):
        first = isinstance(i, int) and i == 0 and u == 0 and k == 0
        end = is_last(i, EDGE_GROUPS // 2) and u == 1 and k == T - 1
        m = pe.matmul(self.ps_gram[0:C, 0:A1], self.msg(u, k, 0, C), self.msg(u, k, 0, A1), start=first, stop=end,
                      skip_group_check=True)
        if k == T - 1:
            m.then_inc(self.gram_done, 1)

    def edge_relu(self, act, g):
        HB = self.HB
        for h in range(HB):
            wait(act, self.ef_mm, HB * g + h + 1)
            wait(act, self.msg_mm, HB * (g - 1) + h + 1)
            act.activation(self.ef[0:C, h * 512:h * 512 + 512], self.ps_ef[0:C, h * 512:h * 512 + 512], ACT.Relu,
                           bias=self.v.be).then_inc(self.ef_relu, 1)

    def add_parts(self, dve, i, u):
        g, HB = 2 * i + u, self.HB
        wait(dve, self.gathered[u], 32 * T * (i + 1))
        for h in range(HB):
            ks = slice(4 * h, 4 * h + 4)
            wait(dve, self.msg_mm, HB * g + h + 1)
            dve.tensor_tensor(self.got[:, u, ks, 0:C], self.got[:, u, ks, 0:C],
                              self.ps_msg[:, h * 512:h * 512 + 4 * C].rearrange("p (k c) -> p k c", k=4), ALU.add).then_inc(self.with_p, 1)
            wait(dve, self.with_p, HB * g + h + 1)
            dve.tensor_tensor(self.got[:, u, ks, 0:C], self.got[:, u, ks, 0:C], self.gotq[:, u, ks, :], ALU.add).then_inc(self.with_q, 1)

    def message_relu(self, act, g, u):
        for h in range(self.HB):
            wait(act, self.with_q, self.HB * g + h + 1)
            self.msg_free(act, g)
            act.activation(self.msg(u, slice(4 * h, 4 * h + 4), 0, C), self.got[:, u, 4 * h:4 * h + 4, 0:C],
                           ACT.Relu).then_inc(self.ready, 1)

    def finish_dve(self, dve):
        dve.wait_ge(self.gram_done, EDGE_GROUPS)
        dve.tensor_copy(self.v.grams[:, 1, :], self.ps_gram[0:C, 0:A1]).then_inc(self.out, 1)
        dve.wait_ge(self.out, 1)


class SortedEdges:

    def __init__(self, nc, v, st, second):
        def sb(name, shape, dt=F32):
            return st.enter_context(nc.sbuf_tensor(name + tag, shape, dt))

        def sem(name):
            return st.enter_context(nc.semaphore(name + tag))
        tag = "g2" if second else "g1"
        H = 2
        self.v, self.second = v, second
        self.idx = sb("idx", [P, H, 4, T], I32)
        self.got = sb("got", [P, H, T, C if second else ROW])
        self.gotq = sb("gotq", [P, H, T, C]) if second else None
        self.rows = sb("rows", [P, H, T, ROW]) if second else self.got
        self.idx_in = [sem(f"idx_in{u}") for u in range(H)]
        self.gathered = [sem(f"gathered{u}") for u in range(H)]
        self.stored = [sem(f"rows_stored{u}") for u in range(H)]
        self.dst_set, self.turn, self.sp_turn = sem("dst_set"), sem("gather_turn"), sem("load_turn")
        self.table = v.pq_tab if second else v.h1_tab
        self.columns = (2, 3) if second else (0,)
        self.NI = len(self.columns)
        if second:
            self.m = Messages(nc, v, st, self.got, self.gotq, lambda u, k, c0, c1: self.rows[:, u, k, c0:c1], self.gathered,
                              lambda act, g: wait(act, self.m.gram_done, g - 1))

    def start(self, dve):
        if self.second:
            self.m.start(dve)
        for u in range(2):
            dve.memset(self.rows[:, u, :, C:A1], 1.0)

    def load(self, sp_wait, sp, j, u):
        g = 2 * j + u
        sp_wait(self.gathered[u], 16 * self.NI * T * j)
        sp_wait(self.dst_set, g - 1)
        sp.dma_start(self.idx[:, u, :, :].rearrange("p q k -> p (q k)"), self.v.edge_idx[:, bass.ds(g * 4 * T, 4 * T)]
                     ).then_inc(self.idx_in[u], 16)
        if self.second:
            m = self.m
            m.load(sp, g, u)
            sp.sem_inc(self.sp_turn, 1)

    def store(self, sp_wait, sp, j, u):
        g = 2 * j + u
        sp_wait(self.dst_set, g + 1)
        if self.second:
            sp_wait(self.m.ready, self.m.HB * (g + 1))
        else:
            sp_wait(self.gathered[u], 16 * T * (j + 1))
        sp.dma_start(self.v.edge_rows[bass.ds(g * T * P, T * P), :].rearrange("(p k) c -> p (k c)", p=P),
                     self.rows[:, u, :, :].rearrange("p k c -> p (k c)")).then_inc(self.stored[u], 16)

    def gather(self, pool, j, u):
        wait(pool, self.idx_in[u], 16 * (j + 1))
        if self.second:
            wait(pool, self.m.ready, self.m.HB * (2 * j + u - 1))
        else:
            wait(pool, self.stored[u], 16 * j)
        pool.sem_inc(self.turn, 1)
        for k in range(T):
            for t, q in enumerate(self.columns):
                pool.indirect_dma_start((self.gotq if t else self.got)[:, u, k, 0:C], None, self.table[:, :],
                                        bass.IndirectOffsetOnAxis(ap=self.idx[:, u, q, k:k + 1], axis=0)).then_inc(self.gathered[u], 16)

    def set_dst(self, dve, j, u):
        wait(dve, self.idx_in[u], 16 * (j + 1))
        wait(dve, self.stored[u], 16 * j)
        dve.tensor_copy(self.rows[:, u, :, A1], self.idx[:, u, 1, :]).then_inc(self.dst_set, 1)
        if self.second:
            self.m.add_parts(dve, j, u)

    def products(self, pe, j, u):
        self.m.message_part(pe, 2 * j + u)

    def gram(self, pe, j, u):
        for k in range(T):
            if k % 4 == 0:
                wait(pe, self.m.ready, self.m.HB * (2 * j + u) + k // 4 + 1)
            self.m.gram(pe, j, u, k)

    def relus(self, act, j, u):
        wait(act, self.stored[u], 16 * j)
        self.m.message_relu(act, 2 * j + u, u)


def scatter_phase(nc, v, second):
    H = 2
    STEPS = EDGE_GROUPS // H
    width = C if second else A1
    tables = v.msgs if second else v.sums
    tag = "b" if second else "a"
    HB = T // 4
    with ExitStack() as st:
        def sb(name, shape, dt=F32):
            return st.enter_context(nc.sbuf_tensor(name + tag, shape, dt))

        def sem(name):
            return st.enter_context(nc.semaphore(name + tag))

        def bank(name, n=1):
            return st.enter_context(nc.psum_tensor(name + tag, [P, n * 512], F32))

        idx = sb("idx", [P, H, 4, T], I32)
        rows = sb("rows", [P, H, T], I32)
        dstf, cnt, away = (sb(n, [P, H, T]) for n in ("dstf", "cnt", "away"))
        scrap = sb("scrap", [P, P])
        if second:
            dst_rows = sb("dst_rows", [P, 1, T * P], I32)
            same = sb("same", [P, 1, T, P])
            got = sb("got", [P, H, T, C])
            gotq = sb("gotq", [P, H, T, C])
            msg = sb("msg", [P, 1, T, A1])
            tot = sb("tot", [P, H, T, C])
            BH = 1
        else:
            dst_rows = sb("dst_rows", [P, H, T * P], I32)
            free = v.x1[:, :]
            o = H * T * P
            same = free[:, 0:o].rearrange("p (u k c) -> p u k c", u=H, k=T)
            got = free[:, o:o + H * T * A1].rearrange("p (u k c) -> p u k c", u=H, k=T)
            tot = free[:, 2 * o:2 * o + H * T * A1].rearrange("p (u k c) -> p u k c", u=H, k=T)
            BH = H
        ps_tot = bank("ps_tot", HB)
        idx_in = [sem(f"idx_in{u}") for u in range(H)]
        marks_in = [sem(f"marks_in{u}") for u in range(H)]
        gathered = [sem(f"gathered{u}") for u in range(H)]
        added = [sem(f"added{a}") for a in range(NACC)]
        floats, marked, differ, masked, rows_ready = (sem(n) for n in ("floats", "marked", "differ", "masked", "rows_ready"))
        totals, copied, turn, ready = (sem(n) for n in ("totals", "copied", "turn", "ready"))
        if second:
            m = Messages(nc, v, st, got, gotq, lambda u, k, c0, c1: msg[:, 0, k, c0:c1], gathered,
                         lambda act, g: wait(act, m.gram_done, g))

        def bu(u):
            return u % BH

        with nc.Block() as block:
            @block.sync
            def _(sp):
                def step(i):
                    for u in range(H):
                        g = H * i + u
                        wait(sp, gathered[u], (32 if second else 16) * T * i)
                        wait(sp, rows_ready, g - 1)
                        sp.dma_start(idx[:, u, :, :].rearrange("p q k -> p (q k)"), v.edge_idx[:, bass.ds(g * 4 * T, 4 * T)]
                                     ).then_inc(idx_in[u], 16)
                        wait(sp, marked, g - BH + 1)
                        sp.dma_start(dst_rows[:, bu(u), :], v.dst_row[:, bass.ds(g * T * P, T * P)]
                                     .to_broadcast([P, T * P])).then_inc(marks_in[u], 16)
                        if second:
                            m.load(sp, g, u)
                loop(sp, STEPS, step)

            @block.gpsimd
            def _(pool):
                def gather(i, u):
                    g = H * i + u
                    wait(pool, idx_in[u], 16 * (i + 1))
                    wait(pool, m.ready if second else totals, (g - 1) * HB)
                    pool.sem_inc(turn, 1)
                    for k in range(T):
                        pool.indirect_dma_start(got[:, u, k, 0:C], None, (v.pq_tab if second else v.h1_tab)[:, :],
                                                bass.IndirectOffsetOnAxis(ap=idx[:, u, 2 if second else 0, k:k + 1], axis=0)
                                                ).then_inc(gathered[u], 16)
                        if second:
                            pool.indirect_dma_start(gotq[:, u, k, :], None, v.pq_tab[:, :],
                                                    bass.IndirectOffsetOnAxis(ap=idx[:, u, 3, k:k + 1], axis=0)
                                                    ).then_inc(gathered[u], 16)

                def scatter(i, u):
                    g = H * i + u
                    wait(pool, rows_ready, g + 1)
                    for k in range(T):
                        if k % 4 == 0:
                            wait(pool, copied, HB * g + k // 4 + 1)
                        wait(pool, added[k % NACC], g * (16 * T // NACC) + 16 * (k // NACC))
                        pool.sem_inc(turn, 1)
                        pool.indirect_dma_start(tables[k % NACC][:, :],
                                                bass.IndirectOffsetOnAxis(ap=rows[:, u, k:k + 1], axis=0),
                                                tot[:, u, k, :], None, compute_op=ALU.add).then_inc(added[k % NACC], 16)
                gather(0, 0)

                def step(i):
                    gather(i, 1)
                    scatter(i, 0)
                    if not is_last(i, STEPS):
                        gather(i + 1, 0)
                    scatter(i, 1)
                loop(pool, STEPS, step)
                for a in range(NACC):
                    pool.wait_ge(added[a], 16 * EDGE_GROUPS * T // NACC)

            @block.vector
            def _(dve):
                if second:
                    m.start(dve)
                    dve.memset(msg[:, 0, :, C:A1], 1.0).then_inc(ready, 1)
                else:
                    for u in range(H):
                        dve.memset(got[:, u, :, C:A1], 1.0).then_inc(ready, 1)

                def step(i):
                    for u in range(H):
                        g = H * i + u
                        wait(dve, idx_in[u], 16 * (i + 1))
                        dve.tensor_copy(dstf[:, u, :], idx[:, u, 1, :]).then_inc(floats, 1)
                        wait(dve, floats, g + 1)
                        wait(dve, marks_in[u], 16 * (i + 1))
                        wait(dve, totals, HB * (g - BH + 1))
                        if second:
                            wait(dve, m.gram_done, g)
                        for k in range(T):
                            line = dst_rows[:, bu(u), k * P:(k + 1) * P]
                            dve.tensor_scalar(same[:, bu(u), k, :], line, dstf[:, u, k:k + 1], None, ALU.is_equal)
                            dve.scalar_tensor_tensor(scrap[:, :], line, dstf[:, u, k:k + 1], v.earlier[:, :],
                                                     ALU.is_equal, ALU.mult, accum_out=cnt[:, u, k:k + 1])
                            last = dve.drain()
                        last.then_inc(marked, 1)
                        wait(dve, marked, g + 1)
                        dve.tensor_scalar(cnt[:, u, :], cnt[:, u, :], 1.0, None, ALU.min)
                        dve.tensor_scalar(away[:, u, :], dstf[:, u, :], -1.0, v.dump_row[:, :], ALU.mult, ALU.add).then_inc(differ, 1)
                        wait(dve, differ, g + 1)
                        dve.tensor_tensor(away[:, u, :], away[:, u, :], cnt[:, u, :], ALU.mult).then_inc(masked, 1)
                        wait(dve, masked, g + 1)
                        for a in range(NACC):
                            wait(dve, added[a], (g - 1) * (16 * T // NACC))
                        dve.tensor_tensor(rows[:, u, :], away[:, u, :], dstf[:, u, :], ALU.add).then_inc(rows_ready, 1)
                        if second:
                            m.add_parts(dve, i, u)
                        for h in range(HB):
                            wait(dve, totals, HB * g + h + 1)
                            dve.tensor_copy(tot[:, u, 4 * h:4 * h + 4, :],
                                            ps_tot[:, h * 512:h * 512 + 4 * width].rearrange("p (k c) -> p k c", k=4)
                                            ).then_inc(copied, 1)
                loop(dve, STEPS, step)
                if second:
                    m.finish_dve(dve)

            @block.tensor
            def _(pe):
                pe.wait_ge(ready, 1 if second else H)

                def step(i):
                    for u in range(H):
                        g = H * i + u
                        if second:
                            m.edge_part(pe, i, u)
                            m.message_part(pe, g)
                        wait(pe, marked, g + 1)
                        if not second:
                            wait(pe, gathered[u], 16 * T * (i + 1))
                        for k in range(T):
                            h = k // 4
                            if k % 4 == 0:
                                wait(pe, copied, HB * (g - 1) + h + 1)
                                if second:
                                    wait(pe, m.ready, HB * g + h + 1)
                            c0 = h * 512 + (k % 4) * width
                            t = pe.matmul(ps_tot[:, c0:c0 + width], same[:, bu(u), k, :],
                                          msg[:, 0, k, 0:C] if second else got[:, u, k, :], start=True, stop=True)
                            if k % 4 == 3:
                                t.then_inc(totals, 1)
                        if second:
                            for k in range(T):
                                m.gram(pe, i, u, k)
                loop(pe, STEPS, step)

            @block.scalar
            def _(act):
                if second:
                    act.wait_ge(ready, 1)

                def step(i):
                    for u in range(H):
                        m.edge_relu(act, H * i + u)
                        m.message_relu(act, H * i + u, u)
                if second:
                    loop(act, STEPS, step)


def scattered_node_phase(nc, v, last):
    H = 2
    STEPS = NODE_GROUPS // H
    width = C if last else A1
    tables = v.msgs if last else v.sums
    tag = "d" if last else "c"
    WP = W * P
    with ExitStack() as st:
        def sb(name, shape, dt=F32):
            return st.enter_context(nc.sbuf_tensor(name + tag, shape, dt))

        def sem(name):
            return st.enter_context(nc.semaphore(name + tag))

        def bank(name, n=1):
            return st.enter_context(nc.psum_tensor(name + tag, [P, n * 512], F32))

        xs = sb("xs", [P, H, W, C])
        sa, sb_ = sb("sa", [P, H, W, width]), sb("sb", [P, H, W, width])
        xn = sb("xn", [P, H, W, C])
        ht = sb("ht", [A1, H, WP])
        ps_t, ps_o = bank("ps_t", H), bank("ps_o", H if last else W)
        mine = sb("mine", [P, H, 3 * W])
        y = sb("y", [P, H, W, C if last else A1])
        if last:
            fin = sb("fin", [P, H, W, C])
        else:
            pq = sb("pq", [P, H, W, 2 * C])
            bn, mom = sb("bn", [P, H, W, 6]), sb("mom", [P, H, 8, W])
            ps_gram = bank("ps_gram")
        names = ("chain", "xn_ready", "t_mm", "ht_ready", "o_mm", "y_ready", "gram_done", "kept_it", "turn",
                 "var_ready", "std_ready", "x1_ready", "scaled", "y_scaled", "fin_ready", "pq_ready", "took", "ready", "pool_chain")
        (chain, xn_ready, t_mm, ht_ready, o_mm, y_ready, gram_done, kept_it, turn, var_ready, std_ready, x1_ready,
         scaled, y_scaled, fin_ready, pq_ready, took, ready, pool_chain) = (sem(n) for n in names)
        loaded = [sem(f"loaded{u}") for u in range(H)]
        stored = [sem(f"stored{u}") for u in range(H)]
        xw = v.x[0:FULL_WIN * P, :].rearrange("(w p) f -> p w f", p=P)
        tw = [t[0:NPAD, :].rearrange("(w p) f -> p w f", p=P) for t in tables]
        LOADS = 16 * (3 if last else 4)
        LAST_LOADS = LOADS + (0 if last else 3 * 16)

        def bias_rows(u):
            return ht[C:A1, u, :]

        with nc.Block() as block:
            @block.sync
            def _(sp):
                def step(i):
                    for u in range(H):
                        g = H * i + u
                        wait(sp, fin_ready if last else x1_ready, g - 1)
                        wait(sp, o_mm, g - 1)
                        if not last:
                            if is_last(i, STEPS) and u == H - 1:
                                k = FULL_WIN - W * g
                                wait(sp, kept_it, g - 1)
                                sp.dma_start(xs[:, u, 0:k, :], xw[:, FULL_WIN - k:FULL_WIN, :]).then_inc(loaded[u], 16)
                                sp.dma_start(xs[0:REST, u, k, :], v.x[FULL_WIN * P:N, :]).then_inc(loaded[u], 16)
                                sp.dma_start(xs[REST:P, u, k, :], v.sums[0][N:(FULL_WIN + 1) * P, 0:C]).then_inc(loaded[u], 16)
                                sp.dma_start(xs[:, u, k + 1:W, :], tw[0][:, FULL_WIN + 1:NWIN, 0:C]).then_inc(loaded[u], 16)
                                assert k + 2 == W
                            else:
                                wait(sp, kept_it, g - 1)
                                sp.dma_start(xs[:, u, :, :], xw[:, bass.ds(W * g, W), :]).then_inc(loaded[u], 16)
                        for s, t in ((sa, tw[0]), (sb_, tw[1])):
                            sp.dma_start(s[:, u, :, :], t[:, bass.ds(W * g, W), :]).then_inc(loaded[u], 16)
                        sp.dma_start(bias_rows(u), v.valid[:, bass.ds(g * WP, WP)]).then_inc(loaded[u], 16)
                loop(sp, STEPS, step)

            @block.gpsimd
            def _(pool):
                def step(i):
                    for u in range(H):
                        g = H * i + u
                        if last:
                            wait(pool, fin_ready, g - 1)
                            pool.sem_inc(turn, 1)
                            pool.tensor_copy(xs[:, u, :, :].rearrange("p w c -> p (w c)"), v.x1[:, bass.ds(g * W * C, W * C)])
                            pool.tensor_copy(mine[:, u, :], v.kept[:, bass.ds(g, 1), :].rearrange("p a c -> p (a c)")).then_inc(took, 1)
                            wait(pool, y_ready, g + 1)
                            a_node = v.rows4[:, 0:C].unsqueeze(1).to_broadcast([P, W, C])
                            pool.tensor_tensor(y[:, u, :, :], y[:, u, :, :], a_node, ALU.mult).then_inc(pool_chain, 1)
                            wait(pool, pool_chain, 2 * g + 1)
                            pool.tensor_tensor(y[:, u, :, :], y[:, u, :, :], xs[:, u, :, :], ALU.add).then_inc(pool_chain, 1)
                            wait(pool, pool_chain, 2 * g + 2)
                            pool.sem_inc(y_scaled, 1)
                        else:
                            wait(pool, xn_ready, g + 1)
                            pool.sem_inc(turn, 1)
                            pool.tensor_copy(v.x1[:, bass.ds(g * W * C, W * C)], xs[:, u, :, :].rearrange("p w c -> p (w c)"))
                            pool.tensor_copy(v.kept[:, bass.ds(g, 1), :].rearrange("p a c -> p (a c)"), mine[:, u, :]).then_inc(kept_it, 1)
                loop(pool, STEPS, step)

            @block.vector
            def _(dve):
                if not last:
                    for u in range(H):
                        dve.memset(y[:, u, :, C:A1], 1.0).then_inc(ready, 1)

                def make_x1(i, u, g):
                    m = [mom[:, u, k, :] for k in range(8)]
                    rstd, shift, dg = (mine[:, u, k * W:(k + 1) * W] for k in range(3))
                    wait(dve, kept_it, g - 1)
                    dve.tensor_tensor(sa[:, u, :, :], sa[:, u, :, :], sb_[:, u, :, :], ALU.add).then_inc(chain, 1)
                    wait(dve, chain, 7 * g + 1)
                    dve.tensor_copy(dg, sa[:, u, :, C])
                    dve.tensor_scalar(m[0], sa[:, u, :, C], 1.0, None, ALU.max).then_inc(chain, 1)
                    wait(dve, chain, 7 * g + 2)
                    dve.reciprocal(m[1], m[0]).then_inc(chain, 1)
                    wait(dve, chain, 7 * g + 3)
                    for w in range(W):
                        last_ = dve.scalar_tensor_tensor(xs[:, u, w, :], sa[:, u, w, 0:C], m[1][:, w:w + 1], xs[:, u, w, :],
                                                         ALU.mult, ALU.add)
                    last_.then_inc(x1_ready, 1)
                    wait(dve, x1_ready, g + 1)
                    for w in range(W):
                        last_ = dve.bn_stats(bn[:, u, w, :], xs[:, u, w, :])
                    last_.then_inc(chain, 1)
                    wait(dve, chain, 7 * g + 4)
                    me, se, mo, so = (bn[:, u, :, k] for k in (1, 2, 4, 5))
                    dve.tensor_tensor(m[2], me, mo, ALU.add)
                    dve.tensor_tensor(m[3], me, mo, ALU.subtract)
                    dve.tensor_tensor(m[4], se, so, ALU.add).then_inc(chain, 1)
                    wait(dve, chain, 7 * g + 5)
                    dve.scalar_tensor_tensor(m[5], m[3], 0.25, m[3], ALU.mult, ALU.mult).then_inc(chain, 1)
                    wait(dve, chain, 7 * g + 6)
                    dve.scalar_tensor_tensor(m[6], m[4], 1.0 / C, m[5], ALU.mult, ALU.add).then_inc(var_ready, 1)
                    wait(dve, std_ready, g + 1)
                    dve.reciprocal(rstd, m[7]).then_inc(chain, 1)
                    wait(dve, chain, 7 * g + 7)
                    dve.scalar_tensor_tensor(shift, m[2], -0.5, rstd, ALU.mult, ALU.mult).then_inc(scaled, 1)
                    wait(dve, scaled, g + 1)

                def step(i):
                    for u in range(H):
                        g = H * i + u
                        wait(dve, loaded[u], LAST_LOADS + LOADS * i if is_last(i, STEPS) and u == H - 1 else LOADS * (i + 1))
                        if last:
                            wait(dve, took, g + 1)
                        else:
                            make_x1(i, u, g)
                        wait(dve, t_mm, g - 1)
                        for w in range(W):
                            last_ = dve.tensor_scalar(xn[:, u, w, :], xs[:, u, w, :], mine[:, u, w:w + 1],
                                                      mine[:, u, W + w:W + w + 1], ALU.mult, ALU.add)
                        last_.then_inc(xn_ready, 1)
                        if last:
                            c_node, a_msg, c_msg = (v.rows4[:, k * C:(k + 1) * C] for k in (1, 2, 3))
                            wait(dve, stored[u], 16 * i)
                            dve.tensor_tensor(sa[:, u, :, :], sa[:, u, :, :], sb_[:, u, :, :], ALU.add).then_inc(chain, 1)
                            wait(dve, chain, 4 * g + 1)
                            dve.tensor_tensor(sa[:, u, :, :], sa[:, u, :, :], a_msg.unsqueeze(1).to_broadcast([P, W, C]),
                                              ALU.mult).then_inc(chain, 1)
                            wait(dve, chain, 4 * g + 2)
                            for w in range(W):
                                last_ = dve.scalar_tensor_tensor(sa[:, u, w, :], c_msg, mine[:, u, 2 * W + w:2 * W + w + 1],
                                                                 sa[:, u, w, :], ALU.mult, ALU.add)
                            last_.then_inc(chain, 1)
                            wait(dve, chain, 4 * g + 3)
                            dve.tensor_tensor(sa[:, u, :, :], sa[:, u, :, :], c_node.unsqueeze(1).to_broadcast([P, W, C]),
                                              ALU.add).then_inc(chain, 1)
                            wait(dve, chain, 4 * g + 4)
                            wait(dve, y_scaled, g + 1)
                            dve.tensor_tensor(fin[:, u, :, :], sa[:, u, :, :], y[:, u, :, :], ALU.add).then_inc(fin_ready, 1)
                loop(dve, STEPS, step)
                if not last:
                    dve.wait_ge(gram_done, NODE_GROUPS)
                    dve.tensor_copy(v.grams[:, 0, :], ps_gram[0:C, 0:A1]).then_inc(ready, 1)
                    dve.wait_ge(ready, H + 1)

            @block.tensor
            def _(pe):
                if not last:
                    pe.wait_ge(ready, H)

                def step(i):
                    for u in range(H):
                        g = H * i + u
                        wait(pe, xn_ready, g + 1)
                        wait(pe, ht_ready, g - 1)
                        for w in range(W):
                            m = pe.transpose(ps_t[0:C, u * 512 + w * P:u * 512 + (w + 1) * P], xn[:, u, w, :], v.ident[:, :])
                        m.then_inc(t_mm, 1)
                        wait(pe, ht_ready, g + 1)
                        wait(pe, loaded[u], LAST_LOADS + LOADS * i if is_last(i, STEPS) and u == H - 1 else LOADS * (i + 1))
                        if last:
                            wait(pe, y_ready, g - 1)
                            for w in range(W):
                                m = pe.matmul(ps_o[:, u * 512 + w * C:u * 512 + (w + 1) * C], ht[:, u, w * P:(w + 1) * P],
                                              v.w_cat[:, 2 * C:], start=True, stop=True)
                            m.then_inc(o_mm, 1)
                        else:
                            wait(pe, y_ready, g)
                            for w in range(W):
                                m = pe.matmul(ps_o[:, w * 512:w * 512 + 3 * C], ht[:, u, w * P:(w + 1) * P], v.w_cat[:, :],
                                              start=True, stop=True)
                            m.then_inc(o_mm, 1)
                            wait(pe, y_ready, g + 1)
                            for w in range(W):
                                first = isinstance(i, int) and i == 0 and u == 0 and w == 0
                                end = is_last(i, STEPS) and u == H - 1 and w == W - 1
                                m = pe.matmul(ps_gram[0:C, 0:A1], y[:, u, w, 0:C], y[:, u, w, :], start=first, stop=end,
                                              skip_group_check=True)
                            m.then_inc(gram_done, 1)
                loop(pe, STEPS, step)

            @block.scalar
            def _(act):
                def step(i):
                    for u in range(H):
                        g = H * i + u
                        if not last:
                            wait(act, var_ready, g + 1)
                            act.activation(mom[:, u, 7, :], mom[:, u, 6, :], ACT.Sqrt, bias=v.eps[:, :]).then_inc(std_ready, 1)
                        wait(act, t_mm, g + 1)
                        wait(act, o_mm, g - 1)
                        act.activation(ht[0:C, u, :], ps_t[0:C, u * 512:u * 512 + WP], ACT.Relu).then_inc(ht_ready, 1)
                        wait(act, o_mm, g + 1)
                        if last:
                            wait(act, fin_ready, g - 1)
                            act.activation(y[:, u, :, :], ps_o[:, u * 512:u * 512 + W * C].rearrange("p (w c) -> p w c", w=W),
                                           ACT.Relu).then_inc(y_ready, 1)
                            wait(act, fin_ready, g + 1)
                            if is_last(i, STEPS) and u == H - 1:
                                k = FULL_WIN - W * g
                                act.dma_start(v.out[W * g * P:FULL_WIN * P, :].rearrange("(w p) f -> p w f", p=P),
                                              fin[:, u, 0:k, :]).then_inc(stored[u], 16)
                                act.dma_start(v.out[FULL_WIN * P:N, :], fin[0:REST, u, k, :]).then_inc(stored[u], 16)
                            else:
                                act.dma_start(v.out[bass.ds(g * WP, WP), :].rearrange("(w p) f -> p w f", p=P),
                                              fin[:, u, :, :]).then_inc(stored[u], 16)
                        else:
                            o = ps_o[:, :].rearrange("p (w c) -> p w c", w=W)
                            wait(act, stored[u], 32 * i)
                            act.activation(pq[:, u, :, :], o[:, :, 0:2 * C], ACT.Copy).then_inc(pq_ready, 1)
                            wait(act, gram_done, g - 1)
                            act.activation(y[:, u, :, 0:C], o[:, :, 2 * C:3 * C], ACT.Relu).then_inc(y_ready, 1)
                            wait(act, pq_ready, g + 1)
                            for t, part in ((0, pq[:, u, :, 0:C]), (1, pq[:, u, :, C:2 * C])):
                                act.dma_start(v.pq_tab[bass.ds(g * WP + t * NPAD, WP), :].rearrange("(p w) f -> p w f", w=W), part
                                              ).then_inc(stored[u], 16)
                loop(act, STEPS, step)
                act.wait_ge(stored[0], (1 if last else 2) * 16 * STEPS)
                act.wait_ge(stored[1], (16 * STEPS + 16) if last else 32 * STEPS)


def sorted_phase(nc, v, second):
    last = second
    H = 2
    STEPS = NODE_GROUPS // H
    tag = "sd" if last else "sc"
    WP = W * P
    RS = W * SLOTS
    EDGE_STEPS = EDGE_GROUPS // H
    with ExitStack() as st:
        def sb(name, shape, dt=F32):
            return st.enter_context(nc.sbuf_tensor(name + tag, shape, dt))

        def sem(name):
            return st.enter_context(nc.semaphore(name + tag))

        def bank(name, n=1):
            return st.enter_context(nc.psum_tensor(name + tag, [P, n * 512], F32))

        er = sb("er", [WP_E, H, W, SLOTS * ROW])
        base = sb("base", [WP_E, RS])
        rel = sb("rel", [WP_E, H, RS])
        hot = sb("hot", [WP_E, H, RS, P])
        xn = sb("xn", [P, H, W, C])
        ht = sb("ht", [A1, H, WP])
        mine = sb("mine", [P, H, 3 * W])
        y = sb("y", [P, H, W, C if last else A1])
        ps_agg, ps_t = bank("ps_agg", H), bank("ps_t")
        edges = SortedEdges(nc, v, st, second)
        if last:
            tot = sb("tot", [P, H, W, C])
            ps_o = bank("ps_o", 1)
        else:
            xs = sb("xs", [P, H, W, C])
            pq = sb("pq", [P, H, W, 2 * C])
            bn, mom = sb("bn", [P, H, W, 6]), sb("mom", [P, H, 8, W])
            ps_o = bank("ps_o", W)
            ps_gram = bank("ps_gram")
        base_set, rel_ready, hot_ready, agg_mm, xn_ready, t_mm, ht_ready, o_mm, y_ready, sp_turn = (sem(n) for n in (
            "base_set", "rel_ready", "hot_ready", "agg_mm", "xn_ready", "t_mm", "ht_ready", "o_mm", "y_ready", "sp_turn"))
        if second:
            took, tot_ready, y_chain, fin_ready, act_turn = (sem(n) for n in ("took", "tot_ready", "y_chain", "fin_ready", "act_turn"))
        else:
            (deg_chain, x1_ready, stats_chain, var_ready, std_ready, rstd_ready, scaled, pq_ready, gram_done, kept_it,
             turn, ready) = (sem(n) for n in ("deg_chain", "x1_ready", "stats_chain", "var_ready", "std_ready", "rstd_ready",
                                              "scaled", "pq_ready", "gram_done", "kept_it", "turn", "ready"))
            x_in = [sem(f"x_in{u}") for u in range(H)]
        rows_in = [sem(f"rows_in{u}") for u in range(H)]
        stored = [sem(f"stored{u}") for u in range(H)]
        xw = v.x[0:FULL_WIN * P, :].rearrange("(w p) f -> p w f", p=P)
        K_END = FULL_WIN - W * (NODE_GROUPS - 1)

        def at(i, u, d):
            return i + (u + d) // H, (u + d) % H

        def pipe(engine, body):
            body(0)
            body(1)
            with engine.Fori(2, EDGE_STEPS - 1 - LEAD) as i:
                body(i)
            for i in range(EDGE_STEPS - 1 - LEAD, STEPS):
                body(i)

        def edges_at(i, u):
            return None if isinstance(i, int) and i + LEAD >= EDGE_STEPS else (i + LEAD, u)

        first_edges = [(j, u) for j in range(LEAD) for u in range(H)]

        def is_first(i, u):
            return isinstance(i, int) and i == 0 and u == 0

        def is_end(i, u):
            return is_last(i, STEPS) and u == H - 1

        def before(i, u):
            return None if is_first(i, u) else at(i, u, -1)

        def after(i, u, d=1):
            a = at(i, u, d)
            return None if isinstance(a[0], int) and a[0] >= STEPS else a

        with nc.Block() as block:
            @block.sync
            def _(sp):
                def sp_wait(sem_, value):
                    wait(sp, sem_, value)
                    if not isinstance(value, int):
                        sp.sem_inc(sp_turn, 1)

                def load_rows(i, u):
                    g = H * i + u
                    _, first_rows = nc.values_load_multi_w_load_instructions(
                        v.starts[0:1, bass.ds(W * g, W)], engines=(sp.engine,), min_val=0, max_val=E,
                        skip_runtime_bounds_check_because="sums of counts of E edges are at most E")
                    sp_wait(agg_mm, g - 1)
                    for h in range(H):
                        sp_wait(edges.stored[h], 16 * (i + 2))
                    for w in range(W):
                        sp.dma_start(er[:, u, w, :], v.edge_rows[bass.ds(first_rows[w], WP_E * SLOTS), :]
                                     .rearrange("(p r) c -> p (r c)", p=WP_E)).then_inc(rows_in[u], 16)

                def load_x(i, u):
                    g = H * i + u
                    sp_wait(kept_it, g - 1)
                    sp_wait(xn_ready, g - 1)
                    if is_end(i, u):
                        k = K_END
                        sp.dma_start(xs[:, u, 0:k, :], xw[:, FULL_WIN - k:FULL_WIN, :]).then_inc(x_in[u], 16)
                        sp.dma_start(xs[0:REST, u, k, :], v.x[FULL_WIN * P:N, :]).then_inc(x_in[u], 16)
                        nothing = v.valid[0:1, N:N + C]
                        sp.dma_start(xs[REST:P, u, k, :], nothing.to_broadcast([P - REST, C])).then_inc(x_in[u], 16)
                        sp.dma_start(xs[:, u, k + 1, :], nothing.to_broadcast([P, C])).then_inc(x_in[u], 16)
                        assert k + 2 == W
                        wait(sp, o_mm, g - 1)
                        sp.dma_start(ht[C:A1, u, :], v.valid[:, g * WP:(g + 1) * WP]).then_inc(x_in[u], 16)
                    else:
                        sp.dma_start(xs[:, u, :, :], xw[:, bass.ds(W * g, W), :]).then_inc(x_in[u], 16)

                def store(i, u):
                    g = H * i + u
                    if last:
                        sp_wait(tot_ready, g + 1)
                        sp.dma_start(v.sum_tab[bass.ds(g * WP, WP), :].rearrange("(p w) f -> p (w f)", w=W),
                                     tot[:, u, :, :].rearrange("p w c -> p (w c)")).then_inc(stored[u], 16)
                    else:
                        sp_wait(pq_ready, g + 1)
                        sp.dma_start(v.pq_tab[0:2 * NPAD, :].rearrange("(t n) f -> t n f", t=2)[:, bass.ds(g * WP, WP), :]
                                     .rearrange("t (p w) f -> p t (w f)", w=W),
                                     pq[:, u, :, :].rearrange("p w (t c) -> p (w t c)", t=2).rearrange("p (t x) -> p t x", t=2)
                                     ).then_inc(stored[u], 16)

                def edge_loads(j, u):
                    n = at(j, u, 1)
                    if not (isinstance(n[0], int) and n[0] >= EDGE_STEPS):
                        edges.load(sp_wait, sp, *n)
                    if before(j, u):
                        edges.store(sp_wait, sp, *before(j, u))
                    if isinstance(j, int) and j == EDGE_STEPS - 1 and u == H - 1:
                        edges.store(sp_wait, sp, j, u)

                edges.load(sp_wait, sp, 0, 0)
                for j, u in first_edges:
                    edge_loads(j, u)
                load_rows(0, 0)
                load_rows(0, 1)
                if not last:
                    load_x(0, 0)

                def step(i):
                    for u in range(H):
                        if after(i, u, 2):
                            load_rows(*after(i, u, 2))
                        if after(i, u) and not last:
                            load_x(*after(i, u))
                        if edges_at(i, u):
                            edge_loads(*edges_at(i, u))
                        if before(i, u):
                            store(*before(i, u))
                pipe(sp, step)
                store(STEPS - 1, H - 1)
                for u in range(H):
                    sp.wait_ge(stored[u], 16 * STEPS)
                    sp.wait_ge(edges.stored[u], 16 * EDGE_STEPS)

            @block.gpsimd
            def _(pool):
                for j, u in first_edges:
                    edges.gather(pool, j, u)

                def step(i):
                    for u in range(H):
                        g = H * i + u
                        if edges_at(i, u):
                            edges.gather(pool, *edges_at(i, u))
                        if not last:
                            wait(pool, x1_ready, g + 1)
                            wait(pool, scaled, g + 1)
                            pool.sem_inc(turn, 1)
                            pool.tensor_copy(v.x1[:, bass.ds(g * W * C, W * C)], xs[:, u, :, :].rearrange("p w c -> p (w c)"))
                            pool.tensor_copy(v.kept[:, bass.ds(g, 1), :].rearrange("p a c -> p (a c)"), mine[:, u, :]).then_inc(kept_it, 1)
                pipe(pool, step)

            @block.vector
            def _(dve):
                for r in range(SLOTS):
                    for w in range(W):
                        dve.memset(base[:, w * SLOTS + r:w * SLOTS + r + 1], float(w * P))
                for u in range(H):
                    dve.memset(ht[C:A1, u, :], 1.0)
                    if not last:
                        dve.memset(y[:, u, :, C:A1], 1.0)
                edges.start(dve)
                dve.drain().then_inc(base_set, 1)

                def one_hot(i, u):
                    g = H * i + u
                    wait(dve, rows_in[u], 16 * W * (i + 1))
                    wait(dve, base_set, g + 1)
                    dst = er[:, u, :, :].rearrange("p w (r c) -> p (w r) c", r=SLOTS)[:, :, A1]
                    dve.tensor_tensor(rel[:, u, :], dst, base[:, :], ALU.subtract).then_inc(rel_ready, 1)
                    wait(dve, rel_ready, g + 1)
                    wait(dve, agg_mm, g - 1)
                    dve.tensor_scalar(base[:, :], base[:, :], float(WP), None, ALU.add).then_inc(base_set, 1)
                    dve.tensor_tensor(hot[:, u, :, :], rel[:, u, :].unsqueeze(2).to_broadcast([WP_E, RS, P]),
                                      v.line[0:WP_E, :].unsqueeze(1).to_broadcast([WP_E, RS, P]), ALU.is_equal).then_inc(hot_ready, 1)

                def sums(u):
                    return ps_agg[:, u * 512:u * 512 + W * A1].rearrange("p (w c) -> p w c", w=W)

                def make_x1(i, u):
                    g = H * i + u
                    m = [mom[:, u, k, :] for k in range(8)]
                    agg = sums(u)
                    wait(dve, agg_mm, g + 1)
                    wait(dve, kept_it, g - 1)
                    dve.tensor_copy(mine[:, u, 2 * W:], agg[:, :, C])
                    dve.tensor_scalar(m[0], agg[:, :, C], 1.0, None, ALU.max).then_inc(deg_chain, 1)
                    wait(dve, deg_chain, 2 * g + 1)
                    dve.reciprocal(m[1], m[0]).then_inc(deg_chain, 1)
                    wait(dve, deg_chain, 2 * g + 2)
                    wait(dve, x_in[u], 16 * STEPS + 4 * 16 if is_end(i, u) else 16 * (i + 1))
                    for w in range(W):
                        op = dve.scalar_tensor_tensor(xs[:, u, w, :], agg[:, w, 0:C], m[1][:, w:w + 1], xs[:, u, w, :],
                                                      ALU.mult, ALU.add)
                    op.then_inc(x1_ready, 1)
                    wait(dve, x1_ready, g + 1)
                    for w in range(W):
                        op = dve.bn_stats(bn[:, u, w, :], xs[:, u, w, :])
                    op.then_inc(stats_chain, 1)
                    wait(dve, stats_chain, 3 * g + 1)
                    me, se, mo, so = (bn[:, u, :, k] for k in (1, 2, 4, 5))
                    dve.tensor_tensor(m[2], me, mo, ALU.add)
                    dve.tensor_tensor(m[3], me, mo, ALU.subtract)
                    dve.tensor_tensor(m[4], se, so, ALU.add).then_inc(stats_chain, 1)
                    wait(dve, stats_chain, 3 * g + 2)
                    dve.scalar_tensor_tensor(m[5], m[3], 0.25, m[3], ALU.mult, ALU.mult).then_inc(stats_chain, 1)
                    wait(dve, stats_chain, 3 * g + 3)
                    dve.scalar_tensor_tensor(m[6], m[4], 1.0 / C, m[5], ALU.mult, ALU.add).then_inc(var_ready, 1)

                def factors(i, u):
                    g = H * i + u
                    wait(dve, std_ready, g + 1)
                    dve.reciprocal(mine[:, u, 0:W], mom[:, u, 7, :]).then_inc(rstd_ready, 1)
                    wait(dve, rstd_ready, g + 1)
                    dve.scalar_tensor_tensor(mine[:, u, W:2 * W], mom[:, u, 2, :], -0.5, mine[:, u, 0:W], ALU.mult, ALU.mult
                                             ).then_inc(scaled, 1)

                def take_factors(i, u):
                    g = H * i + u
                    wait(dve, xn_ready, g - 1)
                    dve.tensor_copy(mine[:, u, :], v.kept[:, bass.ds(g, 1), :].rearrange("p a c -> p (a c)")).then_inc(took, 1)

                def node_part(i, u):
                    g = H * i + u
                    a_node, c_node = (v.rows4[:, k * C:(k + 1) * C].unsqueeze(1).to_broadcast([P, W, C]) for k in (0, 1))
                    x1 = v.x1[:, bass.ds(g * W * C, W * C)]
                    wait(dve, y_ready, g + 1)
                    dve.tensor_tensor(y[:, u, :, :], y[:, u, :, :], a_node, ALU.mult).then_inc(y_chain, 1)
                    wait(dve, y_chain, 2 * g + 1)
                    dve.tensor_tensor(y[:, u, :, :], y[:, u, :, :], c_node, ALU.add).then_inc(y_chain, 1)
                    wait(dve, y_chain, 2 * g + 2)
                    dve.tensor_tensor(x1, x1, y[:, u, :, :].rearrange("p w c -> p (w c)"), ALU.add).then_inc(fin_ready, 1)

                for j, u in first_edges:
                    edges.set_dst(dve, j, u)
                if last:
                    take_factors(0, 0)
                one_hot(0, 0)
                one_hot(0, 1)

                def step(i):
                    for u in range(H):
                        if last:
                            if after(i, u):
                                take_factors(*after(i, u))
                            if after(i, u, 2):
                                one_hot(*after(i, u, 2))
                            if before(i, u):
                                node_part(*before(i, u))
                        else:
                            make_x1(i, u)
                            factors(i, u)
                            if after(i, u, 2):
                                one_hot(*after(i, u, 2))
                        if edges_at(i, u):
                            edges.set_dst(dve, *edges_at(i, u))
                pipe(dve, step)
                if last:
                    node_part(STEPS - 1, H - 1)
                    edges.m.finish_dve(dve)
                else:
                    dve.wait_ge(gram_done, NODE_GROUPS)
                    dve.tensor_copy(v.grams[:, 0, :], ps_gram[0:C, 0:A1]).then_inc(ready, 1)
                    dve.wait_ge(ready, 1)

            @block.tensor
            def _(pe):
                pe.wait_ge(base_set, 1)

                def aggregate(i, u):
                    g = H * i + u
                    wait(pe, hot_ready, g + 1)
                    wait(pe, tot_ready if last else x1_ready, g - 1)
                    for w in range(W):
                        for r in range(SLOTS):
                            m = pe.matmul(ps_agg[:, u * 512 + w * A1:u * 512 + (w + 1) * A1], hot[:, u, w * SLOTS + r, :],
                                          er[:, u, w, r * ROW:r * ROW + A1], start=r == 0, stop=r == SLOTS - 1)
                    m.then_inc(agg_mm, 1)

                def turn_rows(i, u):
                    g = H * i + u
                    wait(pe, xn_ready, g + 1)
                    wait(pe, ht_ready, g)
                    for w in range(W):
                        m = pe.transpose(ps_t[0:C, w * P:(w + 1) * P], xn[:, u, w, :], v.ident[:, :])
                    m.then_inc(t_mm, 1)

                def products(i, u):
                    g = H * i + u
                    wait(pe, ht_ready, g + 1)
                    wait(pe, y_ready, g)
                    if is_end(i, u) and not last:
                        wait(pe, x_in[u], 16 * STEPS + 4 * 16)
                    for w in range(W):
                        if last:
                            m = pe.matmul(ps_o[:, w * C:(w + 1) * C], ht[:, u, w * P:(w + 1) * P], v.w_cat[:, 2 * C:],
                                          start=True, stop=True)
                        else:
                            m = pe.matmul(ps_o[:, w * 512:w * 512 + 3 * C], ht[:, u, w * P:(w + 1) * P], v.w_cat[:, :],
                                          start=True, stop=True)
                    m.then_inc(o_mm, 1)

                def gram(i, u):
                    g = H * i + u
                    wait(pe, y_ready, g + 1)
                    for w in range(W):
                        m = pe.matmul(ps_gram[0:C, 0:A1], y[:, u, w, 0:C], y[:, u, w, :], start=is_first(i, u) and w == 0,
                                      stop=is_end(i, u) and w == W - 1, skip_group_check=True)
                    m.then_inc(gram_done, 1)

                if last:
                    for j, u in first_edges:
                        edges.m.edge_part(pe, j, u)
                        edges.products(pe, j, u)
                        if before(j, u):
                            edges.gram(pe, *before(j, u))
                aggregate(0, 0)

                def step(i):
                    for u in range(H):
                        more = edges_at(i, u) if last else None
                        if more:
                            edges.m.edge_part(pe, *more)
                        if before(i, u):
                            products(*before(i, u))
                        if after(i, u):
                            aggregate(*after(i, u))
                        if more:
                            edges.products(pe, *more)
                        if before(i, u) and not last:
                            gram(*before(i, u))
                        turn_rows(i, u)
                        if more:
                            edges.gram(pe, *at(*more, -1))
                pipe(pe, step)
                products(STEPS - 1, H - 1)
                if last:
                    edges.gram(pe, EDGE_STEPS - 1, H - 1)
                else:
                    gram(STEPS - 1, H - 1)

            @block.scalar
            def _(act):
                def norm(i, u):
                    g = H * i + u
                    if last:
                        wait(act, took, g + 1)
                    else:
                        wait(act, scaled, g + 1)
                    wait(act, t_mm, g - 1)
                    if last:
                        act.sem_inc(act_turn, 1)
                    for w in range(W):
                        rows = v.x1[:, bass.ds(g * W * C + w * C, C)] if last else xs[:, u, w, :]
                        op = act.activation(xn[:, u, w, :], rows, ACT.Identity, scale=mine[:, u, w:w + 1],
                                            bias=mine[:, u, W + w:W + w + 1])
                    op.then_inc(xn_ready, 1)

                def outputs(i, u):
                    g = H * i + u
                    wait(act, o_mm, g + 1)
                    if last:
                        wait(act, fin_ready, g - 1)
                        act.activation(y[:, u, :, :], ps_o[:, 0:W * C].rearrange("p (w c) -> p w c", w=W), ACT.Relu).then_inc(y_ready, 1)
                    else:
                        o = ps_o[:, :].rearrange("p (w c) -> p w c", w=W)
                        wait(act, stored[u], 16 * i)
                        pq_ = pq[:, u, :, :].rearrange("p w c -> p (w c)").rearrange("p (t w c) -> p w t c", t=2, w=W)
                        act.activation(pq_, o[:, :, 0:2 * C].rearrange("p w (t c) -> p w t c", t=2), ACT.Copy).then_inc(pq_ready, 1)
                        wait(act, gram_done, g - 1)
                        act.activation(y[:, u, :, 0:C], o[:, :, 2 * C:3 * C], ACT.Relu).then_inc(y_ready, 1)

                def turned(i, u):
                    g = H * i + u
                    wait(act, t_mm, g + 1)
                    wait(act, o_mm, g - 1)
                    act.activation(ht[0:C, u, :], ps_t[0:C, :], ACT.Relu).then_inc(ht_ready, 1)

                def copy_sums(i, u):
                    g = H * i + u
                    wait(act, agg_mm, g + 1)
                    wait(act, stored[u], 16 * i)
                    act.activation(tot[:, u, :, :], ps_agg[:, u * 512:u * 512 + W * A1].rearrange("p (w c) -> p w c", w=W)[:, :, 0:C],
                                   ACT.Copy).then_inc(tot_ready, 1)

                def step(i):
                    for u in range(H):
                        if last and edges_at(i, u):
                            j, _ = edges_at(i, u)
                            edges.m.edge_relu(act, H * j + u)
                        if not last:
                            g = H * i + u
                            wait(act, var_ready, g + 1)
                            act.activation(mom[:, u, 7, :], mom[:, u, 6, :], ACT.Sqrt, bias=v.eps[:, :]).then_inc(std_ready, 1)
                        if before(i, u):
                            outputs(*before(i, u))
                        norm(i, u)
                        turned(i, u)
                        if last:
                            copy_sums(i, u)
                            if edges_at(i, u):
                                edges.relus(act, *edges_at(i, u))
                if last:
                    for j, u in first_edges:
                        edges.m.edge_relu(act, H * j + u)
                        edges.relus(act, j, u)
                pipe(act, step)
                outputs(STEPS - 1, H - 1)


def finish_phase(nc, v):
    H = 7
    STEPS = NODE_GROUPS // H
    WP = W * P
    with ExitStack() as st:
        def sb(name, shape):
            return st.enter_context(nc.sbuf_tensor(name + "fin", shape, F32))

        def sem(name):
            return st.enter_context(nc.semaphore(name + "fin"))

        tot, fin = sb("tot", [P, H, W, C]), sb("fin", [P, H, W, C])
        deg = sb("deg", [P, H, W])
        sums_in = [sem(f"sums_in{u}") for u in range(H)]
        stored = [sem(f"stored{u}") for u in range(H)]
        scaled, shifted, fin_ready, pool_turn = sem("scaled"), sem("shifted"), sem("fin_ready"), sem("pool_turn")

        with nc.Block() as block:
            @block.sync
            def _(sp):
                def step(i):
                    for u in range(H):
                        g = H * i + u
                        wait(sp, fin_ready, g - H + 1)
                        sp.dma_start(tot[:, u, :, :].rearrange("p w c -> p (w c)"),
                                     v.sum_tab[bass.ds(g * WP, WP), :].rearrange("(p w) f -> p (w f)", w=W)).then_inc(sums_in[u], 16)
                loop(sp, STEPS, step)

            @block.vector
            def _(dve):
                a_msg, c_msg = (v.rows4[:, k * C:(k + 1) * C] for k in (2, 3))

                def step(i):
                    for u in range(H):
                        g = H * i + u
                        wait(dve, sums_in[u], 16 * (i + 1))
                        dve.tensor_copy(deg[:, u, :], v.kept[:, bass.ds(g, 1), 2 * W:].rearrange("p a c -> p (a c)"))
                        dve.tensor_tensor(tot[:, u, :, :], tot[:, u, :, :], a_msg.unsqueeze(1).to_broadcast([P, W, C]),
                                          ALU.mult).then_inc(scaled, 1)
                        wait(dve, scaled, g + 1)
                        for w in range(W):
                            op = dve.scalar_tensor_tensor(tot[:, u, w, :], c_msg, deg[:, u, w:w + 1], tot[:, u, w, :], ALU.mult, ALU.add)
                        op.then_inc(shifted, 1)
                loop(dve, STEPS, step)

            @block.gpsimd
            def _(pool):
                def step(i):
                    for u in range(H):
                        g = H * i + u
                        wait(pool, stored[u], 16 * i)
                        wait(pool, shifted, g + 1)
                        pool.sem_inc(pool_turn, 1)
                        pool.tensor_tensor(fin[:, u, :, :].rearrange("p w c -> p (w c)"), v.x1[:, bass.ds(g * W * C, W * C)],
                                           tot[:, u, :, :].rearrange("p w c -> p (w c)"), ALU.add).then_inc(fin_ready, 1)
                loop(pool, STEPS, step)

            @block.scalar
            def _(act):
                def step(i):
                    for u in range(H):
                        g = H * i + u
                        wait(act, fin_ready, g + 1)
                        if is_last(i, STEPS) and u == H - 1:
                            k = FULL_WIN - W * g
                            act.dma_start(v.out[W * g * P:FULL_WIN * P, :].rearrange("(w p) f -> p w f", p=P),
                                          fin[:, u, 0:k, :]).then_inc(stored[u], 16)
                            act.dma_start(v.out[FULL_WIN * P:N, :], fin[0:REST, u, k, :]).then_inc(stored[u], 16)
                        else:
                            act.dma_start(v.out[bass.ds(g * WP, WP), :].rearrange("(w p) f -> p w f", p=P),
                                          fin[:, u, :, :]).then_inc(stored[u], 16)
                loop(act, STEPS, step)
                for u in range(H):
                    act.wait_ge(stored[u], 16 * STEPS + (16 if u == H - 1 else 0))


def norm_rows_phase(nc, v, which):
    tag = v.tag + str(which[0])
    L = len(which)
    with ExitStack() as st:
        diag = st.enter_context(nc.sbuf_tensor("diag" + tag, [C, 4, C], F32))
        scrap = st.enter_context(nc.sbuf_tensor("scrap_n" + tag, [C, C], F32))
        ps = st.enter_context(nc.psum_tensor("ps_rows" + tag, [P, 512], F32))
        chain, std_ready, diag_ready, rows_mm = (st.enter_context(nc.semaphore(n + tag)) for n in ("chain_n", "std_n", "diag_n", "rows_n"))
        s = v.small
        with nc.Block() as block:
            @block.vector
            def _(dve):
                n = [0]

                def link(ins):
                    n[0] += 1
                    ins.then_inc(chain, 1)
                    dve.wait_ge(chain, n[0])

                for m, l in enumerate(which):
                    gamma, beta = ((v.gn, v.btn), (v.gm, v.btm))[l]
                    sq, mean, msq, var, std, rstd, a, am, c = (s[:, 9 * l + k:9 * l + k + 1] for k in range(9))
                    count = (N, E)[l]
                    link(dve.scalar_tensor_tensor(scrap[:, :], v.grams[:, l, 0:C], 1.0, v.ident[0:C, 0:C], ALU.mult, ALU.mult,
                                                  accum_out=sq))
                    link(dve.tensor_scalar(mean, v.grams[:, l, C:A1], 1.0 / count, None, ALU.mult))
                    link(dve.tensor_tensor(msq, mean, mean, ALU.mult))
                    dve.scalar_tensor_tensor(var, sq, 1.0 / count, msq, ALU.mult, ALU.subtract).then_inc(chain, 1)
                    n[0] += 1
                    dve.wait_ge(std_ready, m + 1)
                    link(dve.reciprocal(rstd, std))
                    link(dve.tensor_tensor(a, gamma, rstd, ALU.mult))
                    link(dve.tensor_tensor(am, a, mean, ALU.mult))
                    link(dve.tensor_tensor(c, beta, am, ALU.subtract))
                    for k, col in ((2 * m, a), (2 * m + 1, c)):
                        dve.tensor_scalar(diag[:, k, :], v.ident[0:C, 0:C], col, None, ALU.mult).then_inc(diag_ready, 1)
                dve.wait_ge(rows_mm, 1)
                link(dve.tensor_copy(v.rows4[:, 2 * which[0] * C:2 * (which[0] + L) * C], ps[:, 0:2 * L * C]))

            @block.scalar
            def _(act):
                for m, l in enumerate(which):
                    act.wait_ge(chain, 8 * m + 4)
                    act.activation(s[:, 9 * l + 4:9 * l + 5], s[:, 9 * l + 3:9 * l + 4], ACT.Sqrt, bias=v.eps[0:C, :]).then_inc(std_ready, 1)

            @block.tensor
            def _(pe):
                pe.wait_ge(diag_ready, 2 * L)
                pe.matmul(ps[:, 0:2 * L * C], v.ones[0:C, :], diag[:, 0:2 * L, :].rearrange("p k c -> p (k c)"),
                          start=True, stop=True).then_inc(rows_mm, 1)


_OUT = ((N, C), "float32")


def kernel(x, src, dst, edge_attr_4, L1_gnn_W_node, L1_gnn_b_node, L1_gnn_g_node, L1_gnn_beta_node, L1_gnn_W_edge,
           L1_gnn_b_edge, L1_gnn_g_edge, L1_gnn_beta_edge, L1_gnn_W_msg, L1_gnn_b_msg, L1_gnn_g_msg, L1_gnn_beta_msg):
    import numpy as np
    import concourse.bacc as bacc
    from concourse.bass_utils import run_bass_kernel_spmd as run

    def padded(a, fill):
        a = np.asarray(a)
        return np.concatenate([a, np.full((EPAD - E,) + a.shape[1:], fill, a.dtype)])

    src_p, dst_p = padded(src, 0), padded(dst, PAD_DST)
    valid = np.zeros((1, NPAD), np.float32)
    valid[0, :N] = 1.0
    def by_partition(a):
        return a.reshape(EDGE_GROUPS, P, T).transpose(1, 0, 2).reshape(P, EDGE_GROUPS * T)

    def by_tile(a):
        return a.reshape(-1, EDGE_GROUPS, P, T).transpose(0, 1, 3, 2).reshape(-1, EPAD)

    arrays = {
        "x": x, "src_g": by_partition(src_p), "dst_g": by_partition(dst_p), "dst_row": by_tile(dst_p),
        "dst_line": np.concatenate([dst_p, np.full(P, PAD_DST, dst_p.dtype)]).reshape(1, -1),
        "ea_t": np.asarray(edge_attr_4).T, "ea_g": by_tile(np.ascontiguousarray(padded(edge_attr_4, 0).T)), "valid": valid,
        "w_node": L1_gnn_W_node, "b_node": L1_gnn_b_node, "g_node": L1_gnn_g_node, "beta_node": L1_gnn_beta_node,
        "w_edge": L1_gnn_W_edge, "b_edge": L1_gnn_b_edge, "g_edge": L1_gnn_g_edge, "beta_edge": L1_gnn_beta_edge,
        "w_msg": L1_gnn_W_msg, "b_msg": L1_gnn_b_msg, "g_msg": L1_gnn_g_msg, "beta_msg": L1_gnn_beta_msg,
    }
    arrays = {k: np.ascontiguousarray(a) for k, a in arrays.items()}
    nc = bacc.Bacc("TRN2", target_bir_lowering=False, num_devices=1)
    args = [nc.dram_tensor("in_" + k, a.shape, mybir.dt.from_np(a.dtype), kind="ExternalInput").ap() for k, a in arrays.items()]
    out = nc.dram_tensor("out", _OUT[0], mybir.dt.from_np(np.dtype(_OUT[1])), kind="ExternalOutput").ap()
    program(nc, *args, out)
    r = run(nc, [{"in_" + k: a for k, a in arrays.items()}], core_ids=[0])
    return r.results[0]["out"]
```
